# Optimizing a Trainium2 kernel written in Bass

```python
import numpy as np
import jax
import jax.numpy as jnp

def _softmax(x, axis=-1):
    return jax.nn.softmax(x, axis=axis)
def _gelu(x):
    return jax.nn.gelu(x, approximate=True)
def _silu(x):
    return jax.nn.silu(x)
def _sigmoid(x):
    return jax.nn.sigmoid(x)
def _layernorm(x, axis=-1, eps=1e-5):
    m = jnp.mean(x, axis=axis, keepdims=True)
    v = jnp.var(x, axis=axis, keepdims=True)
    return (x - m) / jnp.sqrt(v + eps)
def _scatter_add(tgt, idx, src, axis=0):
    return tgt.at[idx].add(src)
def _segment_sum(src, seg, n):
    return jax.ops.segment_sum(src, seg, n)

kernel_name = 'mk_conv_preact_d2_conv_nhwc128_f325e6'

def setup_inputs(seed: int = 0):
    np.random.seed(seed)
    _w = jnp.asarray
    def _rec_inputs():
        import jax
        import jax.numpy as jnp
        _gk = jax.random.key(seed)
        x = -0.0002928 + 1 * jax.random.normal(jax.random.fold_in(_gk, 1), (8, 32, 128, 128), jnp.float32)
        return x
    x = _rec_inputs()
    def _L0_conv_setup():
        import jax, jax.numpy as jnp
        import numpy as np
        B, CIN, COUT, H, W = (8, 32, 32, 128, 128)

        def rfftshift(x):
            return jnp.conj(jnp.flip(jnp.fft.fftshift(x, axes=-2), axis=-1))

        def irfftshift(x):
            return jnp.conj(jnp.flip(jnp.fft.ifftshift(x, axes=-2), axis=-1))

        def symmetric_padding(xf_old, im_shape_old, im_shape_new):
            Ho, Wo = im_shape_old
            Hn, Wn = im_shape_new
            ft_h_old = Ho + (1 - Ho % 2)
            ft_w_old = Wo // 2 + 1
            ft_h_new = Hn + (1 - Hn % 2)
            ft_w_new = Wn // 2 + 1
            nlead = xf_old.ndim - 2
            xf = jnp.pad(xf_old, [(0, 0)] * nlead + [(0, ft_h_old - Ho), (0, 0)])
            if Ho % 2 == 0:
                xf = xf.at[..., 0, :].multiply(0.5)
                xf = xf.at[..., -1, :].set(xf[..., 0, :])
            if Wo % 2 == 0:
                xf = xf.at[..., :, 0].multiply(0.5)
            ph = (ft_h_new - ft_h_old) // 2
            pw = ft_w_new - ft_w_old
            xf = jnp.pad(xf, [(0, 0)] * nlead + [(ph, ph), (pw, 0)])
            if Hn % 2 == 0:
                xf = xf.at[..., 0, :].multiply(2.0)
            if Wn % 2 == 0:
                xf = xf.at[..., :, 0].multiply(2.0)
            return xf[..., :Hn, :]
        key = jax.random.key(seed)
        k1, k2, k3 = jax.random.split(key, 3)
        x = jax.random.normal(k1, (B, CIN, H, W), dtype=jnp.float32)
        weight_real = jax.random.uniform(k2, (CIN, COUT, H, W // 2 + 1), dtype=jnp.float32)
        weight_imag = jax.random.uniform(k3, (CIN, COUT, H, W // 2 + 1), dtype=jnp.float32)
        weight_imag = weight_imag.at[:, :, 0, 0].set(0.0)
        return {'x': x, 'weight_real': weight_real, 'weight_imag': weight_imag}
    _L0_conv_all = _L0_conv_setup()
    _L0_conv_in = {k: v for k, v in _L0_conv_all.items() if k in ('weight_real', 'weight_imag', )}
    del _L0_conv_all

    def _L1_conv_setup():
        import jax, jax.numpy as jnp
        import numpy as np
        N_HEADS = 32
        EPS = 1e-05

        def _inorm(x, w=None, b=None):
            mu = jnp.mean(x, axis=(-2, -1), keepdims=True)
            var = jnp.var(x, axis=(-2, -1), keepdims=True)
            y = (x - mu) * jax.lax.rsqrt(var + EPS)
            if w is not None:
                y = y * w[None, :, None, None] + b[None, :, None, None]
            return y

        def _fourier_resize(x, oh, ow):
            B, C, H, W = x.shape
            if (oh, ow) == (H, W):
                return x
            X = jnp.fft.rfft2(x, norm='forward')
            kh = min(H, oh) // 2
            kw = min(W // 2 + 1, ow // 2 + 1)
            out = jnp.zeros((B, C, oh, ow // 2 + 1), dtype=X.dtype)
            out = out.at[:, :, :kh, :kw].set(X[:, :, :kh, :kw])
            out = out.at[:, :, -kh:, :kw].set(X[:, :, -kh:, :kw])
            return jnp.fft.irfft2(out, s=(oh, ow), norm='forward')

        def _spectral_conv(x, w2, oh, ow):
            w = w2[..., 0] + 1j * w2[..., 1]
            mh = w.shape[2] // 2
            mw = w.shape[3]
            X = jnp.fft.rfft2(x, norm='forward')
            Xk = jnp.concatenate([X[:, :, :mh, :mw], X[:, :, -mh:, :mw]], axis=2)
            Yk = jnp.einsum('bixy,ioxy->boxy', Xk, w)
            B = x.shape[0]
            O = w.shape[1]
            out = jnp.zeros((B, O, oh, ow // 2 + 1), dtype=Yk.dtype)
            out = out.at[:, :, :mh, :mw].set(Yk[:, :, :mh])
            out = out.at[:, :, -mh:, :mw].set(Yk[:, :, mh:])
            return jnp.fft.irfft2(out, s=(oh, ow), norm='forward')

        def _fno_layer(x, conv_w, skip_w, oh, ow, inner_norm=False, act=False):
            skip = jnp.einsum('bixy,oi->boxy', x, skip_w)
            skip = _fourier_resize(skip, oh, ow)
            xf = _spectral_conv(x, conv_w, oh, ow)
            if inner_norm:
                xf = _inorm(xf)
            y = xf + skip
            if act:
                y = jax.nn.gelu(y, approximate=False)
            return y
        key = jax.random.key(seed)
        ks = jax.random.split(key, 16)
        B, T, H, W = (4, 32, 128, 128)

        def cw(k, ci, co, mh2, mw):
            scale = 1.0 / (ci * co)
            return scale * jax.random.normal(k, (ci, co, mh2, mw, 2), jnp.float32)

        def sw(k, co, ci):
            return jax.random.normal(k, (co, ci), jnp.float32) / np.float32(np.sqrt(ci))
        one = jnp.ones((1,), jnp.float32)
        zero = jnp.zeros((1,), jnp.float32)
        return dict(x=jax.random.normal(ks[0], (B, T, H, W), jnp.float32), norm1_w=one, norm1_b=zero, Kcw=cw(ks[1], 1, N_HEADS, 32, 17), Ksw=sw(ks[2], N_HEADS, 1), Qcw=cw(ks[3], 1, N_HEADS, 32, 17), Qsw=sw(ks[4], N_HEADS, 1), Vcw=cw(ks[5], 1, N_HEADS, 32, 17), Vsw=sw(ks[6], N_HEADS, 1), Pcw=cw(ks[7], N_HEADS, 1, 64, 33), Psw=sw(ks[8], 1, N_HEADS), attn_w=one, attn_b=zero, norm2_w=one, norm2_b=zero, m0cw=cw(ks[9], 1, 1, 64, 33), m0sw=sw(ks[10], 1, 1), m1cw=cw(ks[11], 1, 1, 64, 33), m1sw=sw(ks[12], 1, 1), mon_w=one, mon_b=zero)
    _L1_conv_all = _L1_conv_setup()
    _L1_conv_in = {k: v for k, v in _L1_conv_all.items() if k in ('norm1_w', 'norm1_b', 'Kcw', 'Ksw', 'Qcw', 'Qsw', 'Vcw', 'Vsw', 'Pcw', 'Psw', 'attn_w', 'attn_b', 'norm2_w', 'norm2_b', 'm0cw', 'm0sw', 'm1cw', 'm1sw', 'mon_w', 'mon_b', )}
    del _L1_conv_all

    return {
        "x": x,
        "L0_conv_weight_real": _L0_conv_in["weight_real"],
        "L0_conv_weight_imag": _L0_conv_in["weight_imag"],
        "L1_conv_norm1_w": _L1_conv_in["norm1_w"],
        "L1_conv_norm1_b": _L1_conv_in["norm1_b"],
        "L1_conv_Kcw": _L1_conv_in["Kcw"],
        "L1_conv_Ksw": _L1_conv_in["Ksw"],
        "L1_conv_Qcw": _L1_conv_in["Qcw"],
        "L1_conv_Qsw": _L1_conv_in["Qsw"],
        "L1_conv_Vcw": _L1_conv_in["Vcw"],
        "L1_conv_Vsw": _L1_conv_in["Vsw"],
        "L1_conv_Pcw": _L1_conv_in["Pcw"],
        "L1_conv_Psw": _L1_conv_in["Psw"],
        "L1_conv_attn_w": _L1_conv_in["attn_w"],
        "L1_conv_attn_b": _L1_conv_in["attn_b"],
        "L1_conv_norm2_w": _L1_conv_in["norm2_w"],
        "L1_conv_norm2_b": _L1_conv_in["norm2_b"],
        "L1_conv_m0cw": _L1_conv_in["m0cw"],
        "L1_conv_m0sw": _L1_conv_in["m0sw"],
        "L1_conv_m1cw": _L1_conv_in["m1cw"],
        "L1_conv_m1sw": _L1_conv_in["m1sw"],
        "L1_conv_mon_w": _L1_conv_in["mon_w"],
        "L1_conv_mon_b": _L1_conv_in["mon_b"],
    }

def reference(x, L0_conv_weight_real, L0_conv_weight_imag, L1_conv_norm1_w, L1_conv_norm1_b, L1_conv_Kcw, L1_conv_Ksw, L1_conv_Qcw, L1_conv_Qsw, L1_conv_Vcw, L1_conv_Vsw, L1_conv_Pcw, L1_conv_Psw, L1_conv_attn_w, L1_conv_attn_b, L1_conv_norm2_w, L1_conv_norm2_b, L1_conv_m0cw, L1_conv_m0sw, L1_conv_m1cw, L1_conv_m1sw, L1_conv_mon_w, L1_conv_mon_b):
    import jax
    import jax.numpy as jnp
    def _L0_conv_ref(x, weight_real, weight_imag):
        import jax, jax.numpy as jnp
        import numpy as np
        B, CIN, COUT, H, W = (8, 32, 32, 128, 128)

        def rfftshift(x):
            return jnp.conj(jnp.flip(jnp.fft.fftshift(x, axes=-2), axis=-1))

        def irfftshift(x):
            return jnp.conj(jnp.flip(jnp.fft.ifftshift(x, axes=-2), axis=-1))

        def symmetric_padding(xf_old, im_shape_old, im_shape_new):
            Ho, Wo = im_shape_old
            Hn, Wn = im_shape_new
            ft_h_old = Ho + (1 - Ho % 2)
            ft_w_old = Wo // 2 + 1
            ft_h_new = Hn + (1 - Hn % 2)
            ft_w_new = Wn // 2 + 1
            nlead = xf_old.ndim - 2
            xf = jnp.pad(xf_old, [(0, 0)] * nlead + [(0, ft_h_old - Ho), (0, 0)])
            if Ho % 2 == 0:
                xf = xf.at[..., 0, :].multiply(0.5)
                xf = xf.at[..., -1, :].set(xf[..., 0, :])
            if Wo % 2 == 0:
                xf = xf.at[..., :, 0].multiply(0.5)
            ph = (ft_h_new - ft_h_old) // 2
            pw = ft_w_new - ft_w_old
            xf = jnp.pad(xf, [(0, 0)] * nlead + [(ph, ph), (pw, 0)])
            if Hn % 2 == 0:
                xf = xf.at[..., 0, :].multiply(2.0)
            if Wn % 2 == 0:
                xf = xf.at[..., :, 0].multiply(2.0)
            return xf[..., :Hn, :]
        weight = jax.lax.complex(weight_real, weight_imag)
        im_shape = (H, W)
        multiplier = symmetric_padding(weight, im_shape, im_shape)
        x_ft = symmetric_padding(rfftshift(jnp.fft.rfft2(x, norm='forward')), im_shape, im_shape)
        out_ft = jnp.einsum('bixy,ioxy->boxy', x_ft, multiplier)
        out = jnp.fft.irfft2(irfftshift(out_ft), s=im_shape, norm='forward')
        return out

    def _L1_conv_ref(x, norm1_w, norm1_b, Kcw, Ksw, Qcw, Qsw, Vcw, Vsw, Pcw, Psw, attn_w, attn_b, norm2_w, norm2_b, m0cw, m0sw, m1cw, m1sw, mon_w, mon_b):
        import jax, jax.numpy as jnp
        import numpy as np
        N_HEADS = 32
        EPS = 1e-05

        def _inorm(x, w=None, b=None):
            mu = jnp.mean(x, axis=(-2, -1), keepdims=True)
            var = jnp.var(x, axis=(-2, -1), keepdims=True)
            y = (x - mu) * jax.lax.rsqrt(var + EPS)
            if w is not None:
                y = y * w[None, :, None, None] + b[None, :, None, None]
            return y

        def _fourier_resize(x, oh, ow):
            B, C, H, W = x.shape
            if (oh, ow) == (H, W):
                return x
            X = jnp.fft.rfft2(x, norm='forward')
            kh = min(H, oh) // 2
            kw = min(W // 2 + 1, ow // 2 + 1)
            out = jnp.zeros((B, C, oh, ow // 2 + 1), dtype=X.dtype)
            out = out.at[:, :, :kh, :kw].set(X[:, :, :kh, :kw])
            out = out.at[:, :, -kh:, :kw].set(X[:, :, -kh:, :kw])
            return jnp.fft.irfft2(out, s=(oh, ow), norm='forward')

        def _spectral_conv(x, w2, oh, ow):
            w = w2[..., 0] + 1j * w2[..., 1]
            mh = w.shape[2] // 2
            mw = w.shape[3]
            X = jnp.fft.rfft2(x, norm='forward')
            Xk = jnp.concatenate([X[:, :, :mh, :mw], X[:, :, -mh:, :mw]], axis=2)
            Yk = jnp.einsum('bixy,ioxy->boxy', Xk, w)
            B = x.shape[0]
            O = w.shape[1]
            out = jnp.zeros((B, O, oh, ow // 2 + 1), dtype=Yk.dtype)
            out = out.at[:, :, :mh, :mw].set(Yk[:, :, :mh])
            out = out.at[:, :, -mh:, :mw].set(Yk[:, :, mh:])
            return jnp.fft.irfft2(out, s=(oh, ow), norm='forward')

        def _fno_layer(x, conv_w, skip_w, oh, ow, inner_norm=False, act=False):
            skip = jnp.einsum('bixy,oi->boxy', x, skip_w)
            skip = _fourier_resize(skip, oh, ow)
            xf = _spectral_conv(x, conv_w, oh, ow)
            if inner_norm:
                xf = _inorm(xf)
            y = xf + skip
            if act:
                y = jax.nn.gelu(y, approximate=False)
            return y
        B, T, H, W = x.shape
        Hs, Ws = (H // 2, W // 2)
        temperature = 1.0
        xa = x.reshape(B * T, 1, H, W)
        xn = _inorm(xa, norm1_w, norm1_b)
        k = _fno_layer(xn, Kcw, Ksw, Hs, Ws)
        q = _fno_layer(xn, Qcw, Qsw, Hs, Ws)
        v = _fno_layer(xn, Vcw, Vsw, H, W)
        nh = k.shape[1]
        kf = k.reshape(B, T, nh, Hs * Ws).transpose(0, 2, 1, 3)
        qf = q.reshape(B, T, nh, Hs * Ws).transpose(0, 2, 1, 3)
        vf = v.reshape(B, T, nh, H * W).transpose(0, 2, 1, 3)
        scores = jnp.einsum('bntk,bnsk->bnts', qf, kf) / (np.float32(np.sqrt(Hs * Ws)) * temperature)
        p_attn = jax.nn.softmax(scores, axis=-1)
        av = jnp.einsum('bnts,bnsk->bntk', p_attn, vf)
        av = av.reshape(B, nh, T, H, W).transpose(0, 2, 1, 3, 4).reshape(B * T, nh, H, W)
        p = _fno_layer(av, Pcw, Psw, H, W)
        a = _inorm(p + xa, attn_w, attn_b)
        an = _inorm(a, norm2_w, norm2_b)
        m = _fno_layer(an, m0cw, m0sw, H, W, inner_norm=True, act=True)
        m = _fno_layer(m, m1cw, m1sw, H, W, inner_norm=True, act=False)
        out = _inorm(m, mon_w, mon_b) + a
        return out.reshape(B, T, H, W)

    def _gn(v, G=32, eps=1e-5):
        B_, H_, W_, C_ = v.shape
        g = v.reshape(B_, H_, W_, G, C_ // G)
        m = jnp.mean(g, axis=(1, 2, 4), keepdims=True)
        s = jnp.var(g, axis=(1, 2, 4), keepdims=True)
        return ((g - m) / jnp.sqrt(s + eps)).reshape(v.shape)

    def _ln_c(v, eps=1e-6):
        m = jnp.mean(v, axis=-1, keepdims=True)
        s = jnp.var(v, axis=-1, keepdims=True)
        return (v - m) / jnp.sqrt(s + eps)

    def _ln_t(v, eps=1e-5):
        m = jnp.mean(v, axis=-1, keepdims=True)
        s = jnp.var(v, axis=-1, keepdims=True)
        return (v - m) / jnp.sqrt(s + eps)

    def _to_tokens(v):
        B_, H_, W_, C_ = v.shape
        return v.reshape(B_, H_ * W_, C_)
    def _from_tokens(t, like):
        return t.reshape(like.shape)

    x = x + _L0_conv_ref(_gn(x), L0_conv_weight_real, L0_conv_weight_imag)
    x = x + _L1_conv_ref(_gn(x), L1_conv_norm1_w, L1_conv_norm1_b, L1_conv_Kcw, L1_conv_Ksw, L1_conv_Qcw, L1_conv_Qsw, L1_conv_Vcw, L1_conv_Vsw, L1_conv_Pcw, L1_conv_Psw, L1_conv_attn_w, L1_conv_attn_b, L1_conv_norm2_w, L1_conv_norm2_b, L1_conv_m0cw, L1_conv_m0sw, L1_conv_m1cw, L1_conv_m1sw, L1_conv_mon_w, L1_conv_mon_b)
    return x


_drawn_inputs = setup_inputs


def setup_inputs(seed=0):
    import zlib

    import numpy as np

    out = dict(_drawn_inputs(seed))
    spreads = {}
    factors = {'L1_conv_Kcw': 181.56,
     'L1_conv_Ksw': 4.431,
     'L1_conv_Qcw': 200.0,
     'L1_conv_Qsw': 8.0,
     'L1_conv_Vcw': 37.248,
     'L1_conv_Psw': 6.402,
     'L1_conv_Vsw': 3.421,
     'L1_conv_Pcw': 6.578}
    for name, (base, spread) in spreads.items():
        noise = np.random.default_rng([zlib.crc32(name.encode()), seed]).standard_normal(out[name].shape)
        drawn = base * np.exp(spread * noise) if base else spread * noise
        out[name] = jnp.asarray(drawn.astype(out[name].dtype))
    for name, factor in factors.items():
        out[name] = (out[name] * factor).astype(out[name].dtype)
    return out
```

```python
from contextlib import ExitStack

import numpy as np
import concourse.bass as bass
from concourse import mybir

F32 = mybir.dt.float32
ALU = mybir.AluOpType
ACT = mybir.ActivationFunctionType
AX = mybir.AxisListType

B, T, N = 8, 32, 128
NH = 32
P = 128
NIMG = B * T
NF = N // 2 + 1
ND = 2 * NF
MF = 33
HM = 64
JT = 9
CH = 8
CW = CH * N
GRP = 4
PERGRP = float(T * N * GRP)
PIX = N * N
EPS = 1e-5
LOW = list(range(16)) + list(range(-16, 0))
HIGH = list(range(16, 32)) + list(range(-32, -16))
ROW_HF = np.array([(LOW, HIGH)[h][k] for h in range(2) for c in range(2) for k in range(32)])
ROW_C = np.array([c for h in range(2) for c in range(2) for k in range(32)])


def pack(parts):
    at, cols, where = 0, [], {}
    for name, a in parts:
        a = np.ascontiguousarray(a, dtype=np.float32).reshape(P, -1)
        where[name] = (at, a.shape[1])
        at += a.shape[1]
        cols.append(a)
    return np.concatenate(cols, axis=1), where


def shape_constants():
    y = np.arange(N)
    th = 2 * np.pi * np.outer(y, ROW_HF) / N
    c, s = np.cos(th), -np.sin(th)
    f1 = np.concatenate([np.where(ROW_C == 0, c, s), np.where(ROW_C == 0, -s, c)], 1) / N
    wf = np.arange(MF)
    tw = 2 * np.pi * np.outer(y, wf) / N
    fr, fi = np.cos(tw) / N, -np.sin(tw) / N
    tj = 2 * np.pi * np.outer(ROW_HF, y) / N
    cc = ROW_C[:, None] == 0
    inv_re = np.where(cc, np.cos(tj), -np.sin(tj))
    inv_im = np.where(cc, np.sin(tj), np.cos(tj))
    inv_w = np.zeros((P, N))
    m = np.where(wf == 0, 1.0, 2.0)[:, None]
    inv_w[0:MF] = m * np.cos(tw.T)
    inv_w[64:64 + MF] = -m * np.sin(tw.T)
    sym = np.zeros((P, P))
    for r in range(P):
        part = -ROW_HF[r] if ROW_HF[r] != -32 else -32
        r2 = int(np.nonzero((ROW_HF == part) & (ROW_C == ROW_C[r]))[0][0])
        sym[r, r] += 32.0
        sym[r, r2] += 32.0 if ROW_C[r] == 0 else -32.0
    wt = np.full((P, MF), 128.0)
    wt[:, 0] = 64.0
    wt[:64, :17] = 0.0
    wt[(ROW_HF == -32) & (ROW_C == 1), 0] = 0.0
    lw = np.full((P, JT), 128.0)
    lw[:64, 0] = 64.0
    hf = (np.arange(N) + 64) % N
    t0 = 2 * np.pi * np.outer(y, hf) / N
    g1 = np.concatenate([np.cos(t0), -np.sin(t0)], 1) / N
    wj = 64 - np.arange(NF)
    tj0 = 2 * np.pi * np.outer(y, wj) / N
    ar, ai = np.cos(tj0) / N, -np.sin(tj0) / N
    m0 = np.where((wj == 0) | (wj == 64), 1.0, 2.0)[:, None]
    k0 = np.concatenate([m0 * np.cos(tj0.T), (-m0 * np.sin(tj0.T))[1:64]], 0)
    grp = (np.arange(N)[:, None] // GRP == np.arange(N)[None, :] // GRP) / PERGRP
    return pack([
        ("f1", f1), ("ga", np.concatenate([fr, -fi], 1)), ("gb", np.concatenate([fi, fr], 1)),
        ("inv_re", inv_re), ("inv_im", inv_im), ("inv_w", inv_w), ("sym", sym), ("wt", wt), ("lw", lw),
        ("g1", g1), ("g2a", np.concatenate([ar, ai], 1)), ("g2b", np.concatenate([-ai, ar], 1)),
        ("cos0", np.cos(t0.T)), ("sin0", np.sin(t0.T)), ("k0", k0), ("grp", grp),
        ("ones", np.ones((P, P))), ("ident", np.eye(P)), ("mask", np.tile(np.eye(32), (4, 1))),
    ])


def lay_weights(d):
    rows = np.array([[(LOW + HIGH).index(h) for h in (LOW, HIGH)[k]] for k in range(2) for c in range(2)]).reshape(-1)
    std = list(range(32)) + list(range(-32, 0))
    order = [std.index(h) for h in LOW + HIGH]

    def packed(w):
        w = w[0]
        full = np.concatenate([w, np.zeros_like(w[:, :, :1])], 2)
        even, odd = full[:, :, 0::2], full[:, :, 1::2]
        return np.concatenate([even, even, odd, odd], 1).transpose(1, 0, 2)

    def by_row(w):
        return w[:, rows, :].transpose(1, 2, 0)

    def mirrored(w):
        hs = LOW + HIGH
        out = np.zeros_like(w)
        for j, h in enumerate(hs):
            if -h in hs:
                out[:, j] = w[:, hs.index(-h)]
        return out

    groups = {"small": [], "qk": [], "vp": []}
    for c, name in ((0, "r"), (1, "i")):
        q, k = d["L1_conv_Qcw"][..., c], d["L1_conv_Kcw"][..., c]
        v = np.zeros((NH, HM, MF), np.float32)
        v[:, :32, :17] = d["L1_conv_Vcw"][0, ..., c]
        q0 = np.zeros((NH, HM), np.float32)
        q0[:, :32] = q[0, :, :, 0]
        groups["qk"] += [("q_" + name, packed(q)), ("k_" + name, packed(k)), ("qrev_" + name, mirrored(q0)[:, rows].T)]
        groups["vp"] += [("v_" + name, by_row(v)), ("vrev_" + name, mirrored(v[:, :, 0])[:, rows].T),
                         ("p_" + name, by_row(d["L1_conv_Pcw"][:, 0, ..., c][:, order]))]
        groups["small"] += [("m0_" + name, by_row(d["L1_conv_m0cw"][:, 0, ..., c][:, order])),
                            ("m1_" + name, by_row(d["L1_conv_m1cw"][:, 0, ..., c][:, order]))]
    for name in ("Qsw", "Ksw", "Vsw", "Psw"):
        groups["small"].append((name, np.broadcast_to(d["L1_conv_" + name].reshape(1, NH), (P, NH))))
    for name in ("norm1_w", "norm1_b", "attn_w", "attn_b", "norm2_w", "norm2_b", "m0sw", "m1sw", "mon_w", "mon_b"):
        groups["small"].append((name, np.broadcast_to(d["L1_conv_" + name].reshape(1, 1), (P, 1))))
    parts = groups["small"] + groups["qk"] + groups["vp"]
    return pack(parts)


START = {}


def begins(s):
    return START.get((s[0] if isinstance(s, list) else s).name, 0)


def at(s, u):
    return s[u] if isinstance(s, list) else s


def now(s, i, u, by=1):
    return at(s, u), (by * (i + 1) if isinstance(s, list) else by * (2 * i + u + 1)) + begins(s)


def prev(s, i, u, by=1):
    assert begins(s) > 0 or (u and not isinstance(s, list))
    return (s[1 - u], by * (i + u) + begins(s)) if isinstance(s, list) else (s, by * (2 * i + u) + begins(s))


def prev2(s, i, u, by=1):
    assert begins(s) > 0
    return s[u], by * i + begins(s)


def done(s, steps, by=1):
    return by * steps + begins(s)


def build(nc, x, w_re, w_im, consts, cat, weights, wat, out):
    x1_d = nc.dram_tensor("x1_d", (B, T, N, N), F32).ap()
    g_d = nc.dram_tensor("g_d", (B, T, N, N), F32).ap()
    z_d = nc.dram_tensor("z_d", (B, T, N, N), F32).ap()
    y_d = nc.dram_tensor("y_d", (B, T, N, N), F32).ap()
    c0_d = nc.dram_tensor("c0_d", (B, T, N, N), F32).ap()
    c1_d = nc.dram_tensor("c1_d", (B, T, N, N), F32).ap()
    m_d = nc.dram_tensor("m_d", (B, T, N, N), F32).ap()
    xs_d = nc.dram_tensor("xs_d", (N, 2, T, B, NF), F32).ap()
    ds_d = nc.dram_tensor("ds_d", (N, T, B, ND), F32).ap()

    whole = ExitStack()
    pending, in_stage = [], []

    def sem(name, n=None, starts=0):
        if n is not None:
            return [sem(f"{name}{i}", None, starts) for i in range(n)]
        s = nc.alloc_semaphore(name)
        in_stage.append(s)
        if starts:
            START[s.name] = starts
            pending.append(s)
        return s

    def pool_dma_sem(name):
        return [nc.alloc_semaphore(f"{name}{u}") for u in range(2)]

    def free_all(eng):
        for s in pending:
            eng.sem_inc(s, START[s.name])
        pending.clear()

    def end_stage():
        with nc.Block() as block:
            @block.gpsimd
            def _(pool):
                for s in in_stage:
                    pool.sem_clear(s)
        for s in in_stage:
            nc.release_semaphore(s)
        in_stage.clear()

    def chunk_of(t, c):
        return t.rearrange("b t y w -> (b t) y w")[bass.ds(c * CH, CH), :, :].rearrange("n y w -> y n w")

    def channel_of(t, c):
        return t[:, bass.ds(c, 1), :, :].rearrange("b o y w -> y (b o) w")

    with whole:
        def keep(name, cols):
            return whole.enter_context(nc.sbuf_tensor(name, [P, cols], F32))

        cst = keep("cst", consts.shape[1])
        stats = keep("stats", 16)
        def K(name, lo=0, hi=P):
            a, n = cat[name]
            return cst[lo:hi, a:a + n]

        ps = [whole.enter_context(nc.psum_tensor(f"bank{i}", [P, 512], F32)) for i in range(8)]
        gn_scale = keep("gn_scale", B)
        gn_shift = keep("gn_shift", B)

        def linker(eng, link):
            count = [0]

            def run(ins):
                count[0] += 1
                ins.then_inc(link, 1)
                eng.wait_ge(link, count[0])
            return run

        def inv_std(dve, link, v, r, tmp, var_ready, root_ready, n):
            nc.vector.tensor_scalar(v, v, 0.0, EPS, ALU.max, ALU.add).then_inc(var_ready, 1)
            dve.wait_ge(root_ready, n)
            link(nc.vector.reciprocal(r, r))
            link(nc.vector.tensor_tensor(tmp, r, r, ALU.mult))
            link(nc.vector.tensor_tensor(tmp, tmp, v, ALU.mult))
            link(nc.vector.tensor_scalar(tmp, tmp, -0.5, 1.5, ALU.mult, ALU.add))
            link(nc.vector.tensor_tensor(r, r, tmp, ALU.mult))

        with ExitStack() as st:
            def sb(name, cols):
                return st.enter_context(nc.sbuf_tensor(name, [P, cols], F32))
            xin = [sb(f"s0_x{u}", CW) for u in range(2)]
            sq = [sb(f"s0_q{u}", CW) for u in range(2)]
            acc, acq = sb("s0_sum", CW), sb("s0_sumsq", CW)
            cols, grp, tmp = sb("s0_cols", 16), sb("s0_grp", 16), sb("s0_tmp", 8)
            const_in, zeroed = sem("const_in"), sem("s0_zeroed")
            x_in = sem("s0_x_in", 2)
            squared, summed, sqsummed = (sem("s0_" + n, 2, 1) for n in ("squared", "summed", "sqsummed"))
            lk, col_ps, col_sb, grp_ps, var_ready, root_ready = (
                sem("s0_" + n) for n in ("link", "col_ps", "col_sb", "grp_ps", "var_ready", "root_ready"))
            with nc.Block() as block:
                @block.sync
                def _(sp):
                    sp.dma_start(cst[:, :], consts).then_inc(const_in, 16)
                    with sp.Fori(0, T // 2) as i:
                        for u in range(2):
                            sp.wait_ge(*prev2(summed, i, u))
                            sp.wait_ge(*prev2(squared, i, u))
                            sp.dma_start(xin[u][:, :], channel_of(x, 2 * i + u)).then_inc(x_in[u], 16)

                @block.gpsimd
                def _(pool):
                    free_all(pool)

                @block.scalar
                def _(act):
                    with act.Fori(0, T // 2) as i:
                        for u in range(2):
                            act.wait_ge(x_in[u], 16 * i + 16)
                            act.wait_ge(*prev2(sqsummed, i, u))
                            nc.scalar.activation(sq[u][:, :], xin[u][:, :], ACT.Square).then_inc(squared[u], 1)
                    act.wait_ge(var_ready, 1)
                    nc.scalar.activation(gn_scale[:, :], grp[:, 8:16], ACT.Sqrt).then_inc(root_ready, 1)

                @block.vector
                def _(dve):
                    nc.vector.memset(acc[:, :], 0.0).then_inc(zeroed, 1)
                    nc.vector.memset(acq[:, :], 0.0).then_inc(zeroed, 1)
                    dve.wait_ge(zeroed, 2)
                    with dve.Fori(0, T // 2) as i:
                        for u in range(2):
                            dve.wait_ge(x_in[u], 16 * i + 16)
                            dve.wait_ge(*prev(summed, i, u))
                            nc.vector.tensor_tensor(acc[:, :], acc[:, :], xin[u][:, :], ALU.add).then_inc(summed[u], 1)
                            dve.wait_ge(*now(squared, i, u))
                            dve.wait_ge(*prev(sqsummed, i, u))
                            nc.vector.tensor_tensor(acq[:, :], acq[:, :], sq[u][:, :], ALU.add).then_inc(sqsummed[u], 1)
                    link = linker(dve, lk)
                    dve.wait_ge(col_ps, 1)
                    nc.vector.tensor_copy(cols[:, :], ps[0][:, 0:16]).then_inc(col_sb, 1)
                    dve.wait_ge(grp_ps, 1)
                    link(nc.vector.tensor_copy(grp[:, :], ps[1][:, 0:16]))
                    mean, var = grp[:, 0:8], grp[:, 8:16]
                    link(nc.vector.tensor_tensor(tmp[:, :], mean, mean, ALU.mult))
                    link(nc.vector.tensor_tensor(var, var, tmp[:, :], ALU.subtract))
                    inv_std(dve, link, var, gn_scale[:, :], tmp[:, :], var_ready, root_ready, 1)
                    link(nc.vector.tensor_tensor(gn_shift[:, :], mean, gn_scale[:, :], ALU.mult))
                    link(nc.vector.tensor_scalar_mul(gn_shift[:, :], gn_shift[:, :], -1.0))

                @block.tensor
                def _(pe):
                    pe.wait_ge(const_in, 16)
                    for u in range(2):
                        pe.wait_ge(summed[u], done(summed, T // 2))
                        pe.wait_ge(sqsummed[u], done(sqsummed, T // 2))
                    for b in range(B):
                        for h, a in ((0, acc), (8, acq)):
                            last = nc.tensor.matmul(ps[0][:, h + b:h + b + 1], a[:, b * N:(b + 1) * N],
                                                    K("ones")[:, 0:1], start=True, stop=True)
                    last.then_inc(col_ps, 1)
                    pe.wait_ge(col_sb, 1)
                    nc.tensor.matmul(ps[1][:, 0:16], K("grp"), cols[:, :], start=True, stop=True).then_inc(grp_ps, 1)

        end_stage()

        with ExitStack() as st:
            def sb(name, cols):
                return st.enter_context(nc.sbuf_tensor(name, [P, cols], F32))
            xin = [sb(f"s1_x{u}", CW) for u in range(2)]
            rowft = sb("s1_rowft", B * 2 * N)
            spec = [sb(f"s1_spec{u}", B * ND) for u in range(2)]
            rf = rowft[:, :].rearrange("w (b r) -> w b r", b=B)
            row_act, row_dve, row_ready, col_ps = (sem("s1_" + n, 2, st) for n, st in (("row_act", 1), ("row_dve", 1), ("row_ready", 0), ("col_ps", 1)))
            row_ps = [sem("s1_row_ps0"), sem("s1_row_ps1", 2, 1)]
            col_act, col_dve = ([sem(f"s1_{n}{h}", 2, 1) for h in range(2)] for n in ("col_act", "col_dve"))
            x_in, stored = sem("s1_x_in", 2), pool_dma_sem("s1_stored")
            res_free = sem("s1_res_free", 2, 1)
            with nc.Block() as block:
                @block.sync
                def _(sp):
                    with sp.Fori(0, T // 2) as i:
                        for u in range(2):
                            sp.wait_ge(*prev2(row_ps[1], i, u))
                            sp.dma_start(xin[u][:, :], channel_of(x, 2 * i + u)).then_inc(x_in[u], 16)

                @block.gpsimd
                def _(pool):
                    free_all(pool)
                    with pool.Fori(0, T // 2) as i:
                        for u in range(2):
                            for h in range(2):
                                pool.wait_ge(*now(col_act[h], i, u))
                                pool.wait_ge(*now(col_dve[h], i, u))
                            for c in range(2):
                                pool.dma_start(xs_d[:, c, bass.ds(2 * i + u, 1), :, :].rearrange("s t b j -> s (t b j)"),
                                               spec[u][:, c * B * NF:(c + 1) * B * NF]).then_inc(stored[u], 16)
                            pool.wait_ge(*now(stored, i, u, 32))
                            pool.sem_inc(res_free[u], 1)

                @block.tensor
                def _(pe):
                    with pe.Fori(0, T // 2) as i:
                        for u in range(2):
                            pe.wait_ge(*now(x_in, i, u, 16))
                            for h in range(2):
                                pe.wait_ge(*prev(row_act[h], i, u))
                                pe.wait_ge(*prev(row_dve[h], i, u))
                                for k in range(4):
                                    b = 4 * h + k
                                    last = nc.tensor.matmul(ps[2 * h + k // 2][:, (k % 2) * 256:(k % 2) * 256 + 256],
                                                            xin[u][:, b * N:(b + 1) * N], K("g1"), start=True, stop=True)
                                last.then_inc(at(row_ps[h], u), 1)
                            for h in range(2):
                                pe.wait_ge(*now(row_ready[h], i, u))
                                pe.wait_ge(*prev(col_act[h], i, u))
                                pe.wait_ge(*prev(col_dve[h], i, u))
                                for k in range(4):
                                    b = 4 * h + k
                                    o = ps[4 + 2 * h + k // 2][:, (k % 2) * ND:(k % 2) * ND + ND]
                                    nc.tensor.matmul(o, rf[:, b, 0:N], K("g2a"), start=True, stop=False)
                                    last = nc.tensor.matmul(o, rf[:, b, N:2 * N], K("g2b"), start=False, stop=True)
                                last.then_inc(col_ps[h], 1)

                def copy_spectrum(eng, op, k, i, u, h, done):
                    eng.wait_ge(*now(col_ps[h], i, u))
                    o = spec[u][:, :].rearrange("s (c b j) -> s b c j", c=2, b=B)[:, 4 * h + 2 * k:4 * h + 2 * k + 2, :, :]
                    v = ps[4 + 2 * h + k][:, 0:2 * ND].rearrange("s (b c j) -> s b c j", b=2, c=2)
                    op(o, v).then_inc(done[h][u], 1)

                @block.scalar
                def _(act):
                    with act.Fori(0, T // 2) as i:
                        for u in range(2):
                            for h in range(2):
                                act.wait_ge(*now(row_ps[h], i, u))
                                act.wait_ge(*prev(col_ps[h], i, u))
                                for k in range(2):
                                    b = 4 * h + k
                                    last = nc.scalar.activation(rf[:, b, :], ps[2 * h][:, k * 256:k * 256 + 256], ACT.Copy,
                                                                scale=gn_scale[:, b:b + 1])
                                last.then_inc(row_act[h], 1)
                            act.wait_ge(*prev2(res_free, i, u))
                            for h in range(2):
                                copy_spectrum(act, nc.scalar.copy, 0, i, u, h, col_act)

                @block.vector
                def _(dve):
                    with dve.Fori(0, T // 2) as i:
                        for u in range(2):
                            for h in range(2):
                                dve.wait_ge(*now(row_ps[h], i, u))
                                dve.wait_ge(*prev(col_ps[h], i, u))
                                for k in range(2):
                                    b = 4 * h + 2 + k
                                    last = nc.vector.tensor_scalar(rf[:, b, :], ps[2 * h + 1][:, k * 256:k * 256 + 256],
                                                                   gn_scale[:, b:b + 1], None, ALU.mult)
                                last.then_inc(row_dve[h], 1)
                                dve.wait_ge(*now(row_act[h], i, u))
                                dve.wait_ge(*now(row_dve[h], i, u))
                                dc = rf[:, 4 * h:4 * h + 4, 64:65]
                                nc.vector.tensor_tensor(dc, dc, gn_shift[:, 4 * h:4 * h + 4].rearrange("w (b o) -> w b o", o=1),
                                                        ALU.add).then_inc(row_ready[h], 1)
                            dve.wait_ge(*prev2(res_free, i, u))
                            for h in range(2):
                                copy_spectrum(dve, nc.vector.tensor_copy, 1, i, u, h, col_dve)
        end_stage()

        with ExitStack() as st:
            def sb(name, cols):
                return st.enter_context(nc.sbuf_tensor(name, [P, cols], F32))
            GJ = 13
            SLOTS = 4
            wt = [sb(f"s2_w{u}", T * 4 * NF) for u in range(2)]
            mov = [sb(f"s2_x{q}", 2 * 2 * B * NF) for q in range(SLOTS)]
            res = [sb(f"s2_d{u}", 2 * B * ND) for u in range(2)]
            wv = [w[:, :].rearrange("p (o q j) -> p q j o", q=4, j=NF) for w in wt]
            mv = [m[:, :].rearrange("p (f a n) -> p f a n", f=2, a=2) for m in mov]
            w_in, stored, x_in = sem("s2_w_in", 2), pool_dma_sem("s2_stored"), sem("s2_x_in", SLOTS)
            res_free = sem("s2_res_free", 2, 1)
            turned_re, turned_im = sem("s2_turned_re", SLOTS), sem("s2_turned_im", SLOTS)
            used = [sem(f"s2_used{q}", None, 1) for q in range(SLOTS - 1)] + [sem("s2_used3", 2, 1)]
            group_ps, copied = sem("s2_group_ps", 4), sem("s2_copied", 5, 1)
            cleared = sem("s2_cleared")
            NC = N // 8
            with nc.Block() as block:
                @block.sync
                def _(sp):
                    sp.wait_ge(cleared, SLOTS)
                    with sp.Fori(0, NC // 2) as i:
                        for u in range(2):
                            s0 = 16 * i + 8 * u
                            sp.wait_ge(*prev2(used[3], i, u))
                            for f in range(2):
                                for c, w in ((0, w_re), (1, w_im)):
                                    p0 = 64 * f + 32 * c
                                    sp.dma_start(wt[u][p0:p0 + 32, :].rearrange("i (o n) -> i o n", o=T),
                                                 w[:, :, bass.ds(s0 + 4 * f, 4), :].rearrange("i o s j -> i o (s j)")
                                                 ).then_inc(w_in[u], 16)
                            for q in range(4):
                                sp.wait_ge(*prev(used[q], i, u))
                                for f in range(2):
                                    sp.dma_start(mv[q][64 * f:64 * f + 64, f, 0, :],
                                                 xs_d[bass.ds(s0 + 4 * f + q, 1), :, :, :, :].rearrange("s c t b j -> (s c t) (b j)")
                                                 ).then_inc(x_in[q], 16)

                @block.gpsimd
                def _(pool):
                    free_all(pool)
                    for q in range(SLOTS):
                        nc.gpsimd.memset(mov[q][:, :], 0.0).then_inc(cleared, 1)
                    with pool.Fori(0, NC // 2) as i:
                        for u in range(2):
                            for g in range(5):
                                pool.wait_ge(*now(copied[g], i, u))
                            for f in range(2):
                                pool.dma_start(ds_d[bass.ds(16 * i + 8 * u + 4 * f, 4), :, :, :].rearrange("s o b n -> (s o) (b n)"),
                                               res[u][:, f * B * ND:(f + 1) * B * ND]).then_inc(stored[u], 16)
                            pool.wait_ge(*now(stored, i, u, 32))
                            pool.sem_inc(res_free[u], 1)

                @block.tensor
                def _(pe):
                    with pe.Fori(0, NC // 2) as i:
                        for u in range(2):
                            pe.wait_ge(*now(w_in, i, u, 64))
                            for q in range(4):
                                pe.wait_ge(x_in[q], 64 * i + 32 * (u + 1))
                                pe.wait_ge(turned_re[q], 4 * i + 2 * u + 2)
                                pe.wait_ge(turned_im[q], 4 * i + 2 * u + 2)
                                for g in range(5):
                                    if q == 0:
                                        pe.wait_ge(*prev(copied[g], i, u))
                                    for jj in range(GJ):
                                        j = g * GJ + jj
                                        last = nc.tensor.matmul(
                                            ps[g][32 * q:32 * q + 32, 32 * jj:32 * jj + 32], wv[u][:, q, j, :],
                                            mov[q][:, :].rearrange("p (n j) -> p j n", j=NF)[:, j, :], start=True, stop=True)
                                    if q == 3 and g < 4:
                                        last.then_inc(group_ps[g], 1)
                                last.then_inc(at(used[q], u), 1)

                def turn(eng, op, c, done, i, u):
                    sign = 1.0 if c == 0 else -1.0
                    for q in range(4):
                        eng.wait_ge(x_in[q], 64 * i + 32 * (u + 1))
                        for f in range(2):
                            p0, p1 = 64 * f + 32 * c, 64 * f + 32 * (1 - c)
                            op(mv[q][p0:p0 + 32, f, 1, :], mv[q][p1:p1 + 32, f, 0, :], sign).then_inc(done[q], 1)

                def copy_out(eng, op, mine, i, u):
                    eng.wait_ge(*prev2(res_free, i, u))
                    for g in mine:
                        if g < 4:
                            eng.wait_ge(*now(group_ps[g], i, u))
                        else:
                            eng.wait_ge(*now(used[3], i, u))
                        v = ps[g][:, 0:32 * GJ].rearrange("p (j f a b) -> p f a b j", f=2, a=2, b=B)
                        d = res[u][:, :].rearrange("p (f b n) -> p f b n", f=2, b=B)
                        both = res[u][:, :].rearrange("p (f b n) -> p f b n", f=2, b=B)[:, :, :, 1:129]                             .rearrange("p f b (a j) -> p f a b j", a=2)
                        lo, hi = g * GJ, min((g + 1) * GJ, NF - 1)
                        for f in range(2):
                            if g == 0:
                                op(d[:, f, :, 1:2], v[:, f, 0, :, 0:1])
                                op(d[:, f, :, 0:1], v[:, f, 1, :, 0:1])
                                lo = 1
                            if g == 4:
                                op(d[:, f, :, 65:66], v[:, f, 0, :, GJ - 1:GJ])
                                op(d[:, f, :, 129:130], v[:, f, 1, :, GJ - 1:GJ])
                            last = op(both[:, f, :, :, lo:hi], v[:, f, :, :, lo - g * GJ:hi - g * GJ])
                        last.then_inc(copied[g], 1)

                @block.scalar
                def _(act):
                    with act.Fori(0, NC // 2) as i:
                        for u in range(2):
                            turn(act, nc.scalar.mul, 0, turned_re, i, u)
                            copy_out(act, nc.scalar.copy, (0, 2), i, u)

                @block.vector
                def _(dve):
                    with dve.Fori(0, NC // 2) as i:
                        for u in range(2):
                            turn(dve, nc.vector.tensor_scalar_mul, 1, turned_im, i, u)
                            copy_out(dve, nc.vector.tensor_copy, (1, 3, 4), i, u)
        end_stage()

        with ExitStack() as st:
            def sb(name, cols):
                return st.enter_context(nc.sbuf_tensor(name, [P, cols], F32))
            gn2_scale, gn2_shift = keep("gn2_scale", B * 32), keep("gn2_shift", B * 32)
            xin = [sb(f"s3_x{u}", CW) for u in range(2)]
            sp_in = [sb(f"s3_d{u}", B * ND) for u in range(2)]
            sp_neg = [sb(f"s3_n{u}", B * N) for u in range(2)]
            half = [sb(f"s3_h{h}", 4 * N) for h in range(2)]
            x1 = [sb(f"s3_x1_{u}", CW) for u in range(2)]
            sq = sb("s3_sq", CW)
            acc, acq = sb("s3_sum", CW), sb("s3_sumsq", CW)
            grp, tmp = sb("s3_grp", 512), sb("s3_tmp", 256)
            x_in, d_in, negated, stored = sem("s3_x_in", 2), sem("s3_d_in", 2), sem("s3_negated", 2), pool_dma_sem("s3_stored")
            res_free = sem("s3_res_free", 2, 1)
            col_ps = [sem("s3_col_ps0"), sem("s3_col_ps1", 2, 1)]
            col_sb, row_ps = sem("s3_col_sb", 2, 1), sem("s3_row_ps", 2, 1)
            added = [sem("s3_added0", 2, 1), sem("s3_added1", 2, 1)]
            squared, summed, sqsummed = (sem("s3_" + n, None, 1) for n in ("squared", "summed", "sqsummed"))
            zeroed, tot_ps, lk, var_ready, root_ready = (sem("s3_" + n) for n in ("zeroed", "tot_ps", "link", "var_ready", "root_ready"))
            with nc.Block() as block:
                @block.sync
                def _(sp):
                    with sp.Fori(0, T // 2) as i:
                        for u in range(2):
                            sp.wait_ge(*prev2(col_ps[1], i, u))
                            sp.dma_start(sp_in[u][:, :], ds_d[:, bass.ds(2 * i + u, 1), :, :].rearrange("s o b n -> s (o b n)")
                                         ).then_inc(d_in[u], 16)
                            sp.wait_ge(*prev2(added[1], i, u))
                            sp.dma_start(xin[u][:, :], channel_of(x, 2 * i + u)).then_inc(x_in[u], 16)

                @block.gpsimd
                def _(pool):
                    free_all(pool)
                    with pool.Fori(0, T // 2) as i:
                        for u in range(2):
                            for h in range(2):
                                pool.wait_ge(*now(added[h], i, u))
                            pool.dma_start(channel_of(x1_d, 2 * i + u), x1[u][:, :]).then_inc(stored[u], 16)
                            pool.wait_ge(*now(stored, i, u, 16))
                            pool.sem_inc(res_free[u], 1)

                @block.tensor
                def _(pe):
                    with pe.Fori(0, T // 2) as i:
                        for u in range(2):
                            pe.wait_ge(*now(d_in, i, u, 16))
                            pe.wait_ge(*now(negated, i, u, 3))
                            d = sp_in[u][:, :].rearrange("s (b n) -> s b n", b=B)
                            n = sp_neg[u][:, :].rearrange("s (b n) -> s b n", b=B)
                            for h in range(2):
                                pe.wait_ge(*prev(col_sb[h], i, u))
                                for k in range(4):
                                    o = ps[h][:, k * N:(k + 1) * N]
                                    nc.tensor.matmul(o, d[:, 4 * h + k, 1:129], K("cos0"), start=True, stop=False)
                                    last = nc.tensor.matmul(o, n[:, 4 * h + k, :], K("sin0"), start=False, stop=True)
                                last.then_inc(at(col_ps[h], u), 1)
                            for h in range(2):
                                pe.wait_ge(*now(col_sb[h], i, u))
                                pe.wait_ge(*prev(added[h], i, u))
                                for k in range(4):
                                    last = nc.tensor.matmul(ps[2 + h][:, k * N:(k + 1) * N], half[h][:, k * N:(k + 1) * N],
                                                            K("k0"), start=True, stop=True)
                                last.then_inc(row_ps[h], 1)
                    pe.wait_ge(summed, done(summed, T))
                    pe.wait_ge(sqsummed, done(sqsummed, T))
                    for k in range(2):
                        nc.tensor.matmul(ps[4 + k][:, :], K("ones"), acc[:, k * 512:(k + 1) * 512], start=True, stop=True)
                        last = nc.tensor.matmul(ps[6 + k][:, :], K("ones"), acq[:, k * 512:(k + 1) * 512], start=True, stop=True)
                    last.then_inc(tot_ps, 1)

                @block.scalar
                def _(act):
                    with act.Fori(0, T // 2) as i:
                        for u in range(2):
                            for h in range(2):
                                act.wait_ge(*now(col_ps[h], i, u))
                                act.wait_ge(*prev(row_ps[h], i, u))
                                nc.scalar.copy(half[h][:, :], ps[h][:, :]).then_inc(col_sb[h], 1)
                            for h in range(2):
                                act.wait_ge(*now(added[h], i, u))
                            act.wait_ge(*prev(sqsummed, i, u))
                            nc.scalar.activation(sq[:, :], x1[u][:, :], ACT.Square).then_inc(squared, 1)
                    act.wait_ge(var_ready, 1)
                    nc.scalar.activation(gn2_scale[:, :], grp[:, 256:512], ACT.Sqrt).then_inc(root_ready, 1)

                @block.vector
                def _(dve):
                    nc.vector.memset(acc[:, :], 0.0).then_inc(zeroed, 1)
                    nc.vector.memset(acq[:, :], 0.0).then_inc(zeroed, 1)
                    dve.wait_ge(zeroed, 2)
                    with dve.Fori(0, T // 2) as i:
                        for u in range(2):
                            dve.wait_ge(*now(d_in, i, u, 16))
                            dve.wait_ge(*prev2(col_ps[1], i, u))
                            d = sp_in[u][:, :].rearrange("s (b n) -> s b n", b=B)
                            n = sp_neg[u][:, :].rearrange("s (b n) -> s b n", b=B)
                            nc.vector.tensor_scalar_mul(n[:, :, 0:1], d[:, :, 0:1], -1.0).then_inc(negated[u], 1)
                            nc.vector.tensor_scalar_mul(n[:, :, 1:65], d[:, :, 66:130], -1.0).then_inc(negated[u], 1)
                            nc.vector.tensor_copy(n[:, :, 65:128], d[:, :, 2:65]).then_inc(negated[u], 1)
                            dve.wait_ge(*now(x_in, i, u, 16))
                            dve.wait_ge(*prev2(res_free, i, u))
                            for h in range(2):
                                dve.wait_ge(*now(row_ps[h], i, u))
                                nc.vector.tensor_tensor(x1[u][:, 512 * h:512 * h + 512], ps[2 + h][:, :],
                                                        xin[u][:, 512 * h:512 * h + 512], ALU.add).then_inc(added[h][u], 1)
                            for h in range(2):
                                dve.wait_ge(*now(added[h], i, u))
                            dve.wait_ge(*prev(summed, i, u))
                            nc.vector.tensor_tensor(acc[:, :], acc[:, :], x1[u][:, :], ALU.add).then_inc(summed, 1)
                            dve.wait_ge(*now(squared, i, u))
                            dve.wait_ge(*prev(sqsummed, i, u))
                            nc.vector.tensor_tensor(acq[:, :], acq[:, :], sq[:, :], ALU.add).then_inc(sqsummed, 1)
                    link = linker(dve, lk)
                    dve.wait_ge(tot_ps, 1)
                    for k in range(2):
                        for q, c0 in ((4, 0), (6, 256)):
                            link(nc.vector.tensor_reduce(grp[:, c0 + 128 * k:c0 + 128 * k + 128],
                                                         ps[q + k][:, :].rearrange("p (g j) -> p g j", j=GRP), AX.X, ALU.add))
                    link(nc.vector.tensor_scalar_mul(grp[:, :], grp[:, :], 1.0 / PERGRP))
                    mean, var = grp[:, 0:256], grp[:, 256:512]
                    link(nc.vector.tensor_tensor(tmp[:, :], mean, mean, ALU.mult))
                    link(nc.vector.tensor_tensor(var, var, tmp[:, :], ALU.subtract))
                    inv_std(dve, link, var, gn2_scale[:, :], tmp[:, :], var_ready, root_ready, 1)
                    link(nc.vector.tensor_tensor(gn2_shift[:, :], mean, gn2_scale[:, :], ALU.mult))
                    link(nc.vector.tensor_scalar_mul(gn2_shift[:, :], gn2_shift[:, :], -1.0))
        end_stage()

        spec_u = keep("spec_u", MF * NIMG)
        spec_o = keep("spec_o", MF * NIMG)
        probs_bd = keep("probs_bd", 2 * NH * P)
        img_sum, img_sumsq = keep("img_sum", NIMG), keep("img_sumsq", NIMG)
        small = keep("small", wat["q_r"][0])
        def W(name, tile, base):
            a, n = wat[name]
            return tile[:, a - base:a - base + n]

        def SM(name):
            return W(name, small, 0)
        mix_t, mix_const = keep("mix_t", 2 * P), keep("mix_const", 2)
        turned = ExitStack()
        spec_v = turned.enter_context(nc.sbuf_tensor("spec_v", [P, MF * NIMG], F32))
        NT = NIMG // CH // 2

        def images(tile):
            return tile[:, :].rearrange("p (f n) -> p n f", n=NIMG)

        def forward_pe(pe, i, u, tile, ready, rf, row_ps, row_sb, col_ps, col_free):
            pe.wait_ge(*now(ready, i, u))
            for h in range(2):
                for free in row_sb[h]:
                    pe.wait_ge(*prev(free, i, u))
                for k in range(4):
                    last = nc.tensor.matmul(ps[2 * h + k // 2][:, (k % 2) * 256:(k % 2) * 256 + 256],
                                            tile[:, (4 * h + k) * N:(4 * h + k + 1) * N], K("f1"), start=True, stop=True)
                last.then_inc(row_ps[h], 1)
            for h in range(2):
                for here in row_sb[h]:
                    pe.wait_ge(*now(here, i, u))
                pe.wait_ge(*prev(col_free[h], i, u))
                for k in range(4):
                    o = ps[4 + h][:, k * 2 * MF:(k + 1) * 2 * MF]
                    nc.tensor.matmul(o, rf[:, 4 * h + k, 0:N], K("ga"), start=True, stop=False)
                    last = nc.tensor.matmul(o, rf[:, 4 * h + k, N:2 * N], K("gb"), start=False, stop=True)
                last.then_inc(col_ps[h], 1)

        def copy_rows(eng, op, k, i, u, h, rf, row_ps, row_sb, col_ps):
            eng.wait_ge(*now(row_ps[h], i, u))
            eng.wait_ge(*prev(col_ps[h], i, u))
            op(rf[:, 4 * h + 2 * k:4 * h + 2 * k + 2, :], ps[2 * h + k][:, :].rearrange("w (n r) -> w n r", n=2)
               ).then_inc(row_sb[h][k], 1)

        with ExitStack() as st:
            def sb(name, cols):
                return st.enter_context(nc.sbuf_tensor(name, [P, cols], F32))
            xin = [sb(f"s4_x{u}", CW) for u in range(2)]
            g = [sb(f"s4_g{u}", CW) for u in range(2)]
            sq = sb("s4_sq", CW)
            shift = [sb(f"s4_shift{u}", 32) for u in range(2)]
            rf = sb("s4_rowft", CH * 2 * N)[:, :].rearrange("w (n r) -> w n r", n=CH)
            x_in, scaled, stored = sem("s4_x_in", 2), sem("s4_scaled", 2, 2), sem("s4_stored", 2, 16)
            g_ready, squared, reduced = sem("s4_g_ready"), sem("s4_squared"), sem("s4_reduced", None, 1)
            row_ps, col_ps = sem("s4_row_ps", 2), sem("s4_col_ps", 2, 1)
            row_sb = [sem(f"s4_row_sb{h}_", 2, 1) for h in range(2)]
            col_sb = sem("s4_col_sb", 2, 1)
            small_in = sem("s4_small_in")

            with nc.Block() as block:
                @block.sync
                def _(sp):
                    sp.dma_start(small[:, :], weights[:, 0:wat["q_r"][0]]).then_inc(small_in, 16)
                    with sp.Fori(0, NT) as i:
                        for u in range(2):
                            sp.wait_ge(*prev2(scaled, i, u, 2))
                            sp.dma_start(xin[u][:, :], chunk_of(x1_d, 2 * i + u)).then_inc(x_in[u], 16)
                    sp.wait_ge(small_in, 16)

                @block.gpsimd
                def _(pool):
                    free_all(pool)
                    with pool.Fori(0, NT) as i:
                        for u in range(2):
                            pool.wait_ge(*now(scaled, i, u, 2))
                            gv = g[u][:, :].rearrange("y (n g j) -> y n g j", n=CH, j=GRP)
                            sh = shift[u][:, :].unsqueeze(1).unsqueeze(3).broadcast_to([P, CH, 32, GRP])
                            nc.gpsimd.tensor_tensor(gv, gv, sh, ALU.add).then_inc(g_ready, 1)

                @block.tensor
                def _(pe):
                    with pe.Fori(0, NT) as i:
                        for u in range(2):
                            forward_pe(pe, i, u, g[u], g_ready, rf, row_ps, row_sb, col_ps, col_sb)

                def copy_cols(eng, op, i, u, h):
                    eng.wait_ge(*now(col_ps[h], i, u))
                    v = ps[4 + h][:, 0:8 * MF].rearrange("r (n a f) -> r a n f", n=4, a=2)
                    op(images(spec_u)[:, bass.ds(16 * i + 8 * u + 4 * h, 4), :], v[:, 0])
                    op(images(spec_v)[:, bass.ds(16 * i + 8 * u + 4 * h, 4), :], v[:, 1]).then_inc(col_sb[h], 1)

                @block.scalar
                def _(act):
                    with act.Fori(0, NT) as i:
                        for u in range(2):
                            act.wait_ge(*now(g_ready, i, u))
                            act.dma_start(chunk_of(g_d, 2 * i + u), g[u][:, :]).then_inc(stored[u], 16)
                            for h in range(2):
                                copy_rows(act, nc.scalar.copy, 0, i, u, h, rf, row_ps, row_sb, col_ps)
                            act.wait_ge(*prev(reduced, i, u))
                            nc.scalar.activation(sq[:, :], g[u][:, :], ACT.Square).then_inc(squared, 1)
                            copy_cols(act, nc.scalar.copy, i, u, 0)
                    for u in range(2):
                        act.wait_ge(stored[u], done(stored, NT, 16))

                @block.vector
                def _(dve):
                    def scale(i, u):
                        dve.wait_ge(*now(x_in, i, u, 16))
                        dve.wait_ge(*prev2(stored, i, u, 16))
                        nc.vector.tensor_copy(shift[u][:, :], gn2_shift[:, bass.ds((i // 2) * 32, 32)]).then_inc(scaled[u], 1)
                        v = xin[u][:, :].rearrange("y (n g j) -> y n g j", n=CH, j=GRP)
                        sc = gn2_scale[:, bass.ds((i // 2) * 32, 32)].unsqueeze(1).unsqueeze(3).broadcast_to([P, CH, 32, GRP])
                        nc.vector.tensor_tensor(g[u][:, :].rearrange("y (n g j) -> y n g j", n=CH, j=GRP), v, sc,
                                                ALU.mult).then_inc(scaled[u], 1)

                    def turn(i, last):
                        for u in range(2):
                            copy_rows(dve, nc.vector.tensor_copy, 1, i, u, 0, rf, row_ps, row_sb, col_ps)
                            copy_rows(dve, nc.vector.tensor_copy, 1, i, u, 1, rf, row_ps, row_sb, col_ps)
                            dve.wait_ge(*now(g_ready, i, u))
                            c = bass.ds(16 * i + 8 * u, CH)
                            nc.vector.tensor_reduce(img_sum[:, c], g[u][:, :].rearrange("y (n w) -> y n w", n=CH), AX.X, ALU.add)
                            dve.wait_ge(*now(squared, i, u))
                            nc.vector.tensor_reduce(img_sumsq[:, c], sq[:, :].rearrange("y (n w) -> y n w", n=CH), AX.X,
                                                    ALU.add).then_inc(reduced, 1)
                            if not (last and u):
                                scale(i + u, 1 - u)
                            copy_cols(dve, nc.vector.tensor_copy, i, u, 1)
                    scale(0, 0)
                    with dve.Fori(0, NT - 1) as i:
                        turn(i, False)
                    turn(NT - 1, True)
        end_stage()

        with ExitStack() as st:
            def sb(name, cols):
                return st.enter_context(nc.sbuf_tensor(name, [P, cols], F32))
            qk_base, qk_end = wat["q_r"][0], wat["v_r"][0]
            qk = sb("s5_qk", qk_end - qk_base)
            def QK(name):
                return W(name, qk, qk_base)
            NJ = NH * JT
            sym_r, sym_i, g_r, g_i, tmp = (sb("s5_" + n, NJ) for n in ("sym_r", "sym_i", "g_r", "g_i", "tmp"))
            mean, ex2, r, r_tmp = (sb("s5_" + n, NIMG + 2) for n in ("mean", "ex2", "r", "r_tmp"))
            low_u, low_v = sb("s5_low_u", JT * NIMG), sb("s5_low_v", JT * NIMG)
            JI = JT * NIMG
            part = [probs_bd[:, 0:JI], sb("s5_part1", JI)[:, :]]
            prod = [probs_bd[:, JI:2 * JI], probs_bd[:, 2 * JI:3 * JI]]
            scores = sb("s5_scores", 2 * NH * 32)
            common = sb("s5_common", 64)
            red = sb("s5_red", 64)
            vecn = sb("s5_vecn", NH)
            vec = sb("s5_vec", 8)
            qk_in, stat_ps, var_ready, root_ready, lk, lkp, v_done, u_done = (
                sem("s5_" + n) for n in ("qk_in", "stat_ps", "var_ready", "root_ready", "link", "linkp", "v_done", "u_done"))
            packed, sym_ps, weighted, common_ps, part_ready, root2 = (
                sem("s5_" + n) for n in ("packed", "sym_ps", "weighted", "common_ps", "part_ready", "root2"))
            prod_ready, score_ps, taken = sem("s5_prod_ready", 2, 1), sem("s5_score_ps", 2, 1), sem("s5_taken", 2, 1)
            shifted, exped, mix_ready, mix_ps, g_done = (sem("s5_" + n) for n in ("shifted", "exped", "mix_ready", "mix_ps", "g_done"))
            TU = NH // 2
            U3, V3, O3 = (t[:, :].rearrange("p (f n) -> p f n", f=MF) for t in (spec_u, spec_v, spec_o))
            LU3, LV3 = (t[:, :].rearrange("p (f n) -> p f n", f=JT) for t in (low_u, low_v))
            with nc.Block() as block:
                @block.sync
                def _(sp):
                    sp.dma_start(qk[:, :], weights[:, qk_base:qk_end]).then_inc(qk_in, 16)

                @block.tensor
                def _(pe):
                    nc.tensor.matmul(ps[0][:, 0:NIMG], K("ones"), img_sum[:, :], start=True, stop=True)
                    nc.tensor.matmul(ps[0][:, NIMG:2 * NIMG], K("ones"), img_sumsq[:, :], start=True, stop=True)
                    for gb in range(2):
                        for k, s in ((0, img_sum), (2, img_sumsq)):
                            last = nc.tensor.matmul(ps[1][:, k + gb:k + gb + 1], s[:, gb * P:(gb + 1) * P],
                                                    K("ones")[:, 0:1], start=True, stop=True)
                    last.then_inc(stat_ps, 1)
                    pe.wait_ge(u_done, 1)
                    nc.tensor.matmul(ps[2][:, 0:NIMG], K("sym"), U3[:, 32, :], start=True, stop=True).then_inc(sym_ps, 1)
                    pe.wait_ge(weighted, 1)
                    for gb in range(2):
                        for b in range(4):
                            c = slice(gb * P + 32 * b, gb * P + 32 * b + 32)
                            for f in range(MF):
                                last = nc.tensor.matmul(ps[3][32 * b:32 * b + 32, 32 * gb:32 * gb + 32], O3[:, f, c], U3[:, f, c],
                                                        start=(f == 0), stop=(f == MF - 1))
                    last.then_inc(common_ps, 1)
                    pe.wait_ge(packed, 1)
                    with pe.Fori(0, TU) as i:
                        for u in range(2):
                            pe.wait_ge(*now(prod_ready, i, u))
                            pe.wait_ge(*prev2(taken, i, u))
                            pr = prod[u].rearrange("p (f n) -> p f n", f=JT)
                            for gb in range(2):
                                for b in range(4):
                                    c = slice(gb * P + 32 * b, gb * P + 32 * b + 32)
                                    for j in range(JT):
                                        last = nc.tensor.matmul(ps[4 + u][32 * b:32 * b + 32, 32 * gb:32 * gb + 32], pr[:, j, c],
                                                                LU3[:, j, c], start=(j == 0), stop=(j == JT - 1))
                            last.then_inc(score_ps[u], 1)
                    pe.wait_ge(mix_ready, 1)
                    for gb in range(2):
                        last = nc.tensor.matmul(ps[6][:, gb:gb + 1], mix_t[:, gb * P:(gb + 1) * P], vec[:, gb:gb + 1],
                                                start=True, stop=True)
                    last.then_inc(mix_ps, 1)

                @block.scalar
                def _(act):
                    act.wait_ge(var_ready, 1)
                    nc.scalar.activation(r[:, :], ex2[:, :], ACT.Sqrt).then_inc(root_ready, 1)
                    act.wait_ge(v_done, 1)
                    act.wait_ge(u_done, 1)
                    for dst, src in ((LU3, U3), (LV3, V3)):
                        nc.scalar.copy(dst[0:64, :, :], src[0:64, 0:17:2, :])
                        last = nc.scalar.copy(dst[64:128, 0:8, :], src[0:64, 1:17:2, :])
                    last.then_inc(packed, 2)
                    act.wait_ge(packed, 2)
                    act.wait_ge(g_done, 1)
                    with act.Fori(0, TU) as i:
                        for u in range(2):
                            act.wait_ge(*prev2(prod_ready, i, u))
                            for j in range(JT):
                                last = nc.scalar.activation(part[u][:, j * NIMG:(j + 1) * NIMG], LU3[:, j, :], ACT.Copy,
                                                            scale=g_r[:, bass.ds((2 * i + u) * JT + j, 1)])
                            last.then_inc(part_ready, 1)
                    act.wait_ge(shifted, 1)
                    nc.scalar.activation(scores[:, :], scores[:, :], ACT.Exp).then_inc(exped, 1)

                @block.gpsimd
                def _(pool):
                    free_all(pool)
                    link = linker(pool, lkp)
                    link(nc.gpsimd.memset(LU3[64:128, 8, :], 0.0))
                    link(nc.gpsimd.memset(LV3[64:128, 8, :], 0.0))
                    pool.wait_ge(root2, 1)
                    rb = r[:, 0:NIMG].unsqueeze(1).broadcast_to([P, MF, NIMG])
                    link(nc.gpsimd.tensor_tensor(V3, V3, rb, ALU.mult))
                    link(nc.gpsimd.memset(V3[0:1, 0, :], 0.0))
                    link(nc.gpsimd.tensor_scalar(V3[32:33, 0, :], V3[32:33, 0, :], 0.0, SM("norm1_b")[32:33, :], ALU.mult, ALU.add))
                    pool.sem_inc(v_done, 1)

                @block.vector
                def _(dve):
                    link = linker(dve, lk)
                    tt, ts = nc.vector.tensor_tensor, nc.vector.tensor_scalar
                    dve.wait_ge(stat_ps, 1)
                    link(ts(mean[:, 0:NIMG], ps[0][:, 0:NIMG], 1.0 / PIX, None, ALU.mult))
                    link(ts(ex2[:, 0:NIMG], ps[0][:, NIMG:2 * NIMG], 1.0 / PIX, None, ALU.mult))
                    link(ts(mean[:, NIMG:NIMG + 2], ps[1][:, 0:2], 1.0 / PIX, None, ALU.mult))
                    link(ts(ex2[:, NIMG:NIMG + 2], ps[1][:, 2:4], 1.0 / PIX, None, ALU.mult))
                    link(tt(r_tmp[:, :], mean[:, :], mean[:, :], ALU.mult))
                    link(tt(ex2[:, :], ex2[:, :], r_tmp[:, :], ALU.subtract))
                    inv_std(dve, link, ex2[:, :], r[:, :], r_tmp[:, :], var_ready, root_ready, 1)
                    link(ts(r[:, :], r[:, :], SM("norm1_w"), None, ALU.mult))
                    dve.sem_inc(root2, 1)
                    rb = r[:, 0:NIMG].unsqueeze(1).broadcast_to([P, MF, NIMG])
                    link(tt(U3, U3, rb, ALU.mult))
                    link(ts(U3[0:1, 0, :], U3[0:1, 0, :], 0.0, SM("norm1_b")[0:1, :], ALU.mult, ALU.add))
                    link(nc.vector.memset(U3[32:33, 0, :], 0.0))
                    dve.sem_inc(u_done, 1)
                    link(tt(O3[:, 0:32, :], U3[:, 0:32, :], K("wt")[:, 0:32].unsqueeze(2).broadcast_to([P, 32, NIMG]), ALU.mult))
                    dve.wait_ge(sym_ps, 1)
                    link(nc.vector.tensor_copy(O3[:, 32, :], ps[2][:, 0:NIMG]))
                    dve.sem_inc(weighted, 1)
                    dve.wait_ge(qk_in, 16)
                    v3 = lambda t: t.rearrange("p (n j) -> p n j", j=JT)
                    bc = lambda name: SM(name).unsqueeze(2).broadcast_to([P, NH, JT])
                    for c, dst, op in (("r", sym_r, ALU.add), ("i", sym_i, ALU.subtract)):
                        link(nc.vector.tensor_copy(dst[:, :], QK("q_" + c)))
                        z = v3(dst[:, :])[0:64, :, 0:1]
                        link(tt(z, z, QK("qrev_" + c)[0:64, :].unsqueeze(2), op))
                        link(ts(z, z, 0.5, None, ALU.mult))
                    link(tt(v3(sym_r[:, :]), v3(sym_r[:, :]), bc("Qsw"), ALU.add))
                    link(tt(g_r[:, :], sym_r[:, :], QK("k_r"), ALU.mult))
                    link(tt(tmp[:, :], sym_i[:, :], QK("k_i"), ALU.mult))
                    link(tt(g_r[:, :], g_r[:, :], tmp[:, :], ALU.add))
                    link(tt(v3(tmp[:, :]), v3(QK("q_r")), bc("Qsw"), ALU.add))
                    link(tt(v3(tmp[:, :]), v3(tmp[:, :]), bc("Ksw"), ALU.mult))
                    link(tt(g_r[:, :], g_r[:, :], tmp[:, :], ALU.add))
                    link(tt(g_i[:, :], sym_i[:, :], QK("k_r"), ALU.mult))
                    link(tt(tmp[:, :], sym_r[:, :], QK("k_i"), ALU.mult))
                    link(tt(g_i[:, :], g_i[:, :], tmp[:, :], ALU.subtract))
                    link(tt(v3(tmp[:, :]), v3(QK("q_i")), bc("Ksw"), ALU.mult))
                    link(tt(g_i[:, :], g_i[:, :], tmp[:, :], ALU.add))
                    lw = K("lw").unsqueeze(1).broadcast_to([P, NH, JT])
                    link(tt(v3(g_r[:, :]), v3(g_r[:, :]), lw, ALU.mult))
                    link(tt(v3(g_i[:, :]), v3(g_i[:, :]), lw, ALU.mult))
                    dve.sem_inc(g_done, 1)
                    dve.wait_ge(common_ps, 1)
                    link(nc.vector.tensor_copy(common[:, :], ps[3][:, 0:64]))
                    dve.wait_ge(packed, 2)
                    sc4 = scores[:, :].rearrange("p (g n s) -> p g n s", g=2, n=NH)

                    def take(i, u):
                        dve.wait_ge(*now(score_ps, i, u))
                        nc.vector.tensor_copy(sc4[:, :, bass.ds(2 * i + u, 1), :].rearrange("p g o s -> p g (o s)"),
                                              ps[4 + u][:, 0:64].rearrange("p (g s) -> p g s", g=2)).then_inc(taken[u], 1)

                    def head_step(i, u, first):
                        dve.wait_ge(*now(part_ready, i, u))
                        dve.wait_ge(*prev2(score_ps, i, u))
                        for j in range(JT):
                            c = slice(j * NIMG, (j + 1) * NIMG)
                            last = nc.vector.scalar_tensor_tensor(
                                prod[u][:, c], LV3[:, j, :], g_i[:, bass.ds((2 * i + u) * JT + j, 1)],
                                part[u][:, c], ALU.mult, ALU.add)
                        last.then_inc(prod_ready[u], 1)
                        if not first:
                            take(i - 1 + u, 1 - u)
                    head_step(0, 0, True)
                    head_step(0, 1, False)
                    with dve.Fori(1, TU) as i:
                        for u in range(2):
                            head_step(i, u, False)
                    take(TU - 1, 1)
                    for u in range(2):
                        dve.wait_ge(taken[u], done(taken, TU))
                    big = low_u[:, 0:2 * NH * 32]
                    big4 = big.rearrange("p (g n s) -> p g n s", g=2, n=NH)
                    com = common[:, :].rearrange("p (g s) -> p g s", g=2)
                    link(tt(vecn[:, :], SM("Qsw"), SM("Ksw"), ALU.mult))
                    for gb in range(2):
                        link(tt(big4[:, gb], com[:, gb:gb + 1, :].broadcast_to([P, NH, 32]),
                                vecn[:, :].unsqueeze(2).broadcast_to([P, NH, 32]), ALU.mult))
                    link(tt(scores[:, :], scores[:, :], big, ALU.add))
                    s3 = scores[:, :].rearrange("p (m s) -> p m s", s=32)
                    rd = red[:, :].unsqueeze(2).broadcast_to([P, 64, 32])
                    link(nc.vector.tensor_reduce(red[:, :], s3, AX.X, ALU.max))
                    link(tt(s3, s3, rd, ALU.subtract))
                    dve.sem_inc(shifted, 1)
                    dve.wait_ge(exped, 1)
                    link(nc.vector.tensor_reduce(red[:, :], s3, AX.X, ALU.add))
                    link(nc.vector.reciprocal(red[:, :], red[:, :]))
                    link(tt(s3, s3, rd, ALU.mult))
                    link(nc.vector.transpose(big, scores[:, :]))
                    link(nc.vector.memset(probs_bd[:, :], 0.0))
                    bd = probs_bd[:, :].rearrange("p (m c) -> p m c", c=P)
                    for b in range(4):
                        q = slice(32 * b, 32 * b + 32)
                        link(nc.vector.tensor_copy(bd[q, :, q], big[q, :].rearrange("p (m t) -> p m t", t=32)))
                    link(tt(vecn[:, :], SM("Psw"), SM("Vsw"), ALU.mult))
                    for gb in range(2):
                        link(tt(big4[:, gb], sc4[:, gb], vecn[:, :].unsqueeze(2).broadcast_to([P, NH, 32]), ALU.mult))
                    link(nc.vector.tensor_reduce(red[:, :], big.rearrange("p (g n s) -> p g s n", g=2, n=NH), AX.X, ALU.add))
                    link(nc.vector.transpose(common[:, :], red[:, :]))
                    link(nc.vector.memset(mix_t[:, :], 0.0))
                    for b in range(4):
                        q = slice(32 * b, 32 * b + 32)
                        link(nc.vector.tensor_copy(mix_t[:, :].rearrange("p (g c) -> p g c", g=2)[q, :, q],
                                                   common[q, :].rearrange("p (g t) -> p g t", g=2)))
                    link(tt(vec[:, 0:2], r[:, NIMG:NIMG + 2], mean[:, NIMG:NIMG + 2], ALU.mult))
                    link(ts(vec[:, 0:2], vec[:, 0:2], -1.0, SM("norm1_b"), ALU.mult, ALU.add))
                    dve.sem_inc(mix_ready, 1)
                    dve.wait_ge(mix_ps, 1)
                    link(nc.vector.tensor_copy(mix_const[:, :], ps[6][:, 0:2]))
                    for gb in range(2):
                        m = mix_t[:, gb * P:(gb + 1) * P]
                        link(nc.vector.scalar_tensor_tensor(m, m, r[:, NIMG + gb:NIMG + gb + 1], K("ident"), ALU.mult, ALU.add))
        turned.close()
        end_stage()

        with ExitStack() as st:
            def sb(name, cols):
                return st.enter_context(nc.sbuf_tensor(name, [P, cols], F32))
            NM = MF * NH
            hx = sb("s6_hx", 2 * NH * P)
            vp_base = wat["v_r"][0]
            vp_cols = weights.shape[1] - vp_base
            vp = hx[:, 0:vp_cols]

            def VP(name):
                a, n = wat[name]
                return hx[:, a - vp_base:a - vp_base + n]
            diag = [sb(f"s6_diag{u}", NH * 64) for u in range(2)]
            h_r, h_i = diag[0][:, 0:NM], diag[1][:, 0:NM]
            tmp = sb("s6_tmp", NM)[:, :]
            coef = sb("s6_coef", 2 * NM)
            col = [sb(f"s6_col{u}", NIMG) for u in range(2)]
            vp_in, lk, coef_ready = sem("s6_vp_in"), sem("s6_link"), sem("s6_coef_ready")
            ready, step_done = sem("s6_ready", 2), sem("s6_step_done", 2, 1)
            bank_ps, bank_sb = sem("s6_bank_ps", 4), sem("s6_bank_sb", 4, 1)
            out_ps, out_sb = sem("s6_out_ps", 2, 1), sem("s6_out_sb", 2, 1)
            U3, O3 = (t[:, :].rearrange("p (f n) -> p f n", f=MF) for t in (spec_u, spec_o))
            hx4 = hx[:, :].rearrange("p (g n h c) -> p g n h c", g=2, n=NH, h=2)
            FT = MF // 2

            def bank_step(i, u, g, half):
                return 8 * i + 4 * u + 2 * g + half

            with nc.Block() as block:
                @block.sync
                def _(sp):
                    sp.dma_start(vp, weights[:, vp_base:vp_base + vp_cols]).then_inc(vp_in, 16)

                @block.gpsimd
                def _(pool):
                    free_all(pool)

                @block.tensor
                def _(pe):
                    def step(i, u):
                        pe.wait_ge(*now(ready, i, u, 2))
                        for g in range(2):
                            for half in range(2):
                                r0 = 64 * half
                                for q in range(4):
                                    pe.wait_ge(bank_sb[q], bank_step(i, u, g, half) + 1)
                                    last = nc.tensor.matmul(ps[q][:, :], col[u][r0:r0 + 64, g * P:(g + 1) * P],
                                                            diag[u][r0:r0 + 64, 512 * q:512 * q + 512], start=True, stop=True)
                                    last.then_inc(bank_ps[q], 1)
                        for g in range(2):
                            for q in range(4):
                                pe.wait_ge(bank_sb[q], bank_step(i, u, g, 1) + 2)
                            pe.wait_ge(*prev(out_sb[g], i, u))
                            for n in range(NH):
                                m = g * NH + n
                                last = nc.tensor.matmul(ps[4 + g][:, 0:P], hx[:, m * P:(m + 1) * P], probs_bd[:, m * P:(m + 1) * P],
                                                        start=(n == 0), stop=(n == NH - 1))
                            last.then_inc(out_ps[g], 1)
                    with pe.Fori(0, FT) as i:
                        for u in range(2):
                            step(i, u)
                    step(FT, 0)

                def copy_banks(eng, op, qs, i, u, g):
                    for half in range(2):
                        for q in qs:
                            eng.wait_ge(bank_ps[q], bank_step(i, u, g, half) + 1)
                            if half == 0:
                                eng.wait_ge(*prev(out_ps[g], i, u))
                            op(hx4[:, g, 8 * q:8 * q + 8, half, :], ps[q][:, :].rearrange("p (n c) -> p n c", c=64)
                               ).then_inc(bank_sb[q], 1)

                @block.scalar
                def _(act):
                    act.wait_ge(coef_ready, 1)
                    with act.Fori(0, FT) as i:
                        for u in range(2):
                            for g in range(2):
                                copy_banks(act, nc.scalar.copy, (0, 2), i, u, g)
                    for g in range(2):
                        copy_banks(act, nc.scalar.copy, (0, 2), FT, 0, g)

                @block.vector
                def _(dve):
                    link = linker(dve, lk)
                    tt, ts = nc.vector.tensor_tensor, nc.vector.tensor_scalar
                    v3 = lambda t: t.rearrange("p (f n) -> p f n", n=NH)
                    bc = lambda name: SM(name).unsqueeze(1).broadcast_to([P, MF, NH])
                    dve.wait_ge(vp_in, 16)
                    link(tt(v3(h_r), v3(VP("v_r")), bc("Psw"), ALU.mult))
                    link(tt(v3(h_i), v3(VP("v_i")), bc("Psw"), ALU.mult))
                    for c, op in (("r", ALU.add), ("i", ALU.subtract)):
                        z = VP("v_" + c)[:, 0:NH]
                        link(tt(z, z, VP("vrev_" + c), op))
                        link(ts(z, z, 0.5, None, ALU.mult))
                    link(tt(v3(VP("v_r")), v3(VP("v_r")), bc("Vsw"), ALU.add))
                    for dst, a, b, op in ((h_r, "p_r", "v_r", ALU.add), (h_r, "p_i", "v_i", ALU.subtract),
                                          (h_i, "p_r", "v_i", ALU.add), (h_i, "p_i", "v_r", ALU.add)):
                        link(tt(tmp, VP(a), VP(b), ALU.mult))
                        link(tt(dst, dst, tmp, op))
                    c4 = coef[:, :].rearrange("p (m c) -> p m c", c=2)
                    for q in range(4):
                        r4 = slice(32 * q, 32 * q + 32)
                        if q % 2 == 0:
                            link(nc.vector.tensor_copy(c4[r4, :, 0], h_r[r4, :]))
                            link(nc.vector.tensor_copy(c4[r4, :, 1], h_i[r4, :]))
                        else:
                            link(ts(c4[r4, :, 0], h_i[r4, :], -1.0, None, ALU.mult))
                            link(nc.vector.tensor_copy(c4[r4, :, 1], h_r[r4, :]))
                    dve.sem_inc(coef_ready, 1)

                    def prepare(i, u):
                        dve.wait_ge(*prev2(step_done, i, u))
                        f = 2 * i + u
                        nc.vector.tensor_copy(col[u][:, :], spec_u[:, bass.ds(f * NIMG, NIMG)]).then_inc(ready[u], 1)
                        tt(diag[u][:, :].rearrange("p (m k) -> p m k", k=32),
                           coef[:, bass.ds(f * 2 * NH, 2 * NH)].unsqueeze(2).broadcast_to([P, 2 * NH, 32]),
                           K("mask").unsqueeze(1).broadcast_to([P, 2 * NH, 32]), ALU.mult).then_inc(ready[u], 1)

                    def take(i, u, g):
                        dve.wait_ge(*now(out_ps[g], i, u))
                        nc.vector.tensor_copy(spec_o[:, bass.ds((2 * i + u) * NIMG + g * P, P)], ps[4 + g][:, 0:P]
                                              ).then_inc(out_sb[g], 1)

                    def step(i, u, first=False, last=False):
                        copy_banks(dve, nc.vector.tensor_copy, (1, 3), i, u, 0)
                        if not first:
                            for g in range(2):
                                take(i - 1 + u, 1 - u, g)
                            dve.sem_inc(step_done[1 - u], 1)
                        if not last:
                            prepare(i + u, 1 - u)
                        copy_banks(dve, nc.vector.tensor_copy, (1, 3), i, u, 1)
                    prepare(0, 0)
                    step(0, 0, first=True)
                    step(0, 1)
                    with dve.Fori(1, FT) as i:
                        for u in range(2):
                            step(i, u)
                    step(FT, 0, last=True)
                    for g in range(2):
                        take(FT, 0, g)
        end_stage()

        with ExitStack() as st:
            def sb(name, cols):
                return st.enter_context(nc.sbuf_tensor(name, [P, cols], F32))
            PC = 2048
            g = [sb(f"s7_g{u}", PC) for u in range(2)]
            z = [sb(f"s7_z{u}", PC) for u in range(2)]
            g_in, mix_ps, stored = sem("s7_g_in", 2), sem("s7_mix_ps", 2, 1), sem("s7_stored", 2, 16)
            z_act, z_dve = sem("s7_z_act", 2, 1), sem("s7_z_dve", 2, 1)

            def pixels(t, i, u):
                return t.rearrange("b t y w -> (b t) (y w)")[u * P:(u + 1) * P, bass.ds(i * PC, PC)]
            with nc.Block() as block:
                @block.sync
                def _(sp):
                    with sp.Fori(0, PIX // PC) as i:
                        for u in range(2):
                            sp.wait_ge(*prev2(mix_ps, i, u))
                            sp.dma_start(g[u][:, :], pixels(g_d, i, u)).then_inc(g_in[u], 16)

                @block.gpsimd
                def _(pool):
                    free_all(pool)

                @block.tensor
                def _(pe):
                    with pe.Fori(0, PIX // PC) as i:
                        for u in range(2):
                            pe.wait_ge(*now(g_in, i, u, 16))
                            pe.wait_ge(*prev2(z_act, i, u))
                            pe.wait_ge(*prev2(z_dve, i, u))
                            for k in range(4):
                                last = nc.tensor.matmul(ps[4 * u + k][:, :], mix_t[:, u * P:(u + 1) * P],
                                                        g[u][:, k * 512:(k + 1) * 512], start=True, stop=True)
                            last.then_inc(mix_ps[u], 1)

                @block.scalar
                def _(act):
                    with act.Fori(0, PIX // PC) as i:
                        for u in range(2):
                            act.wait_ge(*now(mix_ps, i, u))
                            act.wait_ge(*prev2(stored, i, u, 16))
                            for k in (0, 2):
                                last = nc.scalar.activation(z[u][:, k * 512:(k + 1) * 512], ps[4 * u + k][:, :], ACT.Identity,
                                                            bias=mix_const[:, u:u + 1])
                            last.then_inc(z_act[u], 1)
                            act.wait_ge(*now(z_act, i, u))
                            act.wait_ge(*now(z_dve, i, u))
                            act.dma_start(pixels(z_d, i, u), z[u][:, :]).then_inc(stored[u], 16)
                    for u in range(2):
                        act.wait_ge(stored[u], done(stored, PIX // PC, 16))

                @block.vector
                def _(dve):
                    with dve.Fori(0, PIX // PC) as i:
                        for u in range(2):
                            dve.wait_ge(*now(mix_ps, i, u))
                            dve.wait_ge(*prev2(stored, i, u, 16))
                            for k in (1, 3):
                                last = nc.vector.tensor_scalar(z[u][:, k * 512:(k + 1) * 512], ps[4 * u + k][:, :],
                                                               mix_const[:, u:u + 1], None, ALU.add)
                            last.then_inc(z_dve[u], 1)
        end_stage()

        def inverse_pe(pe, i, u, spectrum, spec_ready, half, half_sb, inv_ps, out_ps, taken):
            for h in range(2):
                pe.wait_ge(*now(spec_ready[h], i, u))
                pe.wait_ge(*prev(taken[h], i, u))
                for k in range(4):
                    s = spectrum(4 * h + k)
                    nc.tensor.matmul(ps[6 + h][0:MF, k * N:(k + 1) * N], s, K("inv_re"), start=True, stop=True)
                    last = nc.tensor.matmul(ps[6 + h][64:64 + MF, k * N:(k + 1) * N], s, K("inv_im"), start=True, stop=True)
                last.then_inc(inv_ps[h], 1)
            for h in range(2):
                pe.wait_ge(*now(half_sb[h], i, u))
                for k in range(4):
                    last = nc.tensor.matmul(ps[6 + h][:, k * N:(k + 1) * N], half[h][0:64 + MF, k * N:(k + 1) * N],
                                            K("inv_w", 0, 64 + MF), start=True, stop=True)
                last.then_inc(out_ps[h], 1)

        def copy_half(act, i, u, h, half, inv_ps, half_sb, out_ps):
            act.wait_ge(*now(inv_ps[h], i, u))
            act.wait_ge(*prev(out_ps[h], i, u))
            nc.scalar.copy(half[h][0:MF, :], ps[6 + h][0:MF, :])
            nc.scalar.copy(half[h][64:64 + MF, :], ps[6 + h][64:64 + MF, :]).then_inc(half_sb[h], 1)

        with ExitStack() as st:
            def sb(name, cols):
                return st.enter_context(nc.sbuf_tensor(name, [P, cols], F32))
            z = [sb(f"s8_z{u}", CW) for u in range(2)]
            y = [sb(f"s8_y{u}", CW) for u in range(2)]
            sq = sb("s8_sq", CW)
            half = [sb(f"s8_half{h}", 512) for h in range(2)]
            chunk = sb("s8_chunk", MF * CH)
            ch3 = chunk[:, :].rearrange("p (f n) -> p f n", n=CH)
            z_in, stored, y_ready = sem("s8_z_in", 2), sem("s8_stored", 2, 16), sem("s8_y_ready", 2, 2)
            chunk_ready, zeroed = sem("s8_chunk_ready"), sem("s8_zeroed")
            inv_ps, half_sb, out_ps, taken = sem("s8_inv_ps", 2, 1), sem("s8_half_sb", 2), sem("s8_out_ps", 2, 1), sem("s8_taken", 2, 1)
            squared, reduced = sem("s8_squared"), sem("s8_reduced", None, 1)
            with nc.Block() as block:
                @block.sync
                def _(sp):
                    with sp.Fori(0, NT) as i:
                        for u in range(2):
                            sp.wait_ge(*prev2(y_ready, i, u, 2))
                            sp.dma_start(z[u][:, :], chunk_of(z_d, 2 * i + u)).then_inc(z_in[u], 16)

                @block.gpsimd
                def _(pool):
                    free_all(pool)
                    for h in range(2):
                        nc.gpsimd.memset(half[h][:, :], 0.0).then_inc(zeroed, 1)

                @block.tensor
                def _(pe):
                    with pe.Fori(0, NT) as i:
                        for u in range(2):
                            inverse_pe(pe, i, u, lambda n: ch3[:, :, n], [chunk_ready, chunk_ready], half, half_sb,
                                       inv_ps, out_ps, taken)

                @block.scalar
                def _(act):
                    act.wait_ge(zeroed, 2)
                    with act.Fori(0, NT) as i:
                        for u in range(2):
                            for h in range(2):
                                copy_half(act, i, u, h, half, inv_ps, half_sb, out_ps)
                            act.wait_ge(*now(y_ready, i, u, 2))
                            act.dma_start(chunk_of(y_d, 2 * i + u), y[u][:, :]).then_inc(stored[u], 16)
                            act.wait_ge(*prev(reduced, i, u))
                            nc.scalar.activation(sq[:, :], y[u][:, :], ACT.Square).then_inc(squared, 1)
                    for u in range(2):
                        act.wait_ge(stored[u], done(stored, NT, 16))

                @block.vector
                def _(dve):
                    with dve.Fori(0, NT) as i:
                        for u in range(2):
                            c = bass.ds(16 * i + 8 * u, CH)
                            for h in range(2):
                                dve.wait_ge(*prev(inv_ps[h], i, u))
                            nc.vector.tensor_copy(ch3, spec_o[:, :].rearrange("p (f n) -> p f n", f=MF)[:, :, c]).then_inc(chunk_ready, 1)
                            dve.wait_ge(*now(z_in, i, u, 16))
                            dve.wait_ge(*prev2(stored, i, u, 16))
                            for h in range(2):
                                dve.wait_ge(*now(out_ps[h], i, u))
                                w = slice(512 * h, 512 * h + 512)
                                nc.vector.tensor_tensor(y[u][:, w], ps[6 + h][:, :], z[u][:, w], ALU.add).then_inc(y_ready[u], 1)
                                dve.sem_inc(taken[h], 1)
                            dve.wait_ge(*now(y_ready, i, u, 2))
                            nc.vector.tensor_reduce(img_sum[:, c], y[u][:, :].rearrange("y (n w) -> y n w", n=CH), AX.X, ALU.add)
                            dve.wait_ge(*now(squared, i, u))
                            nc.vector.tensor_reduce(img_sumsq[:, c], sq[:, :].rearrange("y (n w) -> y n w", n=CH), AX.X,
                                                    ALU.add).then_inc(reduced, 1)
        end_stage()

        alpha, beta, a_scale, a_shift, conv_scale, conv_shift = (
            keep(n, NIMG) for n in ("alpha", "beta", "a_scale", "a_shift", "conv_scale", "conv_shift"))
        mean, var, root, tmp = (keep("img_" + n, NIMG) for n in ("mean", "var", "root", "tmp"))

        def image_stats(name):
            tot_ps, var_ready, root_ready, lk = (sem(f"{name}_{n}") for n in ("tot_ps", "var_ready", "root_ready", "link"))

            def pe_part():
                nc.tensor.matmul(ps[0][:, 0:NIMG], K("ones"), img_sum[:, :], start=True, stop=True)
                nc.tensor.matmul(ps[0][:, NIMG:2 * NIMG], K("ones"), img_sumsq[:, :], start=True, stop=True).then_inc(tot_ps, 1)

            def act_part(act, roots):
                for n in range(roots):
                    act.wait_ge(var_ready, n + 1)
                    nc.scalar.activation(root[:, :], (var if n == 0 else tmp2)[:, :], ACT.Sqrt).then_inc(root_ready, 1)

            def dve_part(dve, keep_var=None):
                link = linker(dve, lk)
                dve.wait_ge(tot_ps, 1)
                link(nc.vector.tensor_scalar(mean[:, :], ps[0][:, 0:NIMG], 1.0 / PIX, None, ALU.mult))
                link(nc.vector.tensor_scalar(var[:, :], ps[0][:, NIMG:2 * NIMG], 1.0 / PIX, None, ALU.mult))
                link(nc.vector.tensor_tensor(tmp[:, :], mean[:, :], mean[:, :], ALU.mult))
                link(nc.vector.tensor_tensor(var[:, :], var[:, :], tmp[:, :], ALU.subtract))
                inv_std(dve, link, var[:, :], root[:, :], tmp[:, :], var_ready, root_ready, 1)
                return link, var_ready, root_ready
            return pe_part, act_part, dve_part

        tmp2 = keep("img_tmp2", NIMG)

        def mixer_layer(layer, src, conv_out):
            name = f"s{9 + layer}"
            with ExitStack() as st:
                def sb(n, cols):
                    return st.enter_context(nc.sbuf_tensor(f"{name}_{n}", [P, cols], F32))

                def lsem(n, k=None, starts=0):
                    return sem(f"{name}_{n}", k, starts)
                yin = [sb(f"y{u}", CW) for u in range(2)]
                cin = [sb(f"c{u}", CW) for u in range(2)] if layer else None
                v = [sb(f"v{u}", CW) for u in range(2)]
                co = [sb(f"co{u}", CW) for u in range(2)]
                sq = sb("sq", CW)
                rf = sb("rowft", CH * 2 * N)[:, :].rearrange("w (n r) -> w n r", n=CH)
                half = [sb(f"half{h}", 512) for h in range(2)]
                spec = [sb(f"spec{h}", 4 * MF) for h in range(2)]
                pr = [sb(f"pr{h}", 4 * MF) for h in range(2)]
                prt = [sb(f"prt{h}", 4 * MF) for h in range(2)]
                y_in, mixed, v_ready = lsem("y_in", 2), lsem("mixed", 2, 1), lsem("v_ready")
                row_ps, col_ps = lsem("row_ps", 2), lsem("col_ps", 2, 1)
                row_sb = [lsem(f"row_sb{h}_", 2, 1) for h in range(2)]
                spec_done = lsem("spec_done", 2, 1)
                half_in = lsem("half_in") if layer else None
                prods = lsem("prods", 2, 2)
                spec_ready = lsem("spec_ready", 2)
                inv_ps, half_sb, out_ps, taken = lsem("inv_ps", 2, 1), lsem("half_sb", 2), lsem("out_ps", 2, 1), lsem("taken", 2, 1)
                squared, reduced, zeroed = lsem("squared"), lsem("reduced", None, 1), lsem("zeroed")
                stored = lsem("stored", 2, 16)
                m_stored = lsem("m_stored", 2, 16) if layer else None
                part = lsem("part", None) if layer else None
                params = lsem("params")
                pe_stats, act_stats, dve_stats = image_stats(name)
                MR, MI = SM(f"m{layer}_r"), SM(f"m{layer}_i")
                with nc.Block() as block:
                    @block.sync
                    def _(sp):
                        with sp.Fori(0, NT) as i:
                            for u in range(2):
                                sp.wait_ge(*prev2(mixed, i, u))
                                sp.dma_start(yin[u][:, :], chunk_of(y_d, 2 * i + u)).then_inc(y_in[u], 16)
                                if layer:
                                    sp.dma_start(cin[u][:, :], chunk_of(src, 2 * i + u)).then_inc(y_in[u], 16)

                    @block.gpsimd
                    def _(pool):
                        free_all(pool)
                        for h in range(2):
                            nc.gpsimd.memset(half[h][:, :], 0.0).then_inc(zeroed, 1)

                    @block.tensor
                    def _(pe):
                        pe_stats()
                        pe.wait_ge(params, 1)
                        with pe.Fori(0, NT) as i:
                            for u in range(2):
                                forward_pe(pe, i, u, v[u], v_ready, rf, row_ps, row_sb, col_ps, spec_done)
                                inverse_pe(pe, i, u, lambda n: spec[n // 4][:, (n % 4) * MF:(n % 4 + 1) * MF], spec_ready,
                                           half, half_sb, inv_ps, out_ps, taken)

                    @block.scalar
                    def _(act):
                        act_stats(act, 1 if layer else 2)
                        act.wait_ge(zeroed, 2)

                        def gelu(i, u):
                            act.wait_ge(part, 2 * i + u + 1)
                            act.wait_ge(*prev2(m_stored, i, u, 16))
                            nc.scalar.activation(v[u][:, :], v[u][:, :], ACT.Gelu).then_inc(v_ready, 1)
                            act.wait_ge(*now(v_ready, i, u))
                            act.dma_start(chunk_of(m_d, 2 * i + u), v[u][:, :]).then_inc(m_stored[u], 16)

                        def turn(i, last):
                            for u in range(2):
                                for h in range(2):
                                    copy_rows(act, nc.scalar.copy, 0, i, u, h, rf, row_ps, row_sb, col_ps)
                                if layer and not (last and u):
                                    gelu(i + u, 1 - u)
                                for h in range(2):
                                    copy_half(act, i, u, h, half, inv_ps, half_sb, out_ps)
                                act.wait_ge(*prev2(stored, i, u, 16))
                                for h in range(2):
                                    act.wait_ge(*now(out_ps[h], i, u))
                                    nc.scalar.copy(co[u][:, 512 * h:512 * h + 512], ps[6 + h][:, :]).then_inc(taken[h], 1)
                                for h in range(2):
                                    act.wait_ge(*now(taken[h], i, u))
                                act.dma_start(chunk_of(conv_out, 2 * i + u), co[u][:, :]).then_inc(stored[u], 16)
                                act.wait_ge(*prev(reduced, i, u))
                                nc.scalar.activation(sq[:, :], co[u][:, :], ACT.Square).then_inc(squared, 1)
                        if layer:
                            gelu(0, 0)
                        with act.Fori(0, NT - 1) as i:
                            turn(i, False)
                        turn(NT - 1, True)
                        for u in range(2):
                            act.wait_ge(stored[u], done(stored, NT, 16))
                            if layer:
                                act.wait_ge(m_stored[u], done(m_stored, NT, 16))

                    @block.vector
                    def _(dve):
                        tt, ts, stt = nc.vector.tensor_tensor, nc.vector.tensor_scalar, nc.vector.scalar_tensor_tensor
                        link, var_ready, root_ready = dve_stats(dve)
                        if layer == 0:
                            link(ts(a_scale[:, :], root[:, :], SM("attn_w"), None, ALU.mult))
                            link(tt(a_shift[:, :], mean[:, :], a_scale[:, :], ALU.mult))
                            link(ts(a_shift[:, :], a_shift[:, :], -1.0, SM("attn_b"), ALU.mult, ALU.add))
                            link(ts(var[:, :], var[:, :], -EPS, None, ALU.add))
                            link(tt(tmp2[:, :], a_scale[:, :], a_scale[:, :], ALU.mult))
                            link(tt(tmp2[:, :], tmp2[:, :], var[:, :], ALU.mult))
                            inv_std(dve, link, tmp2[:, :], root[:, :], tmp[:, :], var_ready, root_ready, 2)
                            link(tt(alpha[:, :], a_scale[:, :], root[:, :], ALU.mult))
                            link(ts(alpha[:, :], alpha[:, :], SM("norm2_w"), None, ALU.mult))
                            link(tt(beta[:, :], mean[:, :], alpha[:, :], ALU.mult))
                            link(ts(beta[:, :], beta[:, :], -1.0, SM("norm2_b"), ALU.mult, ALU.add))
                        else:
                            link(nc.vector.tensor_copy(conv_scale[:, :], root[:, :]))
                            link(tt(tmp[:, :], mean[:, :], root[:, :], ALU.mult))
                            link(ts(alpha[:, :], alpha[:, :], SM("m0sw"), None, ALU.mult))
                            link(ts(beta[:, :], beta[:, :], SM("m0sw"), None, ALU.mult))
                            link(tt(beta[:, :], beta[:, :], tmp[:, :], ALU.subtract))
                        dve.sem_inc(params, 1)

                        def layer_input(i, u):
                            dve.wait_ge(*now(y_in, i, u, 32 if layer else 16))
                            if layer:
                                dve.wait_ge(*prev2(m_stored, i, u, 16))
                            for n in range(CH):
                                c = bass.ds(16 * i + 8 * u + n, 1)
                                w = slice(n * N, (n + 1) * N)
                                last = ts(v[u][:, w], yin[u][:, w], alpha[:, c], beta[:, c], ALU.mult, ALU.add)
                            last.then_inc(mixed[u] if layer == 0 else half_in, 1)
                            if layer:
                                dve.wait_ge(*now(half_in, i, u))
                                for n in range(CH):
                                    c = bass.ds(16 * i + 8 * u + n, 1)
                                    w = slice(n * N, (n + 1) * N)
                                    last = stt(v[u][:, w], cin[u][:, w], conv_scale[:, c], v[u][:, w], ALU.mult, ALU.add)
                                last.then_inc(mixed[u], 1)
                            dve.wait_ge(*now(mixed, i, u))
                            dve.sem_inc(part if layer else v_ready, 1)

                        def turn(i, last):
                            for u in range(2):
                                for h in range(2):
                                    copy_rows(dve, nc.vector.tensor_copy, 1, i, u, h, rf, row_ps, row_sb, col_ps)
                                for h in range(2):
                                    dve.wait_ge(*now(col_ps[h], i, u))
                                    x = ps[4 + h][:, 0:8 * MF].rearrange("r (n a f) -> r a n f", n=4, a=2)
                                    o = lambda t: t[:, :].rearrange("r (n f) -> r n f", n=4)
                                    m = lambda w: w.unsqueeze(1).broadcast_to([P, 4, MF])
                                    tt(o(pr[h]), x[:, 0], m(MR), ALU.mult).then_inc(prods[h], 1)
                                    tt(o(prt[h]), x[:, 1], m(MI), ALU.mult).then_inc(prods[h], 1)
                                    dve.wait_ge(*now(prods[h], i, u, 2))
                                    dve.wait_ge(*prev(inv_ps[h], i, u))
                                    tt(spec[h][:, :], pr[h][:, :], prt[h][:, :], ALU.add).then_inc(spec_ready[h], 1)
                                    dve.sem_inc(spec_done[h], 1)
                                if not (last and u):
                                    layer_input(i + u, 1 - u)
                                for h in range(2):
                                    dve.wait_ge(*now(taken[h], i, u))
                                c = bass.ds(16 * i + 8 * u, CH)
                                nc.vector.tensor_reduce(img_sum[:, c], co[u][:, :].rearrange("y (n w) -> y n w", n=CH), AX.X, ALU.add)
                                dve.wait_ge(*now(squared, i, u))
                                nc.vector.tensor_reduce(img_sumsq[:, c], sq[:, :].rearrange("y (n w) -> y n w", n=CH), AX.X,
                                                        ALU.add).then_inc(reduced, 1)
                        layer_input(0, 0)
                        with dve.Fori(0, NT - 1) as i:
                            turn(i, False)
                        turn(NT - 1, True)

        mixer_layer(0, None, c0_d)
        end_stage()
        mixer_layer(1, c0_d, c1_d)
        end_stage()

        with ExitStack() as st:
            def sb(name, cols):
                return st.enter_context(nc.sbuf_tensor(name, [P, cols], F32))
            names = ("c", "m", "y", "x")
            tin = {n: [sb(f"s11_{n}{u}", CW) for u in range(2)] for n in names}
            m2 = [sb(f"s11_m2{u}", CW) for u in range(2)]
            res = [sb(f"s11_res{u}", CW) for u in range(2)]
            sq = sb("s11_sq", CW)
            cs = sb("s11_sums", 16)
            st_ = [sb(f"s11_{n}", CH) for n in ("mean", "var", "root", "tmp")]
            k1 = sb("s11_k1", NIMG)
            t_in, stored, finished = sem("s11_t_in", 2), sem("s11_stored", 2, 16), sem("s11_finished", 2, 1)
            m2_ready, squared, sums_ready, tot_ps, based = (sem("s11_" + n) for n in ("m2_ready", "squared", "sums_ready", "tot_ps", "based"))
            chain, var_ready, root_ready, lk = (sem("s11_" + n) for n in ("chain", "var_ready", "root_ready", "link"))
            free = sem("s11_free", None, 1)
            pe_stats, act_stats, dve_stats = image_stats("s11_conv")
            src = {"c": c1_d, "m": m_d, "y": y_d, "x": x1_d}
            with nc.Block() as block:
                @block.sync
                def _(sp):
                    with sp.Fori(0, NT) as i:
                        for u in range(2):
                            sp.wait_ge(*prev2(finished, i, u))
                            for n in names:
                                sp.dma_start(tin[n][u][:, :], chunk_of(src[n], 2 * i + u)).then_inc(t_in[u], 16)

                @block.gpsimd
                def _(pool):
                    free_all(pool)

                @block.tensor
                def _(pe):
                    pe_stats()
                    with pe.Fori(0, NT) as i:
                        for u in range(2):
                            pe.wait_ge(*now(sums_ready, i, u))
                            nc.tensor.matmul(ps[1][:, 0:16], K("ones"), cs[:, :], start=True, stop=True).then_inc(tot_ps, 1)

                @block.scalar
                def _(act):
                    act_stats(act, 1)
                    with act.Fori(0, NT) as i:
                        for u in range(2):
                            act.wait_ge(*now(m2_ready, i, u))
                            nc.scalar.activation(sq[:, :], m2[u][:, :], ACT.Square).then_inc(squared, 1)
                            act.wait_ge(*now(var_ready, i, u))
                            nc.scalar.activation(st_[2][:, :], st_[1][:, :], ACT.Sqrt).then_inc(root_ready, 1)
                            act.wait_ge(*now(finished, i, u))
                            act.dma_start(chunk_of(out, 2 * i + u), res[u][:, :]).then_inc(stored[u], 16)
                    for u in range(2):
                        act.wait_ge(stored[u], done(stored, NT, 16))

                @block.vector
                def _(dve):
                    tt, ts, stt = nc.vector.tensor_tensor, nc.vector.tensor_scalar, nc.vector.scalar_tensor_tensor
                    link0, _, _ = dve_stats(dve)
                    link0(nc.vector.tensor_copy(conv_scale[:, :], root[:, :]))
                    link0(tt(conv_shift[:, :], mean[:, :], root[:, :], ALU.mult))
                    link0(ts(conv_shift[:, :], conv_shift[:, :], -1.0, None, ALU.mult))
                    mn, vr, rt, tp = (t[:, :] for t in st_)

                    NL = 18
                    with dve.Fori(0, NT) as i:
                        for u in range(2):
                            count = [0]

                            def link(ins):
                                count[0] += 1
                                ins.then_inc(lk, 1)
                                dve.wait_ge(lk, 2 * NL * i + NL * u + count[0])
                            w = [slice(n * N, (n + 1) * N) for n in range(CH)]
                            c = [bass.ds(16 * i + 8 * u + n, 1) for n in range(CH)]
                            dve.wait_ge(*now(t_in, i, u, 64))
                            dve.wait_ge(*prev2(stored, i, u, 16))
                            for n in range(CH - 1):
                                ts(m2[u][:, w[n]], tin["m"][u][:, w[n]], SM("m1sw"), conv_shift[:, c[n]], ALU.mult, ALU.add)
                            n = CH - 1
                            link(ts(m2[u][:, w[n]], tin["m"][u][:, w[n]], SM("m1sw"), conv_shift[:, c[n]], ALU.mult, ALU.add))
                            for n in range(CH):
                                last = stt(m2[u][:, w[n]], tin["c"][u][:, w[n]], conv_scale[:, c[n]], m2[u][:, w[n]], ALU.mult, ALU.add)
                            last.then_inc(m2_ready, 1)
                            for n in range(CH):
                                last = ts(res[u][:, w[n]], tin["y"][u][:, w[n]], a_scale[:, c[n]], a_shift[:, c[n]], ALU.mult, ALU.add)
                            link(last)
                            link(tt(res[u][:, :], res[u][:, :], tin["x"][u][:, :], ALU.add))
                            dve.wait_ge(*now(m2_ready, i, u))
                            link(nc.vector.tensor_reduce(cs[:, 0:CH], m2[u][:, :].rearrange("y (n w) -> y n w", n=CH), AX.X, ALU.add))
                            dve.wait_ge(*now(squared, i, u))
                            link(nc.vector.tensor_reduce(cs[:, CH:16], sq[:, :].rearrange("y (n w) -> y n w", n=CH), AX.X, ALU.add))
                            dve.sem_inc(sums_ready, 1)
                            dve.wait_ge(*now(tot_ps, i, u))
                            link(ts(mn, ps[1][:, 0:CH], 1.0 / PIX, None, ALU.mult))
                            link(ts(vr, ps[1][:, CH:16], 1.0 / PIX, None, ALU.mult))
                            link(tt(tp, mn, mn, ALU.mult))
                            link(tt(vr, vr, tp, ALU.subtract))
                            ts(vr, vr, 0.0, EPS, ALU.max, ALU.add).then_inc(var_ready, 1)
                            dve.wait_ge(*now(root_ready, i, u))
                            link(nc.vector.reciprocal(rt, rt))
                            link(tt(tp, rt, rt, ALU.mult))
                            link(tt(tp, tp, vr, ALU.mult))
                            link(ts(tp, tp, -0.5, 1.5, ALU.mult, ALU.add))
                            link(tt(rt, rt, tp, ALU.mult))
                            link(ts(rt, rt, SM("mon_w"), None, ALU.mult))
                            link(tt(mn, mn, rt, ALU.mult))
                            link(ts(mn, mn, -1.0, SM("mon_b"), ALU.mult, ALU.add))
                            for n in range(CH):
                                last = ts(m2[u][:, w[n]], m2[u][:, w[n]], rt[:, n:n + 1], mn[:, n:n + 1], ALU.mult, ALU.add)
                            link(last)
                            tt(res[u][:, :], res[u][:, :], m2[u][:, :], ALU.add).then_inc(finished[u], 1)
                            assert count[0] == NL, count


def kernel(**inputs):
    import concourse.bacc as _bacc
    from concourse.bass_utils import run_bass_kernel_spmd as _run

    nc = _bacc.Bacc("TRN2", target_bir_lowering=False, num_devices=1)
    consts, cat = shape_constants()
    weights, wat = lay_weights(inputs)
    arrays = {
        "in_x": np.ascontiguousarray(inputs["x"]),
        "in_w_re": np.ascontiguousarray(inputs["L0_conv_weight_real"]),
        "in_w_im": np.ascontiguousarray(inputs["L0_conv_weight_imag"]),
        "in_consts": consts, "in_weights": weights,
    }
    ap = {k: nc.dram_tensor(k, a.shape, F32, kind="ExternalInput").ap() for k, a in arrays.items()}
    out = nc.dram_tensor("out_0", (B, T, N, N), F32, kind="ExternalOutput").ap()
    build(nc, ap["in_x"], ap["in_w_re"], ap["in_w_im"], ap["in_consts"], cat, ap["in_weights"], wat, out)
    r = _run(nc, [arrays], core_ids=[0])
    return r.results[0]["out_0"]
```

```python
from contextlib import ExitStack

import numpy as np
import concourse.bass as bass
from concourse import mybir

F32 = mybir.dt.float32
ALU = mybir.AluOpType
ACT = mybir.ActivationFunctionType
AX = mybir.AxisListType

B, T, N = 8, 32, 128
NH = 32
P = 128
NIMG = B * T
NF = N // 2 + 1
ND = 2 * NF
MF = 33
HM = 64
JT = 9
CH = 8
CW = CH * N
GRP = 4
PERGRP = float(T * N * GRP)
PIX = N * N
EPS = 1e-5
LOW = list(range(16)) + list(range(-16, 0))
HIGH = list(range(16, 32)) + list(range(-32, -16))
ROW_HF = np.array([(LOW, HIGH)[h][k] for h in range(2) for c in range(2) for k in range(32)])
ROW_C = np.array([c for h in range(2) for c in range(2) for k in range(32)])


def pack(parts):
    at, cols, where = 0, [], {}
    for name, a in parts:
        a = np.ascontiguousarray(a, dtype=np.float32).reshape(P, -1)
        where[name] = (at, a.shape[1])
        at += a.shape[1]
        cols.append(a)
    return np.concatenate(cols, axis=1), where


def shape_constants():
    y = np.arange(N)
    th = 2 * np.pi * np.outer(y, ROW_HF) / N
    c, s = np.cos(th), -np.sin(th)
    f1 = np.concatenate([np.where(ROW_C == 0, c, s), np.where(ROW_C == 0, -s, c)], 1) / N
    wf = np.arange(MF)
    tw = 2 * np.pi * np.outer(y, wf) / N
    fr, fi = np.cos(tw) / N, -np.sin(tw) / N
    tj = 2 * np.pi * np.outer(ROW_HF, y) / N
    cc = ROW_C[:, None] == 0
    inv_re = np.where(cc, np.cos(tj), -np.sin(tj))
    inv_im = np.where(cc, np.sin(tj), np.cos(tj))
    inv_w = np.zeros((P, N))
    m = np.where(wf == 0, 1.0, 2.0)[:, None]
    inv_w[0:MF] = m * np.cos(tw.T)
    inv_w[64:64 + MF] = -m * np.sin(tw.T)
    sym = np.zeros((P, P))
    for r in range(P):
        part = -ROW_HF[r] if ROW_HF[r] != -32 else -32
        r2 = int(np.nonzero((ROW_HF == part) & (ROW_C == ROW_C[r]))[0][0])
        sym[r, r] += 32.0
        sym[r, r2] += 32.0 if ROW_C[r] == 0 else -32.0
    herm, turn = np.zeros((P, P)), np.zeros((P, P))
    for r in range(P):
        if ROW_HF[r] == -32:
            herm[r, r] = 1.0
        else:
            r2 = int(np.nonzero((ROW_HF == -ROW_HF[r]) & (ROW_C == ROW_C[r]))[0][0])
            herm[r, r] += 0.5
            herm[r, r2] += 0.5 if ROW_C[r] == 0 else -0.5
        turn[r + 32 if ROW_C[r] == 0 else r - 32, r] = -1.0 if ROW_C[r] == 0 else 1.0
    herm_y = herm * np.where(ROW_HF == -32, 0.5, 1.0)[None, :]
    cov0 = np.where(ROW_HF == 0, 0.0, 1.0)[:, None] * np.ones((1, P))
    energy0 = cov0 * np.where(ROW_HF == -32, 0.5, 1.0)[:, None]
    wt = np.full((P, MF), 128.0)
    wt[:, 0] = 64.0
    wt[:64, :17] = 0.0
    wt[(ROW_HF == -32) & (ROW_C == 1), 0] = 0.0
    lw = np.full((P, JT), 128.0)
    lw[:64, 0] = 64.0
    hf = (np.arange(N) + 64) % N
    t0 = 2 * np.pi * np.outer(y, hf) / N
    g1 = np.concatenate([np.cos(t0), -np.sin(t0)], 1) / N
    wj = 64 - np.arange(NF)
    tj0 = 2 * np.pi * np.outer(y, wj) / N
    ar, ai = np.cos(tj0) / N, -np.sin(tj0) / N
    m0 = np.where((wj == 0) | (wj == 64), 1.0, 2.0)[:, None]
    k0 = np.concatenate([m0 * np.cos(tj0.T), (-m0 * np.sin(tj0.T))[1:64]], 0)
    grp = (np.arange(N)[:, None] // GRP == np.arange(N)[None, :] // GRP) / PERGRP
    return pack([
        ("f1", f1), ("ga", np.concatenate([fr, -fi], 1)), ("gb", np.concatenate([fi, fr], 1)),
        ("inv_re", inv_re), ("inv_im", inv_im), ("inv_w", inv_w), ("sym", sym), ("wt", wt), ("lw", lw),
        ("g1", g1), ("g2a", np.concatenate([ar, ai], 1)), ("g2b", np.concatenate([-ai, ar], 1)),
        ("cos0", np.cos(t0.T)), ("sin0", np.sin(t0.T)), ("k0", k0), ("grp", grp),
        ("ones", np.ones((P, P))), ("ident", np.eye(P)),
        ("herm", herm), ("herm_y", herm_y), ("turn", turn), ("cov0", cov0), ("energy0", energy0),
        ("twos", np.full((P, P), 2.0)), ("mask", np.tile(np.eye(32), (4, 1))),
    ])


def lay_weights(d):
    rows = np.array([[(LOW + HIGH).index(h) for h in (LOW, HIGH)[k]] for k in range(2) for c in range(2)]).reshape(-1)
    std = list(range(32)) + list(range(-32, 0))
    order = [std.index(h) for h in LOW + HIGH]

    def packed(w):
        w = w[0]
        full = np.concatenate([w, np.zeros_like(w[:, :, :1])], 2)
        even, odd = full[:, :, 0::2], full[:, :, 1::2]
        return np.concatenate([even, even, odd, odd], 1).transpose(1, 0, 2)

    def by_row(w):
        return w[:, rows, :].transpose(1, 2, 0)

    def mirrored(w):
        hs = LOW + HIGH
        out = np.zeros_like(w)
        for j, h in enumerate(hs):
            if -h in hs:
                out[:, j] = w[:, hs.index(-h)]
        return out

    groups = {"small": [], "qk": [], "vp": []}
    for c, name in ((0, "r"), (1, "i")):
        q, k = d["L1_conv_Qcw"][..., c], d["L1_conv_Kcw"][..., c]
        v = np.zeros((NH, HM, MF), np.float32)
        v[:, :32, :17] = d["L1_conv_Vcw"][0, ..., c]
        q0 = np.zeros((NH, HM), np.float32)
        q0[:, :32] = q[0, :, :, 0]
        groups["qk"] += [("q_" + name, packed(q)), ("k_" + name, packed(k)), ("qrev_" + name, mirrored(q0)[:, rows].T)]
        groups["vp"] += [("v_" + name, by_row(v)), ("vrev_" + name, mirrored(v[:, :, 0])[:, rows].T),
                         ("p_" + name, by_row(d["L1_conv_Pcw"][:, 0, ..., c][:, order]))]
        groups["small"] += [("m0_" + name, by_row(d["L1_conv_m0cw"][:, 0, ..., c][:, order])),
                            ("m1_" + name, by_row(d["L1_conv_m1cw"][:, 0, ..., c][:, order]))]
    for name in ("Qsw", "Ksw", "Vsw", "Psw"):
        groups["small"].append((name, np.broadcast_to(d["L1_conv_" + name].reshape(1, NH), (P, NH))))
    for name in ("norm1_w", "norm1_b", "attn_w", "attn_b", "norm2_w", "norm2_b", "m0sw", "m1sw", "mon_w", "mon_b"):
        groups["small"].append((name, np.broadcast_to(d["L1_conv_" + name].reshape(1, 1), (P, 1))))
    parts = groups["small"] + groups["qk"] + groups["vp"]
    return pack(parts)


START = {}


def begins(s):
    return START.get((s[0] if isinstance(s, list) else s).name, 0)


def at(s, u):
    return s[u] if isinstance(s, list) else s


def now(s, i, u, by=1):
    return at(s, u), (by * (i + 1) if isinstance(s, list) else by * (2 * i + u + 1)) + begins(s)


def prev(s, i, u, by=1):
    assert begins(s) > 0 or (u and not isinstance(s, list))
    return (s[1 - u], by * (i + u) + begins(s)) if isinstance(s, list) else (s, by * (2 * i + u) + begins(s))


def prev2(s, i, u, by=1):
    assert begins(s) > 0
    return s[u], by * i + begins(s)


def done(s, steps, by=1):
    return by * steps + begins(s)


def build(nc, x, w_re, w_im, consts, cat, weights, wat, out):
    x1_d = nc.dram_tensor("x1_d", (B, T, N, N), F32).ap()
    g_d = nc.dram_tensor("g_d", (B, T, N, N), F32).ap()
    z_d = nc.dram_tensor("z_d", (B, T, N, N), F32).ap()
    y_d = nc.dram_tensor("y_d", (B, T, N, N), F32).ap()
    u_d = nc.dram_tensor("u_d", (P, MF * NIMG), F32).ap()
    m_d = nc.dram_tensor("m_d", (B, T, N, N), F32).ap()
    xs_d = nc.dram_tensor("xs_d", (N, 2, T, B, NF), F32).ap()
    ds_d = nc.dram_tensor("ds_d", (N, T, B, ND), F32).ap()

    whole = ExitStack()
    pending, in_stage = [], []

    def sem(name, n=None, starts=0):
        if n is not None:
            return [sem(f"{name}{i}", None, starts) for i in range(n)]
        s = nc.alloc_semaphore(name)
        in_stage.append(s)
        if starts:
            START[s.name] = starts
            pending.append(s)
        return s

    def pool_dma_sem(name):
        return [nc.alloc_semaphore(f"{name}{u}") for u in range(2)]

    def free_all(eng):
        for s in pending:
            eng.sem_inc(s, START[s.name])
        pending.clear()

    def end_stage():
        with nc.Block() as block:
            @block.gpsimd
            def _(pool):
                for s in in_stage:
                    pool.sem_clear(s)
        for s in in_stage:
            nc.release_semaphore(s)
        in_stage.clear()

    def chunk_of(t, c):
        return t.rearrange("b t y w -> (b t) y w")[bass.ds(c * CH, CH), :, :].rearrange("n y w -> y n w")

    def channel_of(t, c):
        return t[:, bass.ds(c, 1), :, :].rearrange("b o y w -> y (b o) w")

    with whole:
        def keep(name, cols):
            return whole.enter_context(nc.sbuf_tensor(name, [P, cols], F32))

        cst = keep("cst", consts.shape[1])
        stats = keep("stats", 16)
        def K(name, lo=0, hi=P):
            a, n = cat[name]
            return cst[lo:hi, a:a + n]

        ps = [whole.enter_context(nc.psum_tensor(f"bank{i}", [P, 512], F32)) for i in range(8)]
        gn_scale = keep("gn_scale", B)
        gn_shift = keep("gn_shift", B)

        def linker(eng, link):
            count = [0]

            def run(ins):
                count[0] += 1
                ins.then_inc(link, 1)
                eng.wait_ge(link, count[0])
            return run

        def inv_std(dve, link, v, r, tmp, var_ready, root_ready, n):
            nc.vector.tensor_scalar(v, v, 0.0, EPS, ALU.max, ALU.add).then_inc(var_ready, 1)
            dve.wait_ge(root_ready, n)
            link(nc.vector.reciprocal(r, r))
            link(nc.vector.tensor_tensor(tmp, r, r, ALU.mult))
            link(nc.vector.tensor_tensor(tmp, tmp, v, ALU.mult))
            link(nc.vector.tensor_scalar(tmp, tmp, -0.5, 1.5, ALU.mult, ALU.add))
            link(nc.vector.tensor_tensor(r, r, tmp, ALU.mult))

        with ExitStack() as st:
            def sb(name, cols):
                return st.enter_context(nc.sbuf_tensor(name, [P, cols], F32))
            xin = [sb(f"s0_x{u}", CW) for u in range(2)]
            sq = [sb(f"s0_q{u}", CW) for u in range(2)]
            acc, acq = sb("s0_sum", CW), sb("s0_sumsq", CW)
            cols, grp, tmp = sb("s0_cols", 16), sb("s0_grp", 16), sb("s0_tmp", 8)
            const_in, zeroed = sem("const_in"), sem("s0_zeroed")
            x_in = sem("s0_x_in", 2)
            squared, summed, sqsummed = (sem("s0_" + n, 2, 1) for n in ("squared", "summed", "sqsummed"))
            lk, col_ps, col_sb, grp_ps, var_ready, root_ready = (
                sem("s0_" + n) for n in ("link", "col_ps", "col_sb", "grp_ps", "var_ready", "root_ready"))
            with nc.Block() as block:
                @block.sync
                def _(sp):
                    sp.dma_start(cst[:, :], consts).then_inc(const_in, 16)
                    with sp.Fori(0, T // 2) as i:
                        for u in range(2):
                            sp.wait_ge(*prev2(summed, i, u))
                            sp.wait_ge(*prev2(squared, i, u))
                            sp.dma_start(xin[u][:, :], channel_of(x, 2 * i + u)).then_inc(x_in[u], 16)

                @block.gpsimd
                def _(pool):
                    free_all(pool)

                @block.scalar
                def _(act):
                    with act.Fori(0, T // 2) as i:
                        for u in range(2):
                            act.wait_ge(x_in[u], 16 * i + 16)
                            act.wait_ge(*prev2(sqsummed, i, u))
                            nc.scalar.activation(sq[u][:, :], xin[u][:, :], ACT.Square).then_inc(squared[u], 1)
                    act.wait_ge(var_ready, 1)
                    nc.scalar.activation(gn_scale[:, :], grp[:, 8:16], ACT.Sqrt).then_inc(root_ready, 1)

                @block.vector
                def _(dve):
                    nc.vector.memset(acc[:, :], 0.0).then_inc(zeroed, 1)
                    nc.vector.memset(acq[:, :], 0.0).then_inc(zeroed, 1)
                    dve.wait_ge(zeroed, 2)
                    with dve.Fori(0, T // 2) as i:
                        for u in range(2):
                            dve.wait_ge(x_in[u], 16 * i + 16)
                            dve.wait_ge(*prev(summed, i, u))
                            nc.vector.tensor_tensor(acc[:, :], acc[:, :], xin[u][:, :], ALU.add).then_inc(summed[u], 1)
                            dve.wait_ge(*now(squared, i, u))
                            dve.wait_ge(*prev(sqsummed, i, u))
                            nc.vector.tensor_tensor(acq[:, :], acq[:, :], sq[u][:, :], ALU.add).then_inc(sqsummed[u], 1)
                    link = linker(dve, lk)
                    dve.wait_ge(col_ps, 1)
                    nc.vector.tensor_copy(cols[:, :], ps[0][:, 0:16]).then_inc(col_sb, 1)
                    dve.wait_ge(grp_ps, 1)
                    link(nc.vector.tensor_copy(grp[:, :], ps[1][:, 0:16]))
                    mean, var = grp[:, 0:8], grp[:, 8:16]
                    link(nc.vector.tensor_tensor(tmp[:, :], mean, mean, ALU.mult))
                    link(nc.vector.tensor_tensor(var, var, tmp[:, :], ALU.subtract))
                    inv_std(dve, link, var, gn_scale[:, :], tmp[:, :], var_ready, root_ready, 1)
                    link(nc.vector.tensor_tensor(gn_shift[:, :], mean, gn_scale[:, :], ALU.mult))
                    link(nc.vector.tensor_scalar_mul(gn_shift[:, :], gn_shift[:, :], -1.0))

                @block.tensor
                def _(pe):
                    pe.wait_ge(const_in, 16)
                    for u in range(2):
                        pe.wait_ge(summed[u], done(summed, T // 2))
                        pe.wait_ge(sqsummed[u], done(sqsummed, T // 2))
                    for b in range(B):
                        for h, a in ((0, acc), (8, acq)):
                            last = nc.tensor.matmul(ps[0][:, h + b:h + b + 1], a[:, b * N:(b + 1) * N],
                                                    K("ones")[:, 0:1], start=True, stop=True)
                    last.then_inc(col_ps, 1)
                    pe.wait_ge(col_sb, 1)
                    nc.tensor.matmul(ps[1][:, 0:16], K("grp"), cols[:, :], start=True, stop=True).then_inc(grp_ps, 1)

        end_stage()

        with ExitStack() as st:
            def sb(name, cols):
                return st.enter_context(nc.sbuf_tensor(name, [P, cols], F32))
            xin = [sb(f"s1_x{u}", CW) for u in range(2)]
            rowft = sb("s1_rowft", B * 2 * N)
            spec = [sb(f"s1_spec{u}", B * ND) for u in range(2)]
            rf = rowft[:, :].rearrange("w (b r) -> w b r", b=B)
            row_act, row_dve, row_ready, col_ps = (sem("s1_" + n, 2, st) for n, st in (("row_act", 1), ("row_dve", 1), ("row_ready", 0), ("col_ps", 1)))
            row_ps = [sem("s1_row_ps0"), sem("s1_row_ps1", 2, 1)]
            col_act, col_dve = ([sem(f"s1_{n}{h}", 2, 1) for h in range(2)] for n in ("col_act", "col_dve"))
            x_in, stored = sem("s1_x_in", 2), pool_dma_sem("s1_stored")
            res_free = sem("s1_res_free", 2, 1)
            with nc.Block() as block:
                @block.sync
                def _(sp):
                    with sp.Fori(0, T // 2) as i:
                        for u in range(2):
                            sp.wait_ge(*prev2(row_ps[1], i, u))
                            sp.dma_start(xin[u][:, :], channel_of(x, 2 * i + u)).then_inc(x_in[u], 16)

                @block.gpsimd
                def _(pool):
                    free_all(pool)
                    with pool.Fori(0, T // 2) as i:
                        for u in range(2):
                            for h in range(2):
                                pool.wait_ge(*now(col_act[h], i, u))
                                pool.wait_ge(*now(col_dve[h], i, u))
                            for c in range(2):
                                pool.dma_start(xs_d[:, c, bass.ds(2 * i + u, 1), :, :].rearrange("s t b j -> s (t b j)"),
                                               spec[u][:, c * B * NF:(c + 1) * B * NF]).then_inc(stored[u], 16)
                            pool.wait_ge(*now(stored, i, u, 32))
                            pool.sem_inc(res_free[u], 1)

                @block.tensor
                def _(pe):
                    with pe.Fori(0, T // 2) as i:
                        for u in range(2):
                            pe.wait_ge(*now(x_in, i, u, 16))
                            for h in range(2):
                                pe.wait_ge(*prev(row_act[h], i, u))
                                pe.wait_ge(*prev(row_dve[h], i, u))
                                for k in range(4):
                                    b = 4 * h + k
                                    last = nc.tensor.matmul(ps[2 * h + k // 2][:, (k % 2) * 256:(k % 2) * 256 + 256],
                                                            xin[u][:, b * N:(b + 1) * N], K("g1"), start=True, stop=True)
                                last.then_inc(at(row_ps[h], u), 1)
                            for h in range(2):
                                pe.wait_ge(*now(row_ready[h], i, u))
                                pe.wait_ge(*prev(col_act[h], i, u))
                                pe.wait_ge(*prev(col_dve[h], i, u))
                                for k in range(4):
                                    b = 4 * h + k
                                    o = ps[4 + 2 * h + k // 2][:, (k % 2) * ND:(k % 2) * ND + ND]
                                    nc.tensor.matmul(o, rf[:, b, 0:N], K("g2a"), start=True, stop=False)
                                    last = nc.tensor.matmul(o, rf[:, b, N:2 * N], K("g2b"), start=False, stop=True)
                                last.then_inc(col_ps[h], 1)

                def copy_spectrum(eng, op, k, i, u, h, done):
                    eng.wait_ge(*now(col_ps[h], i, u))
                    o = spec[u][:, :].rearrange("s (c b j) -> s b c j", c=2, b=B)[:, 4 * h + 2 * k:4 * h + 2 * k + 2, :, :]
                    v = ps[4 + 2 * h + k][:, 0:2 * ND].rearrange("s (b c j) -> s b c j", b=2, c=2)
                    op(o, v).then_inc(done[h][u], 1)

                @block.scalar
                def _(act):
                    with act.Fori(0, T // 2) as i:
                        for u in range(2):
                            for h in range(2):
                                act.wait_ge(*now(row_ps[h], i, u))
                                act.wait_ge(*prev(col_ps[h], i, u))
                                for k in range(2):
                                    b = 4 * h + k
                                    last = nc.scalar.activation(rf[:, b, :], ps[2 * h][:, k * 256:k * 256 + 256], ACT.Copy,
                                                                scale=gn_scale[:, b:b + 1])
                                last.then_inc(row_act[h], 1)
                            act.wait_ge(*prev2(res_free, i, u))
                            for h in range(2):
                                copy_spectrum(act, nc.scalar.copy, 0, i, u, h, col_act)

                @block.vector
                def _(dve):
                    with dve.Fori(0, T // 2) as i:
                        for u in range(2):
                            for h in range(2):
                                dve.wait_ge(*now(row_ps[h], i, u))
                                dve.wait_ge(*prev(col_ps[h], i, u))
                                for k in range(2):
                                    b = 4 * h + 2 + k
                                    last = nc.vector.tensor_scalar(rf[:, b, :], ps[2 * h + 1][:, k * 256:k * 256 + 256],
                                                                   gn_scale[:, b:b + 1], None, ALU.mult)
                                last.then_inc(row_dve[h], 1)
                                dve.wait_ge(*now(row_act[h], i, u))
                                dve.wait_ge(*now(row_dve[h], i, u))
                                dc = rf[:, 4 * h:4 * h + 4, 64:65]
                                nc.vector.tensor_tensor(dc, dc, gn_shift[:, 4 * h:4 * h + 4].rearrange("w (b o) -> w b o", o=1),
                                                        ALU.add).then_inc(row_ready[h], 1)
                            dve.wait_ge(*prev2(res_free, i, u))
                            for h in range(2):
                                copy_spectrum(dve, nc.vector.tensor_copy, 1, i, u, h, col_dve)
        end_stage()

        with ExitStack() as st:
            def sb(name, cols):
                return st.enter_context(nc.sbuf_tensor(name, [P, cols], F32))
            GJ = 13
            SLOTS = 4
            wt = [sb(f"s2_w{u}", T * 4 * NF) for u in range(2)]
            mov = [sb(f"s2_x{q}", 2 * 2 * B * NF) for q in range(SLOTS)]
            res = [sb(f"s2_d{u}", 2 * B * ND) for u in range(2)]
            wv = [w[:, :].rearrange("p (o q j) -> p q j o", q=4, j=NF) for w in wt]
            mv = [m[:, :].rearrange("p (f a n) -> p f a n", f=2, a=2) for m in mov]
            w_in, stored, x_in = sem("s2_w_in", 2), pool_dma_sem("s2_stored"), sem("s2_x_in", SLOTS)
            res_free = sem("s2_res_free", 2, 1)
            turned_re, turned_im = sem("s2_turned_re", SLOTS), sem("s2_turned_im", SLOTS)
            used = [sem(f"s2_used{q}", None, 1) for q in range(SLOTS - 1)] + [sem("s2_used3", 2, 1)]
            group_ps, copied = sem("s2_group_ps", 4), sem("s2_copied", 5, 1)
            cleared = sem("s2_cleared")
            NC = N // 8
            with nc.Block() as block:
                @block.sync
                def _(sp):
                    sp.wait_ge(cleared, SLOTS)
                    with sp.Fori(0, NC // 2) as i:
                        for u in range(2):
                            s0 = 16 * i + 8 * u
                            sp.wait_ge(*prev2(used[3], i, u))
                            for f in range(2):
                                for c, w in ((0, w_re), (1, w_im)):
                                    p0 = 64 * f + 32 * c
                                    sp.dma_start(wt[u][p0:p0 + 32, :].rearrange("i (o n) -> i o n", o=T),
                                                 w[:, :, bass.ds(s0 + 4 * f, 4), :].rearrange("i o s j -> i o (s j)")
                                                 ).then_inc(w_in[u], 16)
                            for q in range(4):
                                sp.wait_ge(*prev(used[q], i, u))
                                for f in range(2):
                                    sp.dma_start(mv[q][64 * f:64 * f + 64, f, 0, :],
                                                 xs_d[bass.ds(s0 + 4 * f + q, 1), :, :, :, :].rearrange("s c t b j -> (s c t) (b j)")
                                                 ).then_inc(x_in[q], 16)

                @block.gpsimd
                def _(pool):
                    free_all(pool)
                    for q in range(SLOTS):
                        nc.gpsimd.memset(mov[q][:, :], 0.0).then_inc(cleared, 1)
                    with pool.Fori(0, NC // 2) as i:
                        for u in range(2):
                            for g in range(5):
                                pool.wait_ge(*now(copied[g], i, u))
                            for f in range(2):
                                pool.dma_start(ds_d[bass.ds(16 * i + 8 * u + 4 * f, 4), :, :, :].rearrange("s o b n -> (s o) (b n)"),
                                               res[u][:, f * B * ND:(f + 1) * B * ND]).then_inc(stored[u], 16)
                            pool.wait_ge(*now(stored, i, u, 32))
                            pool.sem_inc(res_free[u], 1)

                @block.tensor
                def _(pe):
                    with pe.Fori(0, NC // 2) as i:
                        for u in range(2):
                            pe.wait_ge(*now(w_in, i, u, 64))
                            for q in range(4):
                                pe.wait_ge(x_in[q], 64 * i + 32 * (u + 1))
                                pe.wait_ge(turned_re[q], 4 * i + 2 * u + 2)
                                pe.wait_ge(turned_im[q], 4 * i + 2 * u + 2)
                                for g in range(5):
                                    if q == 0:
                                        pe.wait_ge(*prev(copied[g], i, u))
                                    for jj in range(GJ):
                                        j = g * GJ + jj
                                        last = nc.tensor.matmul(
                                            ps[g][32 * q:32 * q + 32, 32 * jj:32 * jj + 32], wv[u][:, q, j, :],
                                            mov[q][:, :].rearrange("p (n j) -> p j n", j=NF)[:, j, :], start=True, stop=True)
                                    if q == 3 and g < 4:
                                        last.then_inc(group_ps[g], 1)
                                last.then_inc(at(used[q], u), 1)

                def turn(eng, op, c, done, i, u):
                    sign = 1.0 if c == 0 else -1.0
                    for q in range(4):
                        eng.wait_ge(x_in[q], 64 * i + 32 * (u + 1))
                        for f in range(2):
                            p0, p1 = 64 * f + 32 * c, 64 * f + 32 * (1 - c)
                            op(mv[q][p0:p0 + 32, f, 1, :], mv[q][p1:p1 + 32, f, 0, :], sign).then_inc(done[q], 1)

                def copy_out(eng, op, mine, i, u):
                    eng.wait_ge(*prev2(res_free, i, u))
                    for g in mine:
                        if g < 4:
                            eng.wait_ge(*now(group_ps[g], i, u))
                        else:
                            eng.wait_ge(*now(used[3], i, u))
                        v = ps[g][:, 0:32 * GJ].rearrange("p (j f a b) -> p f a b j", f=2, a=2, b=B)
                        d = res[u][:, :].rearrange("p (f b n) -> p f b n", f=2, b=B)
                        both = res[u][:, :].rearrange("p (f b n) -> p f b n", f=2, b=B)[:, :, :, 1:129]                             .rearrange("p f b (a j) -> p f a b j", a=2)
                        lo, hi = g * GJ, min((g + 1) * GJ, NF - 1)
                        for f in range(2):
                            if g == 0:
                                op(d[:, f, :, 1:2], v[:, f, 0, :, 0:1])
                                op(d[:, f, :, 0:1], v[:, f, 1, :, 0:1])
                                lo = 1
                            if g == 4:
                                op(d[:, f, :, 65:66], v[:, f, 0, :, GJ - 1:GJ])
                                op(d[:, f, :, 129:130], v[:, f, 1, :, GJ - 1:GJ])
                            last = op(both[:, f, :, :, lo:hi], v[:, f, :, :, lo - g * GJ:hi - g * GJ])
                        last.then_inc(copied[g], 1)

                @block.scalar
                def _(act):
                    with act.Fori(0, NC // 2) as i:
                        for u in range(2):
                            turn(act, nc.scalar.mul, 0, turned_re, i, u)
                            copy_out(act, nc.scalar.copy, (0, 2), i, u)

                @block.vector
                def _(dve):
                    with dve.Fori(0, NC // 2) as i:
                        for u in range(2):
                            turn(dve, nc.vector.tensor_scalar_mul, 1, turned_im, i, u)
                            copy_out(dve, nc.vector.tensor_copy, (1, 3, 4), i, u)
        end_stage()

        with ExitStack() as st:
            def sb(name, cols):
                return st.enter_context(nc.sbuf_tensor(name, [P, cols], F32))
            gn2_scale, gn2_shift = keep("gn2_scale", B * 32), keep("gn2_shift", B * 32)
            xin = [sb(f"s3_x{u}", CW) for u in range(2)]
            sp_in = [sb(f"s3_d{u}", B * ND) for u in range(2)]
            sp_neg = [sb(f"s3_n{u}", B * N) for u in range(2)]
            half = [sb(f"s3_h{h}", 4 * N) for h in range(2)]
            x1 = [sb(f"s3_x1_{u}", CW) for u in range(2)]
            sq = sb("s3_sq", CW)
            acc, acq = sb("s3_sum", CW), sb("s3_sumsq", CW)
            grp, tmp = sb("s3_grp", 512), sb("s3_tmp", 256)
            x_in, d_in, negated, stored = sem("s3_x_in", 2), sem("s3_d_in", 2), sem("s3_negated", 2), pool_dma_sem("s3_stored")
            res_free = sem("s3_res_free", 2, 1)
            col_ps = [sem("s3_col_ps0"), sem("s3_col_ps1", 2, 1)]
            col_sb, row_ps = sem("s3_col_sb", 2, 1), sem("s3_row_ps", 2, 1)
            added = [sem("s3_added0", 2, 1), sem("s3_added1", 2, 1)]
            squared, summed, sqsummed = (sem("s3_" + n, None, 1) for n in ("squared", "summed", "sqsummed"))
            zeroed, tot_ps, lk, var_ready, root_ready = (sem("s3_" + n) for n in ("zeroed", "tot_ps", "link", "var_ready", "root_ready"))
            with nc.Block() as block:
                @block.sync
                def _(sp):
                    with sp.Fori(0, T // 2) as i:
                        for u in range(2):
                            sp.wait_ge(*prev2(col_ps[1], i, u))
                            sp.dma_start(sp_in[u][:, :], ds_d[:, bass.ds(2 * i + u, 1), :, :].rearrange("s o b n -> s (o b n)")
                                         ).then_inc(d_in[u], 16)
                            sp.wait_ge(*prev2(added[1], i, u))
                            sp.dma_start(xin[u][:, :], channel_of(x, 2 * i + u)).then_inc(x_in[u], 16)

                @block.gpsimd
                def _(pool):
                    free_all(pool)
                    with pool.Fori(0, T // 2) as i:
                        for u in range(2):
                            for h in range(2):
                                pool.wait_ge(*now(added[h], i, u))
                            pool.dma_start(channel_of(x1_d, 2 * i + u), x1[u][:, :]).then_inc(stored[u], 16)
                            pool.wait_ge(*now(stored, i, u, 16))
                            pool.sem_inc(res_free[u], 1)

                @block.tensor
                def _(pe):
                    with pe.Fori(0, T // 2) as i:
                        for u in range(2):
                            pe.wait_ge(*now(d_in, i, u, 16))
                            pe.wait_ge(*now(negated, i, u, 3))
                            d = sp_in[u][:, :].rearrange("s (b n) -> s b n", b=B)
                            n = sp_neg[u][:, :].rearrange("s (b n) -> s b n", b=B)
                            for h in range(2):
                                pe.wait_ge(*prev(col_sb[h], i, u))
                                for k in range(4):
                                    o = ps[h][:, k * N:(k + 1) * N]
                                    nc.tensor.matmul(o, d[:, 4 * h + k, 1:129], K("cos0"), start=True, stop=False)
                                    last = nc.tensor.matmul(o, n[:, 4 * h + k, :], K("sin0"), start=False, stop=True)
                                last.then_inc(at(col_ps[h], u), 1)
                            for h in range(2):
                                pe.wait_ge(*now(col_sb[h], i, u))
                                pe.wait_ge(*prev(added[h], i, u))
                                for k in range(4):
                                    last = nc.tensor.matmul(ps[2 + h][:, k * N:(k + 1) * N], half[h][:, k * N:(k + 1) * N],
                                                            K("k0"), start=True, stop=True)
                                last.then_inc(row_ps[h], 1)
                    pe.wait_ge(summed, done(summed, T))
                    pe.wait_ge(sqsummed, done(sqsummed, T))
                    for k in range(2):
                        nc.tensor.matmul(ps[4 + k][:, :], K("ones"), acc[:, k * 512:(k + 1) * 512], start=True, stop=True)
                        last = nc.tensor.matmul(ps[6 + k][:, :], K("ones"), acq[:, k * 512:(k + 1) * 512], start=True, stop=True)
                    last.then_inc(tot_ps, 1)

                @block.scalar
                def _(act):
                    with act.Fori(0, T // 2) as i:
                        for u in range(2):
                            for h in range(2):
                                act.wait_ge(*now(col_ps[h], i, u))
                                act.wait_ge(*prev(row_ps[h], i, u))
                                nc.scalar.copy(half[h][:, :], ps[h][:, :]).then_inc(col_sb[h], 1)
                            for h in range(2):
                                act.wait_ge(*now(added[h], i, u))
                            act.wait_ge(*prev(sqsummed, i, u))
                            nc.scalar.activation(sq[:, :], x1[u][:, :], ACT.Square).then_inc(squared, 1)
                    act.wait_ge(var_ready, 1)
                    nc.scalar.activation(gn2_scale[:, :], grp[:, 256:512], ACT.Sqrt).then_inc(root_ready, 1)

                @block.vector
                def _(dve):
                    nc.vector.memset(acc[:, :], 0.0).then_inc(zeroed, 1)
                    nc.vector.memset(acq[:, :], 0.0).then_inc(zeroed, 1)
                    dve.wait_ge(zeroed, 2)
                    with dve.Fori(0, T // 2) as i:
                        for u in range(2):
                            dve.wait_ge(*now(d_in, i, u, 16))
                            dve.wait_ge(*prev2(col_ps[1], i, u))
                            d = sp_in[u][:, :].rearrange("s (b n) -> s b n", b=B)
                            n = sp_neg[u][:, :].rearrange("s (b n) -> s b n", b=B)
                            nc.vector.tensor_scalar_mul(n[:, :, 0:1], d[:, :, 0:1], -1.0).then_inc(negated[u], 1)
                            nc.vector.tensor_scalar_mul(n[:, :, 1:65], d[:, :, 66:130], -1.0).then_inc(negated[u], 1)
                            nc.vector.tensor_copy(n[:, :, 65:128], d[:, :, 2:65]).then_inc(negated[u], 1)
                            dve.wait_ge(*now(x_in, i, u, 16))
                            dve.wait_ge(*prev2(res_free, i, u))
                            for h in range(2):
                                dve.wait_ge(*now(row_ps[h], i, u))
                                nc.vector.tensor_tensor(x1[u][:, 512 * h:512 * h + 512], ps[2 + h][:, :],
                                                        xin[u][:, 512 * h:512 * h + 512], ALU.add).then_inc(added[h][u], 1)
                            for h in range(2):
                                dve.wait_ge(*now(added[h], i, u))
                            dve.wait_ge(*prev(summed, i, u))
                            nc.vector.tensor_tensor(acc[:, :], acc[:, :], x1[u][:, :], ALU.add).then_inc(summed, 1)
                            dve.wait_ge(*now(squared, i, u))
                            dve.wait_ge(*prev(sqsummed, i, u))
                            nc.vector.tensor_tensor(acq[:, :], acq[:, :], sq[:, :], ALU.add).then_inc(sqsummed, 1)
                    link = linker(dve, lk)
                    dve.wait_ge(tot_ps, 1)
                    for k in range(2):
                        for q, c0 in ((4, 0), (6, 256)):
                            link(nc.vector.tensor_reduce(grp[:, c0 + 128 * k:c0 + 128 * k + 128],
                                                         ps[q + k][:, :].rearrange("p (g j) -> p g j", j=GRP), AX.X, ALU.add))
                    link(nc.vector.tensor_scalar_mul(grp[:, :], grp[:, :], 1.0 / PERGRP))
                    mean, var = grp[:, 0:256], grp[:, 256:512]
                    link(nc.vector.tensor_tensor(tmp[:, :], mean, mean, ALU.mult))
                    link(nc.vector.tensor_tensor(var, var, tmp[:, :], ALU.subtract))
                    inv_std(dve, link, var, gn2_scale[:, :], tmp[:, :], var_ready, root_ready, 1)
                    link(nc.vector.tensor_tensor(gn2_shift[:, :], mean, gn2_scale[:, :], ALU.mult))
                    link(nc.vector.tensor_scalar_mul(gn2_shift[:, :], gn2_shift[:, :], -1.0))
        end_stage()

        spec_u = keep("spec_u", MF * NIMG)
        spec_o = keep("spec_o", MF * NIMG)
        probs_bd = keep("probs_bd", 2 * NH * P)
        img_sum, img_sumsq = keep("img_sum", NIMG), keep("img_sumsq", NIMG)
        small = keep("small", wat["q_r"][0])
        def W(name, tile, base):
            a, n = wat[name]
            return tile[:, a - base:a - base + n]

        def SM(name):
            return W(name, small, 0)
        mix_t, mix_const = keep("mix_t", 2 * P), keep("mix_const", 2)
        turned = ExitStack()
        spec_v = turned.enter_context(nc.sbuf_tensor("spec_v", [P, MF * NIMG], F32))
        NT = NIMG // CH // 2

        def images(tile):
            return tile[:, :].rearrange("p (f n) -> p n f", n=NIMG)

        def forward_pe(pe, i, u, tile, ready, rf, row_ps, row_sb, col_ps, col_free):
            pe.wait_ge(*now(ready, i, u))
            for h in range(2):
                for free in row_sb[h]:
                    pe.wait_ge(*prev(free, i, u))
                for k in range(4):
                    last = nc.tensor.matmul(ps[2 * h + k // 2][:, (k % 2) * 256:(k % 2) * 256 + 256],
                                            tile[:, (4 * h + k) * N:(4 * h + k + 1) * N], K("f1"), start=True, stop=True)
                last.then_inc(row_ps[h], 1)
            for h in range(2):
                for here in row_sb[h]:
                    pe.wait_ge(*now(here, i, u))
                pe.wait_ge(*prev(col_free[h], i, u))
                for k in range(4):
                    o = ps[4 + h][:, k * 2 * MF:(k + 1) * 2 * MF]
                    nc.tensor.matmul(o, rf[:, 4 * h + k, 0:N], K("ga"), start=True, stop=False)
                    last = nc.tensor.matmul(o, rf[:, 4 * h + k, N:2 * N], K("gb"), start=False, stop=True)
                last.then_inc(col_ps[h], 1)

        def copy_rows(eng, op, k, i, u, h, rf, row_ps, row_sb, col_ps):
            eng.wait_ge(*now(row_ps[h], i, u))
            eng.wait_ge(*prev(col_ps[h], i, u))
            op(rf[:, 4 * h + 2 * k:4 * h + 2 * k + 2, :], ps[2 * h + k][:, :].rearrange("w (n r) -> w n r", n=2)
               ).then_inc(row_sb[h][k], 1)

        with ExitStack() as st:
            def sb(name, cols):
                return st.enter_context(nc.sbuf_tensor(name, [P, cols], F32))
            xin = [sb(f"s4_x{u}", CW) for u in range(2)]
            g = [sb(f"s4_g{u}", CW) for u in range(2)]
            sq = sb("s4_sq", CW)
            shift = [sb(f"s4_shift{u}", 32) for u in range(2)]
            rf = sb("s4_rowft", CH * 2 * N)[:, :].rearrange("w (n r) -> w n r", n=CH)
            x_in, scaled, stored = sem("s4_x_in", 2), sem("s4_scaled", 2, 2), sem("s4_stored", 2, 16)
            g_ready, squared, reduced = sem("s4_g_ready"), sem("s4_squared"), sem("s4_reduced", None, 1)
            row_ps, col_ps = sem("s4_row_ps", 2), sem("s4_col_ps", 2, 1)
            row_sb = [sem(f"s4_row_sb{h}_", 2, 1) for h in range(2)]
            col_sb = sem("s4_col_sb", 2, 1)
            small_in = sem("s4_small_in")

            with nc.Block() as block:
                @block.sync
                def _(sp):
                    sp.dma_start(small[:, :], weights[:, 0:wat["q_r"][0]]).then_inc(small_in, 16)
                    with sp.Fori(0, NT) as i:
                        for u in range(2):
                            sp.wait_ge(*prev2(scaled, i, u, 2))
                            sp.dma_start(xin[u][:, :], chunk_of(x1_d, 2 * i + u)).then_inc(x_in[u], 16)
                    sp.wait_ge(small_in, 16)

                @block.gpsimd
                def _(pool):
                    free_all(pool)
                    with pool.Fori(0, NT) as i:
                        for u in range(2):
                            pool.wait_ge(*now(scaled, i, u, 2))
                            gv = g[u][:, :].rearrange("y (n g j) -> y n g j", n=CH, j=GRP)
                            sh = shift[u][:, :].unsqueeze(1).unsqueeze(3).broadcast_to([P, CH, 32, GRP])
                            nc.gpsimd.tensor_tensor(gv, gv, sh, ALU.add).then_inc(g_ready, 1)

                @block.tensor
                def _(pe):
                    with pe.Fori(0, NT) as i:
                        for u in range(2):
                            forward_pe(pe, i, u, g[u], g_ready, rf, row_ps, row_sb, col_ps, col_sb)

                def copy_cols(eng, op, i, u, h):
                    eng.wait_ge(*now(col_ps[h], i, u))
                    v = ps[4 + h][:, 0:8 * MF].rearrange("r (n a f) -> r a n f", n=4, a=2)
                    op(images(spec_u)[:, bass.ds(16 * i + 8 * u + 4 * h, 4), :], v[:, 0])
                    op(images(spec_v)[:, bass.ds(16 * i + 8 * u + 4 * h, 4), :], v[:, 1]).then_inc(col_sb[h], 1)

                @block.scalar
                def _(act):
                    with act.Fori(0, NT) as i:
                        for u in range(2):
                            act.wait_ge(*now(g_ready, i, u))
                            act.dma_start(chunk_of(g_d, 2 * i + u), g[u][:, :]).then_inc(stored[u], 16)
                            for h in range(2):
                                copy_rows(act, nc.scalar.copy, 0, i, u, h, rf, row_ps, row_sb, col_ps)
                            act.wait_ge(*prev(reduced, i, u))
                            nc.scalar.activation(sq[:, :], g[u][:, :], ACT.Square).then_inc(squared, 1)
                            copy_cols(act, nc.scalar.copy, i, u, 0)
                    for u in range(2):
                        act.wait_ge(stored[u], done(stored, NT, 16))

                @block.vector
                def _(dve):
                    def scale(i, u):
                        dve.wait_ge(*now(x_in, i, u, 16))
                        dve.wait_ge(*prev2(stored, i, u, 16))
                        nc.vector.tensor_copy(shift[u][:, :], gn2_shift[:, bass.ds((i // 2) * 32, 32)]).then_inc(scaled[u], 1)
                        v = xin[u][:, :].rearrange("y (n g j) -> y n g j", n=CH, j=GRP)
                        sc = gn2_scale[:, bass.ds((i // 2) * 32, 32)].unsqueeze(1).unsqueeze(3).broadcast_to([P, CH, 32, GRP])
                        nc.vector.tensor_tensor(g[u][:, :].rearrange("y (n g j) -> y n g j", n=CH, j=GRP), v, sc,
                                                ALU.mult).then_inc(scaled[u], 1)

                    def turn(i, last):
                        for u in range(2):
                            copy_rows(dve, nc.vector.tensor_copy, 1, i, u, 0, rf, row_ps, row_sb, col_ps)
                            copy_rows(dve, nc.vector.tensor_copy, 1, i, u, 1, rf, row_ps, row_sb, col_ps)
                            dve.wait_ge(*now(g_ready, i, u))
                            c = bass.ds(16 * i + 8 * u, CH)
                            nc.vector.tensor_reduce(img_sum[:, c], g[u][:, :].rearrange("y (n w) -> y n w", n=CH), AX.X, ALU.add)
                            dve.wait_ge(*now(squared, i, u))
                            nc.vector.tensor_reduce(img_sumsq[:, c], sq[:, :].rearrange("y (n w) -> y n w", n=CH), AX.X,
                                                    ALU.add).then_inc(reduced, 1)
                            if not (last and u):
                                scale(i + u, 1 - u)
                            copy_cols(dve, nc.vector.tensor_copy, i, u, 1)
                    scale(0, 0)
                    with dve.Fori(0, NT - 1) as i:
                        turn(i, False)
                    turn(NT - 1, True)
        end_stage()

        with ExitStack() as st:
            def sb(name, cols):
                return st.enter_context(nc.sbuf_tensor(name, [P, cols], F32))
            qk_base, qk_end = wat["q_r"][0], wat["v_r"][0]
            qk = sb("s5_qk", qk_end - qk_base)
            def QK(name):
                return W(name, qk, qk_base)
            NJ = NH * JT
            sym_r, sym_i, g_r, g_i, tmp = (sb("s5_" + n, NJ) for n in ("sym_r", "sym_i", "g_r", "g_i", "tmp"))
            mean, ex2, r, r_tmp = (sb("s5_" + n, NIMG + 2) for n in ("mean", "ex2", "r", "r_tmp"))
            low_u, low_v = sb("s5_low_u", JT * NIMG), sb("s5_low_v", JT * NIMG)
            JI = JT * NIMG
            part = [probs_bd[:, 0:JI], sb("s5_part1", JI)[:, :]]
            prod = [probs_bd[:, JI:2 * JI], probs_bd[:, 2 * JI:3 * JI]]
            scores = sb("s5_scores", 2 * NH * 32)
            common = sb("s5_common", 64)
            red = sb("s5_red", 64)
            vecn = sb("s5_vecn", NH)
            vec = sb("s5_vec", 8)
            qk_in, stat_ps, var_ready, root_ready, lk, lkp, v_done, u_done = (
                sem("s5_" + n) for n in ("qk_in", "stat_ps", "var_ready", "root_ready", "link", "linkp", "v_done", "u_done"))
            packed, sym_ps, weighted, common_ps, part_ready, root2 = (
                sem("s5_" + n) for n in ("packed", "sym_ps", "weighted", "common_ps", "part_ready", "root2"))
            prod_ready, score_ps, taken = sem("s5_prod_ready", 2, 1), sem("s5_score_ps", 2, 1), sem("s5_taken", 2, 1)
            shifted, exped, mix_ready, mix_ps, g_done = (sem("s5_" + n) for n in ("shifted", "exped", "mix_ready", "mix_ps", "g_done"))
            u_saved = sem("s5_u_saved")
            TU = NH // 2
            U3, V3, O3 = (t[:, :].rearrange("p (f n) -> p f n", f=MF) for t in (spec_u, spec_v, spec_o))
            LU3, LV3 = (t[:, :].rearrange("p (f n) -> p f n", f=JT) for t in (low_u, low_v))
            with nc.Block() as block:
                @block.sync
                def _(sp):
                    sp.dma_start(u_d, spec_u[:, :]).then_inc(u_saved, 16)
                    sp.dma_start(qk[:, :], weights[:, qk_base:qk_end]).then_inc(qk_in, 16)

                @block.tensor
                def _(pe):
                    nc.tensor.matmul(ps[0][:, 0:NIMG], K("ones"), img_sum[:, :], start=True, stop=True)
                    nc.tensor.matmul(ps[0][:, NIMG:2 * NIMG], K("ones"), img_sumsq[:, :], start=True, stop=True)
                    for gb in range(2):
                        for k, s in ((0, img_sum), (2, img_sumsq)):
                            last = nc.tensor.matmul(ps[1][:, k + gb:k + gb + 1], s[:, gb * P:(gb + 1) * P],
                                                    K("ones")[:, 0:1], start=True, stop=True)
                    last.then_inc(stat_ps, 1)
                    pe.wait_ge(u_done, 1)
                    nc.tensor.matmul(ps[2][:, 0:NIMG], K("sym"), U3[:, 32, :], start=True, stop=True).then_inc(sym_ps, 1)
                    pe.wait_ge(weighted, 1)
                    for gb in range(2):
                        for b in range(4):
                            c = slice(gb * P + 32 * b, gb * P + 32 * b + 32)
                            for f in range(MF):
                                last = nc.tensor.matmul(ps[3][32 * b:32 * b + 32, 32 * gb:32 * gb + 32], O3[:, f, c], U3[:, f, c],
                                                        start=(f == 0), stop=(f == MF - 1))
                    last.then_inc(common_ps, 1)
                    pe.wait_ge(packed, 1)
                    with pe.Fori(0, TU) as i:
                        for u in range(2):
                            pe.wait_ge(*now(prod_ready, i, u))
                            pe.wait_ge(*prev2(taken, i, u))
                            pr = prod[u].rearrange("p (f n) -> p f n", f=JT)
                            for gb in range(2):
                                for b in range(4):
                                    c = slice(gb * P + 32 * b, gb * P + 32 * b + 32)
                                    for j in range(JT):
                                        last = nc.tensor.matmul(ps[4 + u][32 * b:32 * b + 32, 32 * gb:32 * gb + 32], pr[:, j, c],
                                                                LU3[:, j, c], start=(j == 0), stop=(j == JT - 1))
                            last.then_inc(score_ps[u], 1)
                    pe.wait_ge(mix_ready, 1)
                    for gb in range(2):
                        last = nc.tensor.matmul(ps[6][:, gb:gb + 1], mix_t[:, gb * P:(gb + 1) * P], vec[:, gb:gb + 1],
                                                start=True, stop=True)
                    last.then_inc(mix_ps, 1)

                @block.scalar
                def _(act):
                    act.wait_ge(var_ready, 1)
                    nc.scalar.activation(r[:, :], ex2[:, :], ACT.Sqrt).then_inc(root_ready, 1)
                    act.wait_ge(v_done, 1)
                    act.wait_ge(u_done, 1)
                    for dst, src in ((LU3, U3), (LV3, V3)):
                        nc.scalar.copy(dst[0:64, :, :], src[0:64, 0:17:2, :])
                        last = nc.scalar.copy(dst[64:128, 0:8, :], src[0:64, 1:17:2, :])
                    last.then_inc(packed, 2)
                    act.wait_ge(packed, 2)
                    act.wait_ge(g_done, 1)
                    with act.Fori(0, TU) as i:
                        for u in range(2):
                            act.wait_ge(*prev2(prod_ready, i, u))
                            for j in range(JT):
                                last = nc.scalar.activation(part[u][:, j * NIMG:(j + 1) * NIMG], LU3[:, j, :], ACT.Copy,
                                                            scale=g_r[:, bass.ds((2 * i + u) * JT + j, 1)])
                            last.then_inc(part_ready, 1)
                    act.wait_ge(shifted, 1)
                    nc.scalar.activation(scores[:, :], scores[:, :], ACT.Exp).then_inc(exped, 1)

                @block.gpsimd
                def _(pool):
                    free_all(pool)
                    link = linker(pool, lkp)
                    link(nc.gpsimd.memset(LU3[64:128, 8, :], 0.0))
                    link(nc.gpsimd.memset(LV3[64:128, 8, :], 0.0))
                    pool.wait_ge(root2, 1)
                    rb = r[:, 0:NIMG].unsqueeze(1).broadcast_to([P, MF, NIMG])
                    link(nc.gpsimd.tensor_tensor(V3, V3, rb, ALU.mult))
                    link(nc.gpsimd.memset(V3[0:1, 0, :], 0.0))
                    link(nc.gpsimd.tensor_scalar(V3[32:33, 0, :], V3[32:33, 0, :], 0.0, SM("norm1_b")[32:33, :], ALU.mult, ALU.add))
                    pool.sem_inc(v_done, 1)

                @block.vector
                def _(dve):
                    link = linker(dve, lk)
                    tt, ts = nc.vector.tensor_tensor, nc.vector.tensor_scalar
                    dve.wait_ge(stat_ps, 1)
                    link(ts(mean[:, 0:NIMG], ps[0][:, 0:NIMG], 1.0 / PIX, None, ALU.mult))
                    link(ts(ex2[:, 0:NIMG], ps[0][:, NIMG:2 * NIMG], 1.0 / PIX, None, ALU.mult))
                    link(ts(mean[:, NIMG:NIMG + 2], ps[1][:, 0:2], 1.0 / PIX, None, ALU.mult))
                    link(ts(ex2[:, NIMG:NIMG + 2], ps[1][:, 2:4], 1.0 / PIX, None, ALU.mult))
                    link(tt(r_tmp[:, :], mean[:, :], mean[:, :], ALU.mult))
                    link(tt(ex2[:, :], ex2[:, :], r_tmp[:, :], ALU.subtract))
                    inv_std(dve, link, ex2[:, :], r[:, :], r_tmp[:, :], var_ready, root_ready, 1)
                    link(ts(r[:, :], r[:, :], SM("norm1_w"), None, ALU.mult))
                    dve.sem_inc(root2, 1)
                    rb = r[:, 0:NIMG].unsqueeze(1).broadcast_to([P, MF, NIMG])
                    dve.wait_ge(u_saved, 16)
                    link(tt(U3, U3, rb, ALU.mult))
                    link(ts(U3[0:1, 0, :], U3[0:1, 0, :], 0.0, SM("norm1_b")[0:1, :], ALU.mult, ALU.add))
                    link(nc.vector.memset(U3[32:33, 0, :], 0.0))
                    dve.sem_inc(u_done, 1)
                    link(tt(O3[:, 0:32, :], U3[:, 0:32, :], K("wt")[:, 0:32].unsqueeze(2).broadcast_to([P, 32, NIMG]), ALU.mult))
                    dve.wait_ge(sym_ps, 1)
                    link(nc.vector.tensor_copy(O3[:, 32, :], ps[2][:, 0:NIMG]))
                    dve.sem_inc(weighted, 1)
                    dve.wait_ge(qk_in, 16)
                    v3 = lambda t: t.rearrange("p (n j) -> p n j", j=JT)
                    bc = lambda name: SM(name).unsqueeze(2).broadcast_to([P, NH, JT])
                    for c, dst, op in (("r", sym_r, ALU.add), ("i", sym_i, ALU.subtract)):
                        link(nc.vector.tensor_copy(dst[:, :], QK("q_" + c)))
                        z = v3(dst[:, :])[0:64, :, 0:1]
                        link(tt(z, z, QK("qrev_" + c)[0:64, :].unsqueeze(2), op))
                        link(ts(z, z, 0.5, None, ALU.mult))
                    link(tt(v3(sym_r[:, :]), v3(sym_r[:, :]), bc("Qsw"), ALU.add))
                    link(tt(g_r[:, :], sym_r[:, :], QK("k_r"), ALU.mult))
                    link(tt(tmp[:, :], sym_i[:, :], QK("k_i"), ALU.mult))
                    link(tt(g_r[:, :], g_r[:, :], tmp[:, :], ALU.add))
                    link(tt(v3(tmp[:, :]), v3(QK("q_r")), bc("Qsw"), ALU.add))
                    link(tt(v3(tmp[:, :]), v3(tmp[:, :]), bc("Ksw"), ALU.mult))
                    link(tt(g_r[:, :], g_r[:, :], tmp[:, :], ALU.add))
                    link(tt(g_i[:, :], sym_i[:, :], QK("k_r"), ALU.mult))
                    link(tt(tmp[:, :], sym_r[:, :], QK("k_i"), ALU.mult))
                    link(tt(g_i[:, :], g_i[:, :], tmp[:, :], ALU.subtract))
                    link(tt(v3(tmp[:, :]), v3(QK("q_i")), bc("Ksw"), ALU.mult))
                    link(tt(g_i[:, :], g_i[:, :], tmp[:, :], ALU.add))
                    lw = K("lw").unsqueeze(1).broadcast_to([P, NH, JT])
                    link(tt(v3(g_r[:, :]), v3(g_r[:, :]), lw, ALU.mult))
                    link(tt(v3(g_i[:, :]), v3(g_i[:, :]), lw, ALU.mult))
                    dve.sem_inc(g_done, 1)
                    dve.wait_ge(common_ps, 1)
                    link(nc.vector.tensor_copy(common[:, :], ps[3][:, 0:64]))
                    dve.wait_ge(packed, 2)
                    sc4 = scores[:, :].rearrange("p (g n s) -> p g n s", g=2, n=NH)

                    def take(i, u):
                        dve.wait_ge(*now(score_ps, i, u))
                        nc.vector.tensor_copy(sc4[:, :, bass.ds(2 * i + u, 1), :].rearrange("p g o s -> p g (o s)"),
                                              ps[4 + u][:, 0:64].rearrange("p (g s) -> p g s", g=2)).then_inc(taken[u], 1)

                    def head_step(i, u, first):
                        dve.wait_ge(*now(part_ready, i, u))
                        dve.wait_ge(*prev2(score_ps, i, u))
                        for j in range(JT):
                            c = slice(j * NIMG, (j + 1) * NIMG)
                            last = nc.vector.scalar_tensor_tensor(
                                prod[u][:, c], LV3[:, j, :], g_i[:, bass.ds((2 * i + u) * JT + j, 1)],
                                part[u][:, c], ALU.mult, ALU.add)
                        last.then_inc(prod_ready[u], 1)
                        if not first:
                            take(i - 1 + u, 1 - u)
                    head_step(0, 0, True)
                    head_step(0, 1, False)
                    with dve.Fori(1, TU) as i:
                        for u in range(2):
                            head_step(i, u, False)
                    take(TU - 1, 1)
                    for u in range(2):
                        dve.wait_ge(taken[u], done(taken, TU))
                    big = low_u[:, 0:2 * NH * 32]
                    big4 = big.rearrange("p (g n s) -> p g n s", g=2, n=NH)
                    com = common[:, :].rearrange("p (g s) -> p g s", g=2)
                    link(tt(vecn[:, :], SM("Qsw"), SM("Ksw"), ALU.mult))
                    for gb in range(2):
                        link(tt(big4[:, gb], com[:, gb:gb + 1, :].broadcast_to([P, NH, 32]),
                                vecn[:, :].unsqueeze(2).broadcast_to([P, NH, 32]), ALU.mult))
                    link(tt(scores[:, :], scores[:, :], big, ALU.add))
                    s3 = scores[:, :].rearrange("p (m s) -> p m s", s=32)
                    rd = red[:, :].unsqueeze(2).broadcast_to([P, 64, 32])
                    link(nc.vector.tensor_reduce(red[:, :], s3, AX.X, ALU.max))
                    link(tt(s3, s3, rd, ALU.subtract))
                    dve.sem_inc(shifted, 1)
                    dve.wait_ge(exped, 1)
                    link(nc.vector.tensor_reduce(red[:, :], s3, AX.X, ALU.add))
                    link(nc.vector.reciprocal(red[:, :], red[:, :]))
                    link(tt(s3, s3, rd, ALU.mult))
                    link(nc.vector.transpose(big, scores[:, :]))
                    link(nc.vector.memset(probs_bd[:, :], 0.0))
                    bd = probs_bd[:, :].rearrange("p (m c) -> p m c", c=P)
                    for b in range(4):
                        q = slice(32 * b, 32 * b + 32)
                        link(nc.vector.tensor_copy(bd[q, :, q], big[q, :].rearrange("p (m t) -> p m t", t=32)))
                    link(tt(vecn[:, :], SM("Psw"), SM("Vsw"), ALU.mult))
                    for gb in range(2):
                        link(tt(big4[:, gb], sc4[:, gb], vecn[:, :].unsqueeze(2).broadcast_to([P, NH, 32]), ALU.mult))
                    link(nc.vector.tensor_reduce(red[:, :], big.rearrange("p (g n s) -> p g s n", g=2, n=NH), AX.X, ALU.add))
                    link(nc.vector.transpose(common[:, :], red[:, :]))
                    link(nc.vector.memset(mix_t[:, :], 0.0))
                    for b in range(4):
                        q = slice(32 * b, 32 * b + 32)
                        link(nc.vector.tensor_copy(mix_t[:, :].rearrange("p (g c) -> p g c", g=2)[q, :, q],
                                                   common[q, :].rearrange("p (g t) -> p g t", g=2)))
                    link(tt(vec[:, 0:2], r[:, NIMG:NIMG + 2], mean[:, NIMG:NIMG + 2], ALU.mult))
                    link(ts(vec[:, 0:2], vec[:, 0:2], -1.0, SM("norm1_b"), ALU.mult, ALU.add))
                    dve.sem_inc(mix_ready, 1)
                    dve.wait_ge(mix_ps, 1)
                    link(nc.vector.tensor_copy(mix_const[:, :], ps[6][:, 0:2]))
                    for gb in range(2):
                        m = mix_t[:, gb * P:(gb + 1) * P]
                        link(nc.vector.scalar_tensor_tensor(m, m, r[:, NIMG + gb:NIMG + gb + 1], K("ident"), ALU.mult, ALU.add))
        turned.close()
        end_stage()

        with ExitStack() as st:
            def sb(name, cols):
                return st.enter_context(nc.sbuf_tensor(name, [P, cols], F32))
            NM = MF * NH
            hx = sb("s6_hx", 2 * NH * P)
            vp_base = wat["v_r"][0]
            vp_cols = weights.shape[1] - vp_base
            vp = hx[:, 0:vp_cols]

            def VP(name):
                a, n = wat[name]
                return hx[:, a - vp_base:a - vp_base + n]
            diag = [sb(f"s6_diag{u}", NH * 64) for u in range(2)]
            h_r, h_i = diag[0][:, 0:NM], diag[1][:, 0:NM]
            tmp = sb("s6_tmp", NM)[:, :]
            coef = sb("s6_coef", 2 * NM)
            col = [sb(f"s6_col{u}", NIMG) for u in range(2)]
            vp_in, lk, coef_ready = sem("s6_vp_in"), sem("s6_link"), sem("s6_coef_ready")
            ready, step_done = sem("s6_ready", 2), sem("s6_step_done", 2, 1)
            bank_ps, bank_sb = sem("s6_bank_ps", 4), sem("s6_bank_sb", 4, 1)
            out_ps, out_sb = sem("s6_out_ps", 2, 1), sem("s6_out_sb", 2, 1)
            U3, O3 = (t[:, :].rearrange("p (f n) -> p f n", f=MF) for t in (spec_u, spec_o))
            hx4 = hx[:, :].rearrange("p (g n h c) -> p g n h c", g=2, n=NH, h=2)
            FT = MF // 2

            def bank_step(i, u, g, half):
                return 8 * i + 4 * u + 2 * g + half

            with nc.Block() as block:
                @block.sync
                def _(sp):
                    sp.dma_start(vp, weights[:, vp_base:vp_base + vp_cols]).then_inc(vp_in, 16)

                @block.gpsimd
                def _(pool):
                    free_all(pool)

                @block.tensor
                def _(pe):
                    def step(i, u):
                        pe.wait_ge(*now(ready, i, u, 2))
                        for g in range(2):
                            for half in range(2):
                                r0 = 64 * half
                                for q in range(4):
                                    pe.wait_ge(bank_sb[q], bank_step(i, u, g, half) + 1)
                                    last = nc.tensor.matmul(ps[q][:, :], col[u][r0:r0 + 64, g * P:(g + 1) * P],
                                                            diag[u][r0:r0 + 64, 512 * q:512 * q + 512], start=True, stop=True)
                                    last.then_inc(bank_ps[q], 1)
                        for g in range(2):
                            for q in range(4):
                                pe.wait_ge(bank_sb[q], bank_step(i, u, g, 1) + 2)
                            pe.wait_ge(*prev(out_sb[g], i, u))
                            for n in range(NH):
                                m = g * NH + n
                                last = nc.tensor.matmul(ps[4 + g][:, 0:P], hx[:, m * P:(m + 1) * P], probs_bd[:, m * P:(m + 1) * P],
                                                        start=(n == 0), stop=(n == NH - 1))
                            last.then_inc(out_ps[g], 1)
                    with pe.Fori(0, FT) as i:
                        for u in range(2):
                            step(i, u)
                    step(FT, 0)

                def copy_banks(eng, op, qs, i, u, g):
                    for half in range(2):
                        for q in qs:
                            eng.wait_ge(bank_ps[q], bank_step(i, u, g, half) + 1)
                            if half == 0:
                                eng.wait_ge(*prev(out_ps[g], i, u))
                            op(hx4[:, g, 8 * q:8 * q + 8, half, :], ps[q][:, :].rearrange("p (n c) -> p n c", c=64)
                               ).then_inc(bank_sb[q], 1)

                @block.scalar
                def _(act):
                    act.wait_ge(coef_ready, 1)
                    with act.Fori(0, FT) as i:
                        for u in range(2):
                            for g in range(2):
                                copy_banks(act, nc.scalar.copy, (0, 2), i, u, g)
                    for g in range(2):
                        copy_banks(act, nc.scalar.copy, (0, 2), FT, 0, g)

                @block.vector
                def _(dve):
                    link = linker(dve, lk)
                    tt, ts = nc.vector.tensor_tensor, nc.vector.tensor_scalar
                    v3 = lambda t: t.rearrange("p (f n) -> p f n", n=NH)
                    bc = lambda name: SM(name).unsqueeze(1).broadcast_to([P, MF, NH])
                    dve.wait_ge(vp_in, 16)
                    link(tt(v3(h_r), v3(VP("v_r")), bc("Psw"), ALU.mult))
                    link(tt(v3(h_i), v3(VP("v_i")), bc("Psw"), ALU.mult))
                    for c, op in (("r", ALU.add), ("i", ALU.subtract)):
                        z = VP("v_" + c)[:, 0:NH]
                        link(tt(z, z, VP("vrev_" + c), op))
                        link(ts(z, z, 0.5, None, ALU.mult))
                    link(tt(v3(VP("v_r")), v3(VP("v_r")), bc("Vsw"), ALU.add))
                    for dst, a, b, op in ((h_r, "p_r", "v_r", ALU.add), (h_r, "p_i", "v_i", ALU.subtract),
                                          (h_i, "p_r", "v_i", ALU.add), (h_i, "p_i", "v_r", ALU.add)):
                        link(tt(tmp, VP(a), VP(b), ALU.mult))
                        link(tt(dst, dst, tmp, op))
                    c4 = coef[:, :].rearrange("p (m c) -> p m c", c=2)
                    for q in range(4):
                        r4 = slice(32 * q, 32 * q + 32)
                        if q % 2 == 0:
                            link(nc.vector.tensor_copy(c4[r4, :, 0], h_r[r4, :]))
                            link(nc.vector.tensor_copy(c4[r4, :, 1], h_i[r4, :]))
                        else:
                            link(ts(c4[r4, :, 0], h_i[r4, :], -1.0, None, ALU.mult))
                            link(nc.vector.tensor_copy(c4[r4, :, 1], h_r[r4, :]))
                    dve.sem_inc(coef_ready, 1)

                    def prepare(i, u):
                        dve.wait_ge(*prev2(step_done, i, u))
                        f = 2 * i + u
                        nc.vector.tensor_copy(col[u][:, :], spec_u[:, bass.ds(f * NIMG, NIMG)]).then_inc(ready[u], 1)
                        tt(diag[u][:, :].rearrange("p (m k) -> p m k", k=32),
                           coef[:, bass.ds(f * 2 * NH, 2 * NH)].unsqueeze(2).broadcast_to([P, 2 * NH, 32]),
                           K("mask").unsqueeze(1).broadcast_to([P, 2 * NH, 32]), ALU.mult).then_inc(ready[u], 1)

                    def take(i, u, g):
                        dve.wait_ge(*now(out_ps[g], i, u))
                        nc.vector.tensor_copy(spec_o[:, bass.ds((2 * i + u) * NIMG + g * P, P)], ps[4 + g][:, 0:P]
                                              ).then_inc(out_sb[g], 1)

                    def step(i, u, first=False, last=False):
                        copy_banks(dve, nc.vector.tensor_copy, (1, 3), i, u, 0)
                        if not first:
                            for g in range(2):
                                take(i - 1 + u, 1 - u, g)
                            dve.sem_inc(step_done[1 - u], 1)
                        if not last:
                            prepare(i + u, 1 - u)
                        copy_banks(dve, nc.vector.tensor_copy, (1, 3), i, u, 1)
                    prepare(0, 0)
                    step(0, 0, first=True)
                    step(0, 1)
                    with dve.Fori(1, FT) as i:
                        for u in range(2):
                            step(i, u)
                    step(FT, 0, last=True)
                    for g in range(2):
                        take(FT, 0, g)
        end_stage()

        with ExitStack() as st:
            def sb(name, cols):
                return st.enter_context(nc.sbuf_tensor(name, [P, cols], F32))
            PC = 2048
            g = [sb(f"s7_g{u}", PC) for u in range(2)]
            z = [sb(f"s7_z{u}", PC) for u in range(2)]
            g_in, mix_ps, stored = sem("s7_g_in", 2), sem("s7_mix_ps", 2, 1), sem("s7_stored", 2, 16)
            z_act, z_dve = sem("s7_z_act", 2, 1), sem("s7_z_dve", 2, 1)

            def pixels(t, i, u):
                return t.rearrange("b t y w -> (b t) (y w)")[u * P:(u + 1) * P, bass.ds(i * PC, PC)]
            with nc.Block() as block:
                @block.sync
                def _(sp):
                    with sp.Fori(0, PIX // PC) as i:
                        for u in range(2):
                            sp.wait_ge(*prev2(mix_ps, i, u))
                            sp.dma_start(g[u][:, :], pixels(g_d, i, u)).then_inc(g_in[u], 16)

                @block.gpsimd
                def _(pool):
                    free_all(pool)

                @block.tensor
                def _(pe):
                    with pe.Fori(0, PIX // PC) as i:
                        for u in range(2):
                            pe.wait_ge(*now(g_in, i, u, 16))
                            pe.wait_ge(*prev2(z_act, i, u))
                            pe.wait_ge(*prev2(z_dve, i, u))
                            for k in range(4):
                                last = nc.tensor.matmul(ps[4 * u + k][:, :], mix_t[:, u * P:(u + 1) * P],
                                                        g[u][:, k * 512:(k + 1) * 512], start=True, stop=True)
                            last.then_inc(mix_ps[u], 1)

                @block.scalar
                def _(act):
                    with act.Fori(0, PIX // PC) as i:
                        for u in range(2):
                            act.wait_ge(*now(mix_ps, i, u))
                            act.wait_ge(*prev2(stored, i, u, 16))
                            for k in (0, 2):
                                last = nc.scalar.activation(z[u][:, k * 512:(k + 1) * 512], ps[4 * u + k][:, :], ACT.Identity,
                                                            bias=mix_const[:, u:u + 1])
                            last.then_inc(z_act[u], 1)
                            act.wait_ge(*now(z_act, i, u))
                            act.wait_ge(*now(z_dve, i, u))
                            act.dma_start(pixels(z_d, i, u), z[u][:, :]).then_inc(stored[u], 16)
                    for u in range(2):
                        act.wait_ge(stored[u], done(stored, PIX // PC, 16))

                @block.vector
                def _(dve):
                    with dve.Fori(0, PIX // PC) as i:
                        for u in range(2):
                            dve.wait_ge(*now(mix_ps, i, u))
                            dve.wait_ge(*prev2(stored, i, u, 16))
                            for k in (1, 3):
                                last = nc.vector.tensor_scalar(z[u][:, k * 512:(k + 1) * 512], ps[4 * u + k][:, :],
                                                               mix_const[:, u:u + 1], None, ALU.add)
                            last.then_inc(z_dve[u], 1)
        end_stage()

        conv_var = keep("conv_var", NIMG)
        conv = spec_u
        with ExitStack() as st:
            def sb(name, cols):
                return st.enter_context(nc.sbuf_tensor(name, [P, cols], F32))
            gs = [sb(f"s8_gs{u}", NIMG) for u in range(2)]
            gt = [sb(f"s8_gt{u}", NIMG) for u in range(2)]
            ys = [sb(f"s8_ys{u}", NIMG) for u in range(2)]
            pr = [sb(f"s8_pr{u}", NIMG) for u in range(2)]
            sq = [sb(f"s8_sq{u}", NIMG) for u in range(2)]
            h0 = sb("s8_h0", NIMG)
            g_in, t_ps, t_sb, y_ps, y_sb, j_ps, pr_sb, c_sb, sq_sb, e_ps = (
                sem("s8_" + n, 2, s) for n, s in (("g_in", 0), ("t_ps", 1), ("t_sb", 1), ("y_ps", 1), ("y_sb", 1), ("j_ps", 1),
                                                  ("pr_sb", 0), ("c_sb", 1), ("sq_sb", 0), ("e_ps", 1)))
            h_ps, h_sb, d_ps, d_sb, e0_ps = (sem("s8_" + n) for n in ("h_ps", "h_sb", "d_ps", "d_sb", "e0_ps"))
            FT = MF // 2
            E = ps[6][:, 0:NIMG]
            with nc.Block() as block:
                @block.sync
                def _(sp):
                    with sp.Fori(0, FT) as i:
                        for u in range(2):
                            sp.wait_ge(*prev2(t_ps, i, u))
                            sp.dma_start(gs[u][:, :], u_d[:, bass.ds((2 * i + u + 1) * NIMG, NIMG)]).then_inc(g_in[u], 16)
                    sp.wait_ge(*prev2(t_ps, FT, 0))
                    sp.dma_start(gs[0][:, :], u_d[:, 0:NIMG]).then_inc(g_in[0], 16)

                @block.gpsimd
                def _(pool):
                    free_all(pool)

                @block.tensor
                def _(pe):
                    def transpose(i, u):
                        pe.wait_ge(*now(g_in, i, u, 16))
                        pe.wait_ge(*prev2(t_sb, i, u))
                        for g in range(2):
                            last = nc.tensor.matmul(ps[u][:, g * P:(g + 1) * P], gs[u][:, g * P:(g + 1) * P], K("ident"),
                                                    start=True, stop=True)
                        last.then_inc(t_ps[u], 1)

                    def mix(i, u):
                        pe.wait_ge(*now(t_sb, i, u))
                        pe.wait_ge(*prev2(y_sb, i, u))
                        for g in range(2):
                            last = nc.tensor.matmul(ps[2 + u][:, g * P:(g + 1) * P], gt[u][:, g * P:(g + 1) * P],
                                                    mix_t[:, g * P:(g + 1) * P], start=True, stop=True)
                        last.then_inc(y_ps[u], 1)

                    def turn(i, u):
                        pe.wait_ge(*now(y_sb, i, u))
                        pe.wait_ge(*prev2(c_sb, i, u))
                        nc.tensor.matmul(ps[4 + u][:, 0:NIMG], K("turn"), ys[u][:, :], start=True, stop=True).then_inc(j_ps[u], 1)

                    def energy(i, u, first=False):
                        pe.wait_ge(*now(sq_sb, i, u))
                        nc.tensor.matmul(E, K("twos"), sq[u][:, :], start=first, stop=False).then_inc(e_ps[u], 1)

                    def step(i, u, first=False, last=False):
                        mix(i, u)
                        if not last:
                            transpose(i + u, 1 - u)
                        if not first:
                            energy(i - 1 + u, 1 - u, first=(type(i) is int and i + u == 1))
                        turn(i, u)
                    nc.tensor.matmul(ps[7][:, 0:NIMG], K("herm_y"), spec_o[:, 0:NIMG], start=True, stop=True).then_inc(h_ps, 1)
                    transpose(0, 0)
                    step(0, 0, first=True)
                    step(0, 1)
                    with pe.Fori(1, FT) as i:
                        for u in range(2):
                            step(i, u)
                    step(FT, 0, last=True)
                    pe.wait_ge(*now(c_sb, FT, 0))
                    nc.tensor.matmul(ps[7][:, 0:NIMG], K("herm"), conv[:, 0:NIMG], start=True, stop=True).then_inc(d_ps, 1)
                    pe.wait_ge(d_sb, 1)
                    nc.tensor.matmul(E, K("energy0"), sq[0][:, :], start=False, stop=True).then_inc(e0_ps, 1)

                @block.scalar
                def _(act):
                    def copy_turned(i, u):
                        act.wait_ge(*now(t_ps, i, u))
                        act.wait_ge(*prev2(y_ps, i, u))
                        nc.scalar.copy(gt[u][:, :], ps[u][:, 0:NIMG]).then_inc(t_sb[u], 1)

                    def square(i, u):
                        act.wait_ge(*now(c_sb, i, u))
                        act.wait_ge(*prev2(e_ps, i, u))
                        nc.scalar.activation(sq[u][:, :], conv[:, bass.ds((2 * i + u + 1) * NIMG, NIMG)], ACT.Square
                                             ).then_inc(sq_sb[u], 1)
                    copy_turned(0, 0)
                    with act.Fori(0, FT) as i:
                        for u in range(2):
                            copy_turned(i + u, 1 - u)
                            square(i, u)
                    act.wait_ge(d_ps, 1)
                    act.wait_ge(*prev2(e_ps, FT, 0))
                    nc.scalar.activation(sq[0][:, :], ps[7][:, 0:NIMG], ACT.Square).then_inc(d_sb, 1)

                @block.vector
                def _(dve):
                    dve.wait_ge(h_ps, 1)
                    nc.vector.tensor_copy(h0[:, :], ps[7][:, 0:NIMG]).then_inc(h_sb, 1)
                    dve.wait_ge(h_sb, 1)

                    def step(i, u, f, attention):
                        dve.wait_ge(*now(y_ps, i, u))
                        dve.wait_ge(*prev2(j_ps, i, u))
                        nc.vector.tensor_tensor(ys[u][:, :], ps[2 + u][:, 0:NIMG], attention, ALU.add).then_inc(y_sb[u], 1)
                        dve.wait_ge(*now(y_sb, i, u))
                        nc.vector.tensor_scalar(pr[u][:, :], ys[u][:, :], SM("m0_r")[:, f], None, ALU.mult).then_inc(pr_sb[u], 1)
                        dve.wait_ge(*now(pr_sb, i, u))
                        dve.wait_ge(*now(j_ps, i, u))
                        nc.vector.scalar_tensor_tensor(conv[:, bass.ds(f.start * NIMG, NIMG) if type(f) is slice else
                                                            bass.ds((2 * i + u + 1) * NIMG, NIMG)],
                                                       ps[4 + u][:, 0:NIMG], SM("m0_i")[:, f], pr[u][:, :], ALU.mult, ALU.add
                                                       ).then_inc(c_sb[u], 1)
                    with dve.Fori(0, FT) as i:
                        for u in range(2):
                            step(i, u, bass.ds(2 * i + u + 1, 1), spec_o[:, bass.ds((2 * i + u + 1) * NIMG, NIMG)])
                    step(FT, 0, slice(0, 1), h0[:, :])
                    dve.wait_ge(e0_ps, 1)
                    nc.vector.tensor_copy(conv_var[:, :], E)
        end_stage()

        def inverse_rows(pe, i, u, h, spectrum, ready, bank, free, inv_ps):
            pe.wait_ge(*ready)
            pe.wait_ge(*free)
            for k in range(4):
                s = spectrum(4 * h + k)
                nc.tensor.matmul(bank[0:MF, k * N:(k + 1) * N], s, K("inv_re"), start=True, stop=True)
                last = nc.tensor.matmul(bank[64:64 + MF, k * N:(k + 1) * N], s, K("inv_im"), start=True, stop=True)
            last.then_inc(at(inv_ps[h], u), 1)

        def inverse_cols(pe, i, u, h, half, half_sb, bank, free, out_ps):
            pe.wait_ge(*now(half_sb[h], i, u))
            if free:
                pe.wait_ge(*free)
            for k in range(4):
                last = nc.tensor.matmul(bank[:, k * N:(k + 1) * N], half[0:64 + MF, k * N:(k + 1) * N],
                                        K("inv_w", 0, 64 + MF), start=True, stop=True)
            last.then_inc(at(out_ps[h], u), 1)

        def copy_half(i, u, h, half, bank, inv_ps, half_sb, out_ps):
            act = nc.scalar
            act.wait_ge(*now(inv_ps[h], i, u))
            act.wait_ge(*prev2(out_ps[h], i, u))
            nc.scalar.copy(half[0:MF, :], bank[0:MF, :])
            nc.scalar.copy(half[64:64 + MF, :], bank[64:64 + MF, :]).then_inc(half_sb[h][u], 1)

        with ExitStack() as st:
            def sb(name, cols):
                return st.enter_context(nc.sbuf_tensor(name, [P, cols], F32))
            z = [sb(f"s9_z{u}", CW) for u in range(2)]
            y = [sb(f"s9_y{u}", CW) for u in range(2)]
            sq = sb("s9_sq", CW)
            half = [[sb(f"s9_half{u}{h}", 512) for h in range(2)] for u in range(2)]
            chunk = [sb(f"s9_chunk{u}", MF * CH) for u in range(2)]
            ch3 = [c[:, :].rearrange("p (f n) -> p f n", n=CH) for c in chunk]
            z_in, stored, y_ready = sem("s9_z_in", 2), sem("s9_stored", 2, 16), sem("s9_y_ready", 2, 2)
            chunk_ready, zeroed = sem("s9_chunk_ready", 2), sem("s9_zeroed")
            inv_ps, half_sb, out_ps, taken = ([sem(f"s9_{n}{h}_", 2, 1) for h in range(2)] for n in ("inv_ps", "half_sb", "out_ps", "taken"))
            squared, reduced = sem("s9_squared"), sem("s9_reduced", None, 1)
            with nc.Block() as block:
                @block.sync
                def _(sp):
                    with sp.Fori(0, NT) as i:
                        for u in range(2):
                            sp.wait_ge(*prev2(y_ready, i, u, 2))
                            sp.dma_start(z[u][:, :], chunk_of(z_d, 2 * i + u)).then_inc(z_in[u], 16)

                @block.gpsimd
                def _(pool):
                    free_all(pool)
                    for t in half[0] + half[1]:
                        nc.gpsimd.memset(t[:, :], 0.0).then_inc(zeroed, 1)

                @block.tensor
                def _(pe):
                    def rows(i, u):
                        for h in range(2):
                            inverse_rows(pe, i, u, h, lambda n: ch3[u][:, :, n], now(chunk_ready, i, u), ps[2 * u + h],
                                         prev2(half_sb[h], i, u), inv_ps)

                    def turn(i, last):
                        for u in range(2):
                            if not (last and u):
                                rows(i + u, 1 - u)
                            for h in range(2):
                                inverse_cols(pe, i, u, h, half[u][h], half_sb, ps[4 + 2 * u + h], prev2(taken[h], i, u), out_ps)
                    rows(0, 0)
                    with pe.Fori(0, NT - 1) as i:
                        turn(i, False)
                    turn(NT - 1, True)

                @block.scalar
                def _(act):
                    def halves(i, u):
                        for h in range(2):
                            copy_half(i, u, h, half[u][h], ps[2 * u + h], inv_ps, half_sb, out_ps)

                    def turn(i, last):
                        for u in range(2):
                            if not (last and u):
                                halves(i + u, 1 - u)
                            act.wait_ge(*now(y_ready, i, u, 2))
                            act.dma_start(chunk_of(y_d, 2 * i + u), y[u][:, :]).then_inc(stored[u], 16)
                            act.wait_ge(*prev(reduced, i, u))
                            nc.scalar.activation(sq[:, :], y[u][:, :], ACT.Square).then_inc(squared, 1)
                    act.wait_ge(zeroed, 4)
                    halves(0, 0)
                    with act.Fori(0, NT - 1) as i:
                        turn(i, False)
                    turn(NT - 1, True)
                    for u in range(2):
                        act.wait_ge(stored[u], done(stored, NT, 16))

                @block.vector
                def _(dve):
                    def prepare(i, u):
                        dve.wait_ge(*prev2(inv_ps[1], i, u))
                        nc.vector.tensor_copy(ch3[u], spec_o[:, :].rearrange("p (f n) -> p f n", f=MF)[:, :, bass.ds(16 * i + 8 * u, CH)]
                                              ).then_inc(chunk_ready[u], 1)

                    def turn(i, last):
                        for u in range(2):
                            c = bass.ds(16 * i + 8 * u, CH)
                            dve.wait_ge(*now(z_in, i, u, 16))
                            dve.wait_ge(*prev2(stored, i, u, 16))
                            for h in range(2):
                                dve.wait_ge(*now(out_ps[h], i, u))
                                w = slice(512 * h, 512 * h + 512)
                                nc.vector.tensor_tensor(y[u][:, w], ps[4 + 2 * u + h][:, :], z[u][:, w], ALU.add).then_inc(y_ready[u], 1)
                                dve.sem_inc(taken[h][u], 1)
                            if not last:
                                prepare(i + 1, u)
                            dve.wait_ge(*now(y_ready, i, u, 2))
                            nc.vector.tensor_reduce(img_sum[:, c], y[u][:, :].rearrange("y (n w) -> y n w", n=CH), AX.X, ALU.add)
                            dve.wait_ge(*now(squared, i, u))
                            nc.vector.tensor_reduce(img_sumsq[:, c], sq[:, :].rearrange("y (n w) -> y n w", n=CH), AX.X,
                                                    ALU.add).then_inc(reduced, 1)
                    prepare(0, 0)
                    prepare(0, 1)
                    with dve.Fori(0, NT - 1) as i:
                        turn(i, False)
                    turn(NT - 1, True)
        end_stage()

        alpha, a_scale, a_shift, conv_scale, const, y_scale = (
            keep(n, NIMG) for n in ("alpha", "a_scale", "a_shift", "conv_scale", "const", "y_scale"))
        mean, var, root, tmp, tmp2 = (keep("img_" + n, NIMG) for n in ("mean", "var", "root", "tmp", "tmp2"))
        esum = keep("esum", 2 * NIMG)
        cross0 = keep("cross0", NIMG)
        conv1 = spec_o
        conv1_3 = conv1[:, :].rearrange("p (n f) -> p n f", f=MF)

        def counted(eng, link, i, u, per_step):
            count = [0]

            def run(ins, n=1):
                count[0] += n
                ins.then_inc(link, 1)
                eng.wait_ge(link, 2 * per_step * i + per_step * u + count[0])
            return run, count

        with ExitStack() as st:
            def sb(name, cols):
                return st.enter_context(nc.sbuf_tensor("s10_" + name, [P, cols], F32))

            def lsem(n, k=None, starts=0):
                return sem("s10_" + n, k, starts)
            yin = [sb(f"y{u}", CW) for u in range(2)]
            v = [sb(f"v{u}", CW) for u in range(2)]
            sq = sb("sq", CW)
            rf = sb("rowft", CH * 2 * N)[:, :].rearrange("w (n r) -> w n r", n=CH)
            half = [[sb(f"half{u}{h}", 512) for h in range(2)] for u in range(2)]
            chunk = [sb(f"chunk{u}", MF * CH) for u in range(2)]
            ch3 = [c[:, :].rearrange("p (f n) -> p f n", n=CH) for c in chunk]
            pr = [sb(f"pr{h}", 4 * MF) for h in range(2)]
            prt = [sb(f"prt{h}", 4 * MF) for h in range(2)]
            prod = [sb(f"prod{h}", 8 * MF) for h in range(2)]
            y_in, chunk_scaled, chunk_ready = lsem("y_in", 2), lsem("chunk_scaled", 2), lsem("chunk_ready", 2)
            inv_ps, half_sb, out_ps, taken, v_ready = ([lsem(f"{n}{h}_", 2, s) for h in range(2)] for n, s in (
                ("inv_ps", 1), ("half_sb", 0), ("out_ps", 1), ("taken", 1), ("v_ready", 0)))
            row_ps, col_ps, spec_done = lsem("row_ps", 2), lsem("col_ps", 2, 1), lsem("spec_done", 2, 1)
            row_sb = [lsem(f"row_sb{h}_", 2, 1) for h in range(2)]
            squared, reduced, zeroed, loop_link = lsem("squared"), lsem("reduced", None, 1), lsem("zeroed"), lsem("loop_link")
            m_stored = lsem("m_stored", 2, 16)
            tot_ps, var_ready, root_ready, lk = (lsem(n) for n in ("tot_ps", "var_ready", "root_ready", "link"))
            MR, MI = SM("m1_r"), SM("m1_i")
            with nc.Block() as block:
                @block.sync
                def _(sp):
                    with sp.Fori(0, NT) as i:
                        for u in range(2):
                            sp.wait_ge(*prev2(taken[1], i, u))
                            sp.dma_start(yin[u][:, :], chunk_of(y_d, 2 * i + u)).then_inc(y_in[u], 16)

                @block.gpsimd
                def _(pool):
                    free_all(pool)
                    for t in half[0] + half[1]:
                        nc.gpsimd.memset(t[:, :], 0.0).then_inc(zeroed, 1)

                @block.tensor
                def _(pe):
                    nc.tensor.matmul(ps[0][:, 0:NIMG], K("ones"), img_sum[:, :], start=True, stop=True)
                    nc.tensor.matmul(ps[0][:, NIMG:2 * NIMG], K("ones"), img_sumsq[:, :], start=True, stop=True).then_inc(tot_ps, 1)

                    def inv_rows(i, u):
                        for h in range(2):
                            inverse_rows(pe, i, u, h, lambda n: ch3[u][:, :, n], now(chunk_ready, i, u), ps[6 + h],
                                         prev(taken[h], i, u), inv_ps)

                    def inv_cols(i, u):
                        for h in range(2):
                            inverse_cols(pe, i, u, h, half[u][h], half_sb, ps[6 + h], None, out_ps)

                    def rows(i, u):
                        for h in range(2):
                            pe.wait_ge(*now(v_ready[h], i, u))
                            for free in row_sb[h]:
                                pe.wait_ge(*prev(free, i, u))
                            for k in range(4):
                                last = nc.tensor.matmul(ps[2 * h + k // 2][:, (k % 2) * 256:(k % 2) * 256 + 256],
                                                        v[u][:, (4 * h + k) * N:(4 * h + k + 1) * N], K("f1"), start=True, stop=True)
                            last.then_inc(row_ps[h], 1)

                    def cols(i, u):
                        for h in range(2):
                            for here in row_sb[h]:
                                pe.wait_ge(*now(here, i, u))
                            pe.wait_ge(*prev(spec_done[h], i, u))
                            for k in range(4):
                                o = ps[4 + h][:, k * 2 * MF:(k + 1) * 2 * MF]
                                nc.tensor.matmul(o, rf[:, 4 * h + k, 0:N], K("ga"), start=True, stop=False)
                                last = nc.tensor.matmul(o, rf[:, 4 * h + k, N:2 * N], K("gb"), start=False, stop=True)
                            last.then_inc(col_ps[h], 1)

                    def turn(i, last):
                        for u in range(2):
                            more = not (last and u)
                            if more:
                                inv_rows(i + u, 1 - u)
                            rows(i, u)
                            if more:
                                inv_cols(i + u, 1 - u)
                            cols(i, u)
                    inv_rows(0, 0)
                    inv_cols(0, 0)
                    with pe.Fori(0, NT - 1) as i:
                        turn(i, False)
                    turn(NT - 1, True)

                @block.scalar
                def _(act):
                    for n, t in enumerate((var, tmp2, tmp2)):
                        act.wait_ge(var_ready, n + 1)
                        nc.scalar.activation(root[:, :], t[:, :], ACT.Sqrt).then_inc(root_ready, 1)

                    def halves(i, u):
                        for h in range(2):
                            copy_half(i, u, h, half[u][h], ps[6 + h], inv_ps, half_sb, out_ps)

                    def gelu(i, u):
                        for h in range(2):
                            act.wait_ge(*now(taken[h], i, u))
                            w = slice(512 * h, 512 * h + 512)
                            nc.scalar.activation(v[u][:, w], v[u][:, w], ACT.Gelu).then_inc(v_ready[h][u], 1)
                        for h in range(2):
                            act.wait_ge(*now(v_ready[h], i, u))
                        act.dma_start(chunk_of(m_d, 2 * i + u), v[u][:, :]).then_inc(m_stored[u], 16)

                    def turn(i, last):
                        for u in range(2):
                            more = not (last and u)
                            if more:
                                halves(i + u, 1 - u)
                            for h in range(2):
                                copy_rows(act, nc.scalar.copy, 0, i, u, h, rf, row_ps, row_sb, col_ps)
                            if more:
                                gelu(i + u, 1 - u)
                            act.wait_ge(*prev(reduced, i, u))
                            nc.scalar.activation(sq[:, :], v[u][:, :], ACT.Square).then_inc(squared, 1)
                    act.wait_ge(zeroed, 4)
                    halves(0, 0)
                    gelu(0, 0)
                    with act.Fori(0, NT - 1) as i:
                        turn(i, False)
                    turn(NT - 1, True)
                    for u in range(2):
                        act.wait_ge(m_stored[u], done(m_stored, NT, 16))

                @block.vector
                def _(dve):
                    tt, ts, stt = nc.vector.tensor_tensor, nc.vector.tensor_scalar, nc.vector.scalar_tensor_tensor
                    link = linker(dve, lk)
                    dve.wait_ge(tot_ps, 1)
                    link(ts(mean[:, :], ps[0][:, 0:NIMG], 1.0 / PIX, None, ALU.mult))
                    link(ts(var[:, :], ps[0][:, NIMG:2 * NIMG], 1.0 / PIX, None, ALU.mult))
                    link(tt(tmp[:, :], mean[:, :], mean[:, :], ALU.mult))
                    link(tt(var[:, :], var[:, :], tmp[:, :], ALU.subtract))
                    inv_std(dve, link, var[:, :], root[:, :], tmp[:, :], var_ready, root_ready, 1)
                    link(ts(a_scale[:, :], root[:, :], SM("attn_w"), None, ALU.mult))
                    link(tt(a_shift[:, :], mean[:, :], a_scale[:, :], ALU.mult))
                    link(ts(a_shift[:, :], a_shift[:, :], -1.0, SM("attn_b"), ALU.mult, ALU.add))
                    link(ts(var[:, :], var[:, :], -EPS, None, ALU.add))
                    link(tt(tmp2[:, :], a_scale[:, :], a_scale[:, :], ALU.mult))
                    link(tt(tmp2[:, :], tmp2[:, :], var[:, :], ALU.mult))
                    inv_std(dve, link, tmp2[:, :], root[:, :], tmp[:, :], var_ready, root_ready, 2)
                    link(tt(alpha[:, :], a_scale[:, :], root[:, :], ALU.mult))
                    link(ts(alpha[:, :], alpha[:, :], SM("norm2_w"), None, ALU.mult))
                    link(tt(const[:, :], mean[:, :], alpha[:, :], ALU.mult))
                    link(ts(const[:, :], const[:, :], -1.0, SM("norm2_b"), ALU.mult, ALU.add))
                    link(ts(const[:, :], const[:, :], SM("m0sw"), None, ALU.mult))
                    link(ts(y_scale[:, :], alpha[:, :], SM("m0sw"), None, ALU.mult))
                    link(tt(tmp2[:, :], alpha[:, :], alpha[:, :], ALU.mult))
                    link(tt(tmp2[:, :], tmp2[:, :], conv_var[:, :], ALU.mult))
                    inv_std(dve, link, tmp2[:, :], root[:, :], tmp[:, :], var_ready, root_ready, 3)
                    link(tt(conv_scale[:, :], alpha[:, :], root[:, :], ALU.mult))
                    conv3 = conv[:, :].rearrange("p (f n) -> p f n", f=MF)

                    def prepare(i, u):
                        c = bass.ds(16 * i + 8 * u, CH)
                        dve.wait_ge(*prev2(inv_ps[1], i, u))
                        tt(ch3[u], conv3[:, :, c], conv_scale[:, c].unsqueeze(1).broadcast_to([P, MF, CH]), ALU.mult
                           ).then_inc(chunk_scaled[u], 1)
                        dve.wait_ge(*now(chunk_scaled, i, u))
                        nc.vector.tensor_copy(ch3[u][0:1, 0, :], const[0:1, c]).then_inc(chunk_ready[u], 1)

                    def layer_input(i, u):
                        dve.wait_ge(*now(y_in, i, u, 16))
                        dve.wait_ge(*prev2(m_stored, i, u, 16))
                        for h in range(2):
                            dve.wait_ge(*now(out_ps[h], i, u))
                            for n in range(4 * h, 4 * h + 4):
                                w = slice(n * N, (n + 1) * N)
                                k = n - 4 * h
                                last = stt(v[u][:, w], yin[u][:, w], y_scale[:, bass.ds(16 * i + 8 * u + n, 1)],
                                           ps[6 + h][:, k * N:(k + 1) * N], ALU.mult, ALU.add)
                            last.then_inc(taken[h][u], 1)

                    def turn(i, last):
                        for u in range(2):
                            run, count = counted(dve, loop_link, i, u, 6)
                            for h in range(2):
                                copy_rows(dve, nc.vector.tensor_copy, 1, i, u, h, rf, row_ps, row_sb, col_ps)
                            if not (last and u):
                                dve.wait_ge(*prev(reduced, i, u))
                                layer_input(i + u, 1 - u)
                            for h in range(2):
                                dve.wait_ge(*now(col_ps[h], i, u))
                                x = ps[4 + h][:, 0:8 * MF].rearrange("r (n a f) -> r a n f", n=4, a=2)
                                o = lambda t: t[:, :].rearrange("r (n f) -> r n f", n=4)
                                m = lambda w: w.unsqueeze(1).broadcast_to([P, 4, MF])
                                four = bass.ds(16 * i + 8 * u + 4 * h, 4)
                                tt(o(pr[h]), x[:, 0], m(MR), ALU.mult)
                                run(tt(o(prt[h]), x[:, 1], m(MI), ALU.mult))
                                run(tt(conv1_3[:, four, :], o(pr[h]), o(prt[h]), ALU.add))
                                pd = prod[h][:, :].rearrange("p (a n f) -> p a n f", a=2, f=MF)
                                tt(pd[:, 0], conv1_3[:, four, :], conv1_3[:, four, :], ALU.mult)
                                run(tt(pd[:, 1], conv1_3[:, four, :], x[:, 0], ALU.mult))
                                dve.sem_inc(spec_done[h], 1)
                                nc.vector.tensor_reduce(esum[:, :].rearrange("p (a n) -> p a n", a=2)[:, :, four], pd[:, :, :, 1:MF],
                                                        AX.X, ALU.add)
                                nc.vector.tensor_copy(cross0[:, four], pd[:, 1, :, 0])
                            assert count[0] == 6
                            if not last:
                                prepare(i + 1, u)
                            c = bass.ds(16 * i + 8 * u, CH)
                            nc.vector.tensor_reduce(img_sum[:, c], v[u][:, :].rearrange("y (n w) -> y n w", n=CH), AX.X, ALU.add)
                            dve.wait_ge(*now(squared, i, u))
                            nc.vector.tensor_reduce(img_sumsq[:, c], sq[:, :].rearrange("y (n w) -> y n w", n=CH), AX.X,
                                                    ALU.add).then_inc(reduced, 1)
                    prepare(0, 0)
                    prepare(0, 1)
                    layer_input(0, 0)
                    with dve.Fori(0, NT - 1) as i:
                        turn(i, False)
                    turn(NT - 1, True)
        end_stage()

        with ExitStack() as st:
            def sb(name, cols):
                return st.enter_context(nc.sbuf_tensor("s11_" + name, [P, cols], F32))

            def lsem(n, k=None, starts=0):
                return sem("s11_" + n, k, starts)
            names = ("x", "m", "y")
            tin = {n: [sb(f"{n}{u}", CW) for u in range(2)] for n in names}
            res = [sb(f"res{u}", CW) for u in range(2)]
            half = [[sb(f"half{u}{h}", 512) for h in range(2)] for u in range(2)]
            chunk = [sb(f"chunk{u}", MF * CH) for u in range(2)]
            ch3 = [c[:, :].rearrange("p (n f) -> p n f", f=MF) for c in chunk]
            herm_sq = sb("herm_sq", NIMG)
            m_scale, energy, cov = (sb(n, NIMG) for n in ("m_scale", "energy", "cov"))
            t_in, stored, finished, part = lsem("t_in", 2), lsem("stored", 2, 16), lsem("finished", 2, 1), lsem("part")
            chunk_scaled, chunk_ready = lsem("chunk_scaled", 2), lsem("chunk_ready", 2)
            inv_ps, half_sb, out_ps, taken = ([lsem(f"{n}{h}_", 2, 1) for h in range(2)] for n in ("inv_ps", "half_sb", "out_ps", "taken"))
            herm_ps, herm_sb, tot_ps, var_ready, root_ready, lk, zeroed = (
                lsem(n) for n in ("herm_ps", "herm_sb", "tot_ps", "var_ready", "root_ready", "link", "zeroed"))
            src = {"m": m_d, "y": y_d, "x": x1_d}
            with nc.Block() as block:
                @block.sync
                def _(sp):
                    with sp.Fori(0, NT) as i:
                        for u in range(2):
                            sp.wait_ge(*prev2(finished, i, u))
                            for n in names:
                                sp.dma_start(tin[n][u][:, :], chunk_of(src[n], 2 * i + u)).then_inc(t_in[u], 16)

                @block.gpsimd
                def _(pool):
                    free_all(pool)
                    for t in half[0] + half[1]:
                        nc.gpsimd.memset(t[:, :], 0.0).then_inc(zeroed, 1)

                @block.tensor
                def _(pe):
                    nc.tensor.matmul(ps[2][:, 0:NIMG], K("herm"), conv1_3[:, :, 0], start=True, stop=True).then_inc(herm_ps, 1)
                    nc.tensor.matmul(ps[0][:, 0:NIMG], K("ones"), img_sum[:, :], start=True, stop=True)
                    nc.tensor.matmul(ps[0][:, NIMG:2 * NIMG], K("ones"), img_sumsq[:, :], start=True, stop=True)
                    nc.tensor.matmul(ps[3][:, 0:NIMG], K("twos"), esum[:, NIMG:2 * NIMG], start=True, stop=False)
                    nc.tensor.matmul(ps[3][:, 0:NIMG], K("cov0"), cross0[:, :], start=False, stop=True)
                    nc.tensor.matmul(ps[1][:, 0:NIMG], K("twos"), esum[:, 0:NIMG], start=True, stop=False)
                    pe.wait_ge(herm_sb, 1)
                    nc.tensor.matmul(ps[1][:, 0:NIMG], K("energy0"), herm_sq[:, :], start=False, stop=True).then_inc(tot_ps, 1)

                    def rows(i, u):
                        for h in range(2):
                            inverse_rows(pe, i, u, h, lambda n: ch3[u][:, n, :], now(chunk_ready, i, u), ps[2 * u + h],
                                         prev2(half_sb[h], i, u), inv_ps)

                    def turn(i, last):
                        for u in range(2):
                            if not (last and u):
                                rows(i + u, 1 - u)
                            for h in range(2):
                                inverse_cols(pe, i, u, h, half[u][h], half_sb, ps[4 + 2 * u + h], prev2(taken[h], i, u), out_ps)
                    rows(0, 0)
                    with pe.Fori(0, NT - 1) as i:
                        turn(i, False)
                    turn(NT - 1, True)

                @block.scalar
                def _(act):
                    act.wait_ge(herm_ps, 1)
                    nc.scalar.activation(herm_sq[:, :], ps[2][:, 0:NIMG], ACT.Square).then_inc(herm_sb, 1)
                    for n in range(2):
                        act.wait_ge(var_ready, n + 1)
                        nc.scalar.activation(root[:, :], var[:, :], ACT.Sqrt).then_inc(root_ready, 1)

                    def halves(i, u):
                        for h in range(2):
                            copy_half(i, u, h, half[u][h], ps[2 * u + h], inv_ps, half_sb, out_ps)

                    def turn(i, last):
                        for u in range(2):
                            if not (last and u):
                                halves(i + u, 1 - u)
                            act.wait_ge(*now(finished, i, u))
                            act.dma_start(chunk_of(out, 2 * i + u), res[u][:, :]).then_inc(stored[u], 16)
                    act.wait_ge(zeroed, 4)
                    halves(0, 0)
                    with act.Fori(0, NT - 1) as i:
                        turn(i, False)
                    turn(NT - 1, True)
                    for u in range(2):
                        act.wait_ge(stored[u], done(stored, NT, 16))

                @block.vector
                def _(dve):
                    tt, ts, stt = nc.vector.tensor_tensor, nc.vector.tensor_scalar, nc.vector.scalar_tensor_tensor
                    link = linker(dve, lk)
                    dve.wait_ge(tot_ps, 1)
                    link(nc.vector.tensor_copy(energy[:, :], ps[1][:, 0:NIMG]))
                    link(nc.vector.tensor_copy(cov[:, :], ps[3][:, 0:NIMG]))
                    link(nc.vector.tensor_copy(var[:, :], energy[:, :]))
                    inv_std(dve, link, var[:, :], root[:, :], tmp[:, :], var_ready, root_ready, 1)
                    link(nc.vector.tensor_copy(conv_scale[:, :], root[:, :]))
                    link(ts(mean[:, :], ps[0][:, 0:NIMG], 1.0 / PIX, None, ALU.mult))
                    link(ts(var[:, :], ps[0][:, NIMG:2 * NIMG], 1.0 / PIX, None, ALU.mult))
                    link(tt(tmp[:, :], mean[:, :], mean[:, :], ALU.mult))
                    link(tt(var[:, :], var[:, :], tmp[:, :], ALU.subtract))
                    link(tt(cov[:, :], cov[:, :], conv_scale[:, :], ALU.mult))
                    link(ts(cov[:, :], cov[:, :], 2.0, None, ALU.mult))
                    link(stt(var[:, :], var[:, :], SM("m1sw"), cov[:, :], ALU.mult, ALU.add))
                    link(tt(energy[:, :], energy[:, :], conv_scale[:, :], ALU.mult))
                    link(tt(energy[:, :], energy[:, :], conv_scale[:, :], ALU.mult))
                    link(stt(var[:, :], var[:, :], SM("m1sw"), energy[:, :], ALU.mult, ALU.add))
                    inv_std(dve, link, var[:, :], root[:, :], tmp[:, :], var_ready, root_ready, 2)
                    link(ts(root[:, :], root[:, :], SM("mon_w"), None, ALU.mult))
                    link(tt(conv_scale[:, :], conv_scale[:, :], root[:, :], ALU.mult))
                    link(ts(m_scale[:, :], root[:, :], SM("m1sw"), None, ALU.mult))
                    link(tt(tmp[:, :], mean[:, :], m_scale[:, :], ALU.mult))
                    link(tt(tmp[:, :], a_shift[:, :], tmp[:, :], ALU.subtract))
                    link(ts(const[:, :], tmp[:, :], SM("mon_b"), None, ALU.add))

                    def prepare(i, u):
                        c = bass.ds(16 * i + 8 * u, CH)
                        dve.wait_ge(*prev2(inv_ps[1], i, u))
                        tt(ch3[u], conv1_3[:, c, :], conv_scale[:, c].unsqueeze(2).broadcast_to([P, CH, MF]), ALU.mult
                           ).then_inc(chunk_scaled[u], 1)
                        dve.wait_ge(*now(chunk_scaled, i, u))
                        nc.vector.tensor_copy(ch3[u][0:1, :, 0], const[0:1, c]).then_inc(chunk_ready[u], 1)

                    def turn(i, last):
                        for u in range(2):
                            dve.wait_ge(*now(t_in, i, u, 48))
                            dve.wait_ge(*prev2(stored, i, u, 16))
                            for h in range(2):
                                dve.wait_ge(*now(out_ps[h], i, u))
                                w = slice(512 * h, 512 * h + 512)
                                tt(res[u][:, w], ps[4 + 2 * u + h][:, :], tin["x"][u][:, w], ALU.add).then_inc(taken[h][u], 1)
                            if not last:
                                prepare(i + 1, u)
                            for h in range(2):
                                dve.wait_ge(*now(taken[h], i, u))
                            for n in range(CH):
                                w = slice(n * N, (n + 1) * N)
                                c = bass.ds(16 * i + 8 * u + n, 1)
                                last_m = stt(res[u][:, w], tin["m"][u][:, w], m_scale[:, c], res[u][:, w], ALU.mult, ALU.add)
                            last_m.then_inc(part, 1)
                            dve.wait_ge(*now(part, i, u))
                            for n in range(CH):
                                w = slice(n * N, (n + 1) * N)
                                c = bass.ds(16 * i + 8 * u + n, 1)
                                last_y = stt(res[u][:, w], tin["y"][u][:, w], a_scale[:, c], res[u][:, w], ALU.mult, ALU.add)
                            last_y.then_inc(finished[u], 1)
                    prepare(0, 0)
                    prepare(0, 1)
                    with dve.Fori(0, NT - 1) as i:
                        turn(i, False)
                    turn(NT - 1, True)


def kernel(**inputs):
    import concourse.bacc as _bacc
    from concourse.bass_utils import run_bass_kernel_spmd as _run

    nc = _bacc.Bacc("TRN2", target_bir_lowering=False, num_devices=1)
    consts, cat = shape_constants()
    weights, wat = lay_weights(inputs)
    arrays = {
        "in_x": np.ascontiguousarray(inputs["x"]),
        "in_w_re": np.ascontiguousarray(inputs["L0_conv_weight_real"]),
        "in_w_im": np.ascontiguousarray(inputs["L0_conv_weight_imag"]),
        "in_consts": consts, "in_weights": weights,
    }
    ap = {k: nc.dram_tensor(k, a.shape, F32, kind="ExternalInput").ap() for k, a in arrays.items()}
    out = nc.dram_tensor("out_0", (B, T, N, N), F32, kind="ExternalOutput").ap()
    build(nc, ap["in_x"], ap["in_w_re"], ap["in_w_im"], ap["in_consts"], cat, ap["in_weights"], wat, out)
    r = _run(nc, [arrays], core_ids=[0])
    return r.results[0]["out_0"]
```

```python
from contextlib import ExitStack

import numpy as np
import concourse.bass as bass
from concourse import mybir

F32 = mybir.dt.float32
ALU = mybir.AluOpType
ACT = mybir.ActivationFunctionType
AX = mybir.AxisListType

B, T, N = 8, 32, 128
NH = 32
P = 128
NIMG = B * T
NF = N // 2 + 1
ND = 2 * NF
MF = 33
HM = 64
JT = 9
CH = B
CW = CH * N
GRP = 4
PERGRP = float(T * N * GRP)
PIX = N * N
EPS = 1e-5
LOW = list(range(16)) + list(range(-16, 0))
HIGH = list(range(16, 32)) + list(range(-32, -16))
ROW_HF = np.array([(LOW, HIGH)[h][k] for h in range(2) for c in range(2) for k in range(32)])
ROW_C = np.array([c for h in range(2) for c in range(2) for k in range(32)])


def pack(parts):
    at, cols, where = 0, [], {}
    for name, a in parts:
        a = np.ascontiguousarray(a, dtype=np.float32).reshape(P, -1)
        where[name] = (at, a.shape[1])
        at += a.shape[1]
        cols.append(a)
    return np.concatenate(cols, axis=1), where


def shape_constants():
    y = np.arange(N)
    th = 2 * np.pi * np.outer(y, ROW_HF) / N
    c, s = np.cos(th), -np.sin(th)
    f1 = np.concatenate([np.where(ROW_C == 0, c, s), np.where(ROW_C == 0, -s, c)], 1) / N
    wf = np.arange(MF)
    tw = 2 * np.pi * np.outer(y, wf) / N
    fr, fi = np.cos(tw) / N, -np.sin(tw) / N
    tj = 2 * np.pi * np.outer(ROW_HF, y) / N
    cc = ROW_C[:, None] == 0
    inv_re = np.where(cc, np.cos(tj), -np.sin(tj))
    inv_im = np.where(cc, np.sin(tj), np.cos(tj))
    inv_w = np.zeros((P, N))
    m = np.where(wf == 0, 1.0, 2.0)[:, None]
    inv_w[0:MF] = m * np.cos(tw.T)
    inv_w[64:64 + MF] = -m * np.sin(tw.T)
    sym = np.zeros((P, P))
    for r in range(P):
        part = -ROW_HF[r] if ROW_HF[r] != -32 else -32
        r2 = int(np.nonzero((ROW_HF == part) & (ROW_C == ROW_C[r]))[0][0])
        sym[r, r] += 32.0
        sym[r, r2] += 32.0 if ROW_C[r] == 0 else -32.0
    herm, turn = np.zeros((P, P)), np.zeros((P, P))
    for r in range(P):
        if ROW_HF[r] == -32:
            herm[r, r] = 1.0
        else:
            r2 = int(np.nonzero((ROW_HF == -ROW_HF[r]) & (ROW_C == ROW_C[r]))[0][0])
            herm[r, r] += 0.5
            herm[r, r2] += 0.5 if ROW_C[r] == 0 else -0.5
        turn[r + 32 if ROW_C[r] == 0 else r - 32, r] = -1.0 if ROW_C[r] == 0 else 1.0
    herm_y = herm * np.where(ROW_HF == -32, 0.5, 1.0)[None, :]
    cov0 = np.where(ROW_HF == 0, 0.0, 1.0)[:, None] * np.ones((1, P))
    energy0 = cov0 * np.where(ROW_HF == -32, 0.5, 1.0)[:, None]
    wt = np.full((P, MF), 128.0)
    wt[:, 0] = 64.0
    wt[:64, :17] = 0.0
    wt[(ROW_HF == -32) & (ROW_C == 1), 0] = 0.0
    lw = np.full((P, JT), 128.0)
    lw[:64, 0] = 64.0
    hf = (np.arange(N) + 64) % N
    t0 = 2 * np.pi * np.outer(y, hf) / N
    g1 = np.concatenate([np.cos(t0), -np.sin(t0)], 1) / N
    wj = 64 - np.arange(NF)
    tj0 = 2 * np.pi * np.outer(y, wj) / N
    ar, ai = np.cos(tj0) / N, -np.sin(tj0) / N
    m0 = np.where((wj == 0) | (wj == 64), 1.0, 2.0)[:, None]
    k0 = np.concatenate([m0 * np.cos(tj0.T), (-m0 * np.sin(tj0.T))[1:64]], 0)
    grp = (np.arange(N)[:, None] // GRP == np.arange(N)[None, :] // GRP) / PERGRP
    return pack([
        ("f1", f1), ("ga", np.concatenate([fr, -fi], 1)), ("gb", np.concatenate([fi, fr], 1)),
        ("inv_re", inv_re), ("inv_im", inv_im), ("inv_w", inv_w), ("sym", sym), ("wt", wt), ("lw", lw),
        ("g1", g1), ("g2a", np.concatenate([ar, ai], 1)), ("g2b", np.concatenate([-ai, ar], 1)),
        ("cos0", np.cos(t0.T)), ("sin0", np.sin(t0.T)), ("k0", k0), ("grp", grp),
        ("ones", np.ones((P, P))), ("ident", np.eye(P)),
        ("batch", (np.arange(P)[:, None] // (P // B) == np.arange(B)[None, :]) * 1.0),
        ("herm", herm), ("herm_y", herm_y), ("turn", turn), ("cov0", cov0), ("energy0", energy0),
        ("twos", np.full((P, P), 2.0)), ("mask", np.tile(np.eye(32), (4, 1))),
    ])


def lay_weights(d):
    rows = np.array([[(LOW + HIGH).index(h) for h in (LOW, HIGH)[k]] for k in range(2) for c in range(2)]).reshape(-1)
    std = list(range(32)) + list(range(-32, 0))
    order = [std.index(h) for h in LOW + HIGH]

    def packed(w):
        w = w[0]
        full = np.concatenate([w, np.zeros_like(w[:, :, :1])], 2)
        even, odd = full[:, :, 0::2], full[:, :, 1::2]
        return np.concatenate([even, even, odd, odd], 1).transpose(1, 0, 2)

    def by_row(w):
        return w[:, rows, :].transpose(1, 2, 0)

    def mirrored(w):
        hs = LOW + HIGH
        out = np.zeros_like(w)
        for j, h in enumerate(hs):
            if -h in hs:
                out[:, j] = w[:, hs.index(-h)]
        return out

    groups = {"small": [], "qk": [], "vp": []}
    for c, name in ((0, "r"), (1, "i")):
        q, k = d["L1_conv_Qcw"][..., c], d["L1_conv_Kcw"][..., c]
        v = np.zeros((NH, HM, MF), np.float32)
        v[:, :32, :17] = d["L1_conv_Vcw"][0, ..., c]
        q0 = np.zeros((NH, HM), np.float32)
        q0[:, :32] = q[0, :, :, 0]
        groups["qk"] += [("q_" + name, packed(q)), ("k_" + name, packed(k)), ("qrev_" + name, mirrored(q0)[:, rows].T)]
        groups["vp"] += [("v_" + name, by_row(v)), ("vrev_" + name, mirrored(v[:, :, 0])[:, rows].T),
                         ("p_" + name, by_row(d["L1_conv_Pcw"][:, 0, ..., c][:, order]))]
        groups["small"] += [("m0_" + name, by_row(d["L1_conv_m0cw"][:, 0, ..., c][:, order])),
                            ("m1_" + name, by_row(d["L1_conv_m1cw"][:, 0, ..., c][:, order]))]
    for name in ("Qsw", "Ksw", "Vsw", "Psw"):
        groups["small"].append((name, np.broadcast_to(d["L1_conv_" + name].reshape(1, NH), (P, NH))))
    for name in ("norm1_w", "norm1_b", "attn_w", "attn_b", "norm2_w", "norm2_b", "m0sw", "m1sw", "mon_w", "mon_b"):
        groups["small"].append((name, np.broadcast_to(d["L1_conv_" + name].reshape(1, 1), (P, 1))))
    parts = groups["small"] + groups["qk"] + groups["vp"]
    return pack(parts)


START = {}


def begins(s):
    return START.get((s[0] if isinstance(s, list) else s).name, 0)


def at(s, u):
    return s[u] if isinstance(s, list) else s


def now(s, i, u, by=1):
    return at(s, u), (by * (i + 1) if isinstance(s, list) else by * (2 * i + u + 1)) + begins(s)


def prev(s, i, u, by=1):
    assert begins(s) > 0 or (u and not isinstance(s, list))
    return (s[1 - u], by * (i + u) + begins(s)) if isinstance(s, list) else (s, by * (2 * i + u) + begins(s))


def prev2(s, i, u, by=1):
    assert begins(s) > 0
    return s[u], by * i + begins(s)


def done(s, steps, by=1):
    return by * steps + begins(s)


def build(nc, x, w_re, w_im, consts, cat, weights, wat, out):
    x1_d = nc.dram_tensor("x1_d", (T, P, CW), F32).ap()
    g_d = nc.dram_tensor("g_d", (B, T, N, N), F32).ap()
    z_d = nc.dram_tensor("z_d", (B, T, N, N), F32).ap()
    y_d = nc.dram_tensor("y_d", (T, P, CW), F32).ap()
    u_d = nc.dram_tensor("u_d", (P, MF * NIMG), F32).ap()
    m_d = nc.dram_tensor("m_d", (T, P, CW), F32).ap()
    xs_d = nc.dram_tensor("xs_d", (N, 2, T, B, NF), F32).ap()
    ds_d = nc.dram_tensor("ds_d", (N, T, B, ND), F32).ap()

    whole = ExitStack()
    pending, in_stage = [], []

    def sem(name, n=None, starts=0):
        if n is not None:
            return [sem(f"{name}{i}", None, starts) for i in range(n)]
        s = nc.alloc_semaphore(name)
        in_stage.append(s)
        if starts:
            START[s.name] = starts
            pending.append(s)
        return s

    def pool_dma_sem(name):
        return [nc.alloc_semaphore(f"{name}{u}") for u in range(2)]

    def free_all(eng):
        for s in pending:
            eng.sem_inc(s, START[s.name])
        pending.clear()

    def end_stage():
        with nc.Block() as block:
            @block.gpsimd
            def _(pool):
                for s in in_stage:
                    pool.sem_clear(s)
        for s in in_stage:
            nc.release_semaphore(s)
        in_stage.clear()

    def laid_channel(t, c):
        return t[bass.ds(c, 1), :, :].rearrange("o y n -> y (o n)")

    def channel_of(t, c):
        return t[:, bass.ds(c, 1), :, :].rearrange("b o y w -> y (b o) w")

    with whole:
        def keep(name, cols):
            return whole.enter_context(nc.sbuf_tensor(name, [P, cols], F32))

        cst = keep("cst", consts.shape[1])
        def K(name, lo=0, hi=P):
            a, n = cat[name]
            return cst[lo:hi, a:a + n]

        ps = [whole.enter_context(nc.psum_tensor(f"bank{i}", [P, 512], F32)) for i in range(8)]
        gn_scale = keep("gn_scale", B)
        gn_shift = keep("gn_shift", B)

        def linker(eng, link):
            count = [0]

            def run(ins):
                count[0] += 1
                ins.then_inc(link, 1)
                eng.wait_ge(link, count[0])
            return run

        def inv_std(dve, link, v, r, tmp, var_ready, root_ready, n):
            nc.vector.tensor_scalar(v, v, 0.0, EPS, ALU.max, ALU.add).then_inc(var_ready, 1)
            dve.wait_ge(root_ready, n)
            link(nc.vector.reciprocal(r, r))
            link(nc.vector.tensor_tensor(tmp, r, r, ALU.mult))
            link(nc.vector.tensor_tensor(tmp, tmp, v, ALU.mult))
            link(nc.vector.tensor_scalar(tmp, tmp, -0.5, 1.5, ALU.mult, ALU.add))
            link(nc.vector.tensor_tensor(r, r, tmp, ALU.mult))

        with ExitStack() as st:
            def sb(name, cols):
                return st.enter_context(nc.sbuf_tensor(name, [P, cols], F32))
            SW = 2 * CW
            STEPS = 2 * PIX // SW
            xin = [sb(f"s0_x{u}", SW) for u in range(2)]
            sq = [sb(f"s0_q{u}", SW) for u in range(2)]
            acc, acq = sb("s0_sum", SW), sb("s0_sumsq", SW)
            x_flat = x.rearrange("b (q t) y w -> (b q) (t y w)", t=2)
            cols, grp, tmp = sb("s0_cols", 16), sb("s0_grp", 16), sb("s0_tmp", 8)
            const_in, zeroed, col_ps = sem("const_in"), sem("s0_zeroed"), sem("s0_col_ps")
            x_in = sem("s0_x_in", 2)
            squared, summed, sqsummed = (sem("s0_" + n, 2, 1) for n in ("squared", "summed", "sqsummed"))
            lk, col_sb, grp_ps, var_ready, root_ready = (
                sem("s0_" + n) for n in ("link", "col_sb", "grp_ps", "var_ready", "root_ready"))
            with nc.Block() as block:
                @block.sync
                def _(sp):
                    sp.dma_start(cst[:, :], consts).then_inc(const_in, 16)
                    with sp.Fori(0, STEPS // 2) as i:
                        for u in range(2):
                            sp.wait_ge(*prev2(summed, i, u))
                            sp.wait_ge(*prev2(squared, i, u))
                            sp.dma_start(xin[u][:, :], x_flat[:, bass.ds((2 * i + u) * SW, SW)]).then_inc(x_in[u], 16)

                @block.gpsimd
                def _(pool):
                    free_all(pool)

                @block.scalar
                def _(act):
                    with act.Fori(0, STEPS // 2) as i:
                        for u in range(2):
                            act.wait_ge(*now(x_in, i, u, 16))
                            act.wait_ge(*prev2(sqsummed, i, u))
                            nc.scalar.activation(sq[u][:, :], xin[u][:, :], ACT.Square).then_inc(squared[u], 1)
                    act.wait_ge(var_ready, 1)
                    nc.scalar.activation(gn_scale[:, :], grp[:, 8:16], ACT.Sqrt).then_inc(root_ready, 1)

                @block.vector
                def _(dve):
                    nc.vector.memset(acc[:, :], 0.0).then_inc(zeroed, 1)
                    nc.vector.memset(acq[:, :], 0.0).then_inc(zeroed, 1)
                    dve.wait_ge(zeroed, 2)
                    with dve.Fori(0, STEPS // 2) as i:
                        for u in range(2):
                            dve.wait_ge(*now(x_in, i, u, 16))
                            dve.wait_ge(*prev(summed, i, u))
                            nc.vector.tensor_tensor(acc[:, :], acc[:, :], xin[u][:, :], ALU.add).then_inc(summed[u], 1)
                            dve.wait_ge(*now(squared, i, u))
                            dve.wait_ge(*prev(sqsummed, i, u))
                            nc.vector.tensor_tensor(acq[:, :], acq[:, :], sq[u][:, :], ALU.add).then_inc(sqsummed[u], 1)
                    link = linker(dve, lk)
                    dve.wait_ge(col_ps, 1)
                    link(nc.vector.tensor_copy(cols[:, 0:8], ps[0][:, 0:8]))
                    nc.vector.tensor_copy(cols[:, 8:16], ps[2][:, 0:8]).then_inc(col_sb, 1)
                    dve.wait_ge(grp_ps, 1)
                    link(nc.vector.tensor_copy(grp[:, :], ps[1][:, 0:16]))
                    mean, var = grp[:, 0:8], grp[:, 8:16]
                    link(nc.vector.tensor_tensor(tmp[:, :], mean, mean, ALU.mult))
                    link(nc.vector.tensor_tensor(var, var, tmp[:, :], ALU.subtract))
                    inv_std(dve, link, var, gn_scale[:, :], tmp[:, :], var_ready, root_ready, 1)
                    link(nc.vector.tensor_tensor(gn_shift[:, :], mean, gn_scale[:, :], ALU.mult))
                    link(nc.vector.tensor_scalar_mul(gn_shift[:, :], gn_shift[:, :], -1.0))

                @block.tensor
                def _(pe):
                    pe.wait_ge(const_in, 16)
                    for u in range(2):
                        pe.wait_ge(summed[u], done(summed, STEPS // 2))
                        pe.wait_ge(sqsummed[u], done(sqsummed, STEPS // 2))
                    for bank, t in ((0, acc), (2, acq)):
                        for j in range(SW // N):
                            last = nc.tensor.matmul(ps[bank][:, 0:B], t[:, j * N:(j + 1) * N], K("batch"),
                                                    start=(j == 0), stop=(j == SW // N - 1))
                    last.then_inc(col_ps, 1)
                    pe.wait_ge(col_sb, 1)
                    nc.tensor.matmul(ps[1][:, 0:16], K("grp"), cols[:, :], start=True, stop=True).then_inc(grp_ps, 1)

        end_stage()

        with ExitStack() as st:
            def sb(name, cols):
                return st.enter_context(nc.sbuf_tensor(name, [P, cols], F32))
            xin = [sb(f"s1_x{u}", CW) for u in range(2)]
            rowft = [sb(f"s1_rowft{u}", B * 2 * N) for u in range(2)]
            spec = [sb(f"s1_spec{u}", B * ND) for u in range(2)]
            rf = [t[:, :].rearrange("w (b r) -> w b r", b=B) for t in rowft]
            row_act, row_dve, row_ready, col_ps, row_ps = ([sem(f"s1_{n}{h}_", 2, s) for h in range(2)] for n, s in (
                ("row_act", 1), ("row_dve", 1), ("row_ready", 0), ("col_ps", 1), ("row_ps", 1)))
            col_act, col_dve = ([sem(f"s1_{n}{h}", 2, 1) for h in range(2)] for n in ("col_act", "col_dve"))
            x_in, stored = sem("s1_x_in", 2), sem("s1_stored", 2, 32)
            with nc.Block() as block:
                @block.sync
                def _(sp):
                    with sp.Fori(0, T // 2) as i:
                        for u in range(2):
                            sp.wait_ge(*prev2(row_ps[1], i, u))
                            sp.dma_start(xin[u][:, :], channel_of(x, 2 * i + u)).then_inc(x_in[u], 16)

                @block.gpsimd
                def _(pool):
                    free_all(pool)

                @block.tensor
                def _(pe):
                    def rows(i, u):
                        pe.wait_ge(*now(x_in, i, u, 16))
                        for h in range(2):
                            pe.wait_ge(*prev(row_act[h], i, u))
                            pe.wait_ge(*prev(row_dve[h], i, u))
                            for k in range(4):
                                b = 4 * h + k
                                last = nc.tensor.matmul(ps[2 * h + k // 2][:, (k % 2) * 256:(k % 2) * 256 + 256],
                                                        xin[u][:, b * N:(b + 1) * N], K("g1"), start=True, stop=True)
                            last.then_inc(row_ps[h][u], 1)

                    def turn(i, last_turn):
                        for u in range(2):
                            if not (last_turn and u):
                                rows(i + u, 1 - u)
                            for h in range(2):
                                pe.wait_ge(*now(row_ready[h], i, u))
                                pe.wait_ge(*prev(col_act[h], i, u))
                                pe.wait_ge(*prev(col_dve[h], i, u))
                                for k in range(4):
                                    b = 4 * h + k
                                    o = ps[4 + 2 * h + k // 2][:, (k % 2) * ND:(k % 2) * ND + ND]
                                    nc.tensor.matmul(o, rf[u][:, b, 0:N], K("g2a"), start=True, stop=False)
                                    last = nc.tensor.matmul(o, rf[u][:, b, N:2 * N], K("g2b"), start=False, stop=True)
                                last.then_inc(col_ps[h][u], 1)
                    rows(0, 0)
                    with pe.Fori(0, T // 2 - 1) as i:
                        turn(i, False)
                    turn(T // 2 - 1, True)

                def copy_spectrum(eng, op, k, i, u, h, done):
                    eng.wait_ge(*now(col_ps[h], i, u))
                    o = spec[u][:, :].rearrange("s (c b j) -> s b c j", c=2, b=B)[:, 4 * h + 2 * k:4 * h + 2 * k + 2, :, :]
                    v = ps[4 + 2 * h + k][:, 0:2 * ND].rearrange("s (b c j) -> s b c j", b=2, c=2)
                    op(o, v).then_inc(done[h][u], 1)

                @block.scalar
                def _(act):
                    def rows(i, u):
                        for h in range(2):
                            act.wait_ge(*now(row_ps[h], i, u))
                            act.wait_ge(*prev2(col_ps[h], i, u))
                            for k in range(2):
                                b = 4 * h + k
                                last = nc.scalar.activation(rf[u][:, b, :], ps[2 * h][:, k * 256:k * 256 + 256], ACT.Copy,
                                                            scale=gn_scale[:, b:b + 1])
                            last.then_inc(row_act[h][u], 1)

                    def turn(i, last):
                        for u in range(2):
                            if not (last and u):
                                rows(i + u, 1 - u)
                            act.wait_ge(*prev2(stored, i, u, 32))
                            for h in range(2):
                                copy_spectrum(act, nc.scalar.copy, 0, i, u, h, col_act)
                            for h in range(2):
                                act.wait_ge(*now(col_act[h], i, u))
                                act.wait_ge(*now(col_dve[h], i, u))
                            for c in range(2):
                                act.dma_start(xs_d[:, c, bass.ds(2 * i + u, 1), :, :].rearrange("s t b j -> s (t b j)"),
                                              spec[u][:, c * B * NF:(c + 1) * B * NF]).then_inc(stored[u], 16)
                    rows(0, 0)
                    with act.Fori(0, T // 2 - 1) as i:
                        turn(i, False)
                    turn(T // 2 - 1, True)
                    for u in range(2):
                        act.wait_ge(stored[u], done(stored, T // 2, 32))

                @block.vector
                def _(dve):
                    def rows(i, u):
                        for h in range(2):
                            dve.wait_ge(*now(row_ps[h], i, u))
                            dve.wait_ge(*prev2(col_ps[h], i, u))
                            for k in range(2):
                                b = 4 * h + 2 + k
                                last = nc.vector.tensor_scalar(rf[u][:, b, :], ps[2 * h + 1][:, k * 256:k * 256 + 256],
                                                               gn_scale[:, b:b + 1], None, ALU.mult)
                            last.then_inc(row_dve[h][u], 1)
                        for h in range(2):
                            dve.wait_ge(*now(row_act[h], i, u))
                            dve.wait_ge(*now(row_dve[h], i, u))
                            dc = rf[u][:, 4 * h:4 * h + 4, 64:65]
                            nc.vector.tensor_tensor(dc, dc, gn_shift[:, 4 * h:4 * h + 4].rearrange("w (b o) -> w b o", o=1),
                                                    ALU.add).then_inc(row_ready[h][u], 1)

                    def turn(i, last):
                        for u in range(2):
                            if not (last and u):
                                rows(i + u, 1 - u)
                            dve.wait_ge(*prev2(stored, i, u, 32))
                            for h in range(2):
                                copy_spectrum(dve, nc.vector.tensor_copy, 1, i, u, h, col_dve)
                    rows(0, 0)
                    with dve.Fori(0, T // 2 - 1) as i:
                        turn(i, False)
                    turn(T // 2 - 1, True)
        end_stage()

        with ExitStack() as st:
            def sb(name, cols):
                return st.enter_context(nc.sbuf_tensor(name, [P, cols], F32))
            GJ = 13
            SLOTS = 4
            wt = [sb(f"s2_w{u}", T * 4 * NF) for u in range(2)]
            mov = [sb(f"s2_x{q}", 2 * 2 * B * NF) for q in range(SLOTS)]
            res = [sb(f"s2_d{u}", 2 * B * ND) for u in range(2)]
            wv = [w[:, :].rearrange("p (o q j) -> p q j o", q=4, j=NF) for w in wt]
            mv = [m[:, :].rearrange("p (f a n) -> p f a n", f=2, a=2) for m in mov]
            w_in, stored, x_in = sem("s2_w_in", 2), pool_dma_sem("s2_stored"), sem("s2_x_in", SLOTS)
            res_free = sem("s2_res_free", 2, 1)
            turned_re, turned_im = sem("s2_turned_re", SLOTS), sem("s2_turned_im", SLOTS)
            used = [sem(f"s2_used{q}", None, 1) for q in range(SLOTS - 1)] + [sem("s2_used3", 2, 1)]
            group_ps, copied = sem("s2_group_ps", 4), sem("s2_copied", 5, 1)
            cleared = sem("s2_cleared")
            NC = N // 8
            with nc.Block() as block:
                @block.sync
                def _(sp):
                    sp.wait_ge(cleared, SLOTS)
                    with sp.Fori(0, NC // 2) as i:
                        for u in range(2):
                            s0 = 16 * i + 8 * u
                            sp.wait_ge(*prev2(used[3], i, u))
                            for f in range(2):
                                for c, w in ((0, w_re), (1, w_im)):
                                    p0 = 64 * f + 32 * c
                                    sp.dma_start(wt[u][p0:p0 + 32, :].rearrange("i (o n) -> i o n", o=T),
                                                 w[:, :, bass.ds(s0 + 4 * f, 4), :].rearrange("i o s j -> i o (s j)")
                                                 ).then_inc(w_in[u], 16)
                            for q in range(4):
                                sp.wait_ge(*prev(used[q], i, u))
                                for f in range(2):
                                    sp.dma_start(mv[q][64 * f:64 * f + 64, f, 0, :],
                                                 xs_d[bass.ds(s0 + 4 * f + q, 1), :, :, :, :].rearrange("s c t b j -> (s c t) (b j)")
                                                 ).then_inc(x_in[q], 16)

                @block.gpsimd
                def _(pool):
                    free_all(pool)
                    for q in range(SLOTS):
                        nc.gpsimd.memset(mov[q][:, :], 0.0).then_inc(cleared, 1)
                    with pool.Fori(0, NC // 2) as i:
                        for u in range(2):
                            for g in range(5):
                                pool.wait_ge(*now(copied[g], i, u))
                            for f in range(2):
                                pool.dma_start(ds_d[bass.ds(16 * i + 8 * u + 4 * f, 4), :, :, :].rearrange("s o b n -> (s o) (b n)"),
                                               res[u][:, f * B * ND:(f + 1) * B * ND]).then_inc(stored[u], 16)
                            pool.wait_ge(*now(stored, i, u, 32))
                            pool.sem_inc(res_free[u], 1)

                @block.tensor
                def _(pe):
                    with pe.Fori(0, NC // 2) as i:
                        for u in range(2):
                            pe.wait_ge(*now(w_in, i, u, 64))
                            for q in range(4):
                                pe.wait_ge(x_in[q], 64 * i + 32 * (u + 1))
                                pe.wait_ge(turned_re[q], 4 * i + 2 * u + 2)
                                pe.wait_ge(turned_im[q], 4 * i + 2 * u + 2)
                                for g in range(5):
                                    if q == 0:
                                        pe.wait_ge(*prev(copied[g], i, u))
                                    for jj in range(GJ):
                                        j = g * GJ + jj
                                        last = nc.tensor.matmul(
                                            ps[g][32 * q:32 * q + 32, 32 * jj:32 * jj + 32], wv[u][:, q, j, :],
                                            mov[q][:, :].rearrange("p (n j) -> p j n", j=NF)[:, j, :], start=True, stop=True)
                                    if q == 3 and g < 4:
                                        last.then_inc(group_ps[g], 1)
                                last.then_inc(at(used[q], u), 1)

                def turn(eng, op, c, done, i, u):
                    sign = 1.0 if c == 0 else -1.0
                    for q in range(4):
                        eng.wait_ge(x_in[q], 64 * i + 32 * (u + 1))
                        for f in range(2):
                            p0, p1 = 64 * f + 32 * c, 64 * f + 32 * (1 - c)
                            op(mv[q][p0:p0 + 32, f, 1, :], mv[q][p1:p1 + 32, f, 0, :], sign).then_inc(done[q], 1)

                def copy_out(eng, op, mine, i, u):
                    eng.wait_ge(*prev2(res_free, i, u))
                    for g in mine:
                        if g < 4:
                            eng.wait_ge(*now(group_ps[g], i, u))
                        else:
                            eng.wait_ge(*now(used[3], i, u))
                        v = ps[g][:, 0:32 * GJ].rearrange("p (j f a b) -> p f a b j", f=2, a=2, b=B)
                        d = res[u][:, :].rearrange("p (f b n) -> p f b n", f=2, b=B)
                        both = res[u][:, :].rearrange("p (f b n) -> p f b n", f=2, b=B)[:, :, :, 1:129]                             .rearrange("p f b (a j) -> p f a b j", a=2)
                        lo, hi = g * GJ, min((g + 1) * GJ, NF - 1)
                        for f in range(2):
                            if g == 0:
                                op(d[:, f, :, 1:2], v[:, f, 0, :, 0:1])
                                op(d[:, f, :, 0:1], v[:, f, 1, :, 0:1])
                                lo = 1
                            if g == 4:
                                op(d[:, f, :, 65:66], v[:, f, 0, :, GJ - 1:GJ])
                                op(d[:, f, :, 129:130], v[:, f, 1, :, GJ - 1:GJ])
                            last = op(both[:, f, :, :, lo:hi], v[:, f, :, :, lo - g * GJ:hi - g * GJ])
                        last.then_inc(copied[g], 1)

                @block.scalar
                def _(act):
                    with act.Fori(0, NC // 2) as i:
                        for u in range(2):
                            turn(act, nc.scalar.mul, 0, turned_re, i, u)
                            copy_out(act, nc.scalar.copy, (0, 2), i, u)

                @block.vector
                def _(dve):
                    with dve.Fori(0, NC // 2) as i:
                        for u in range(2):
                            turn(dve, nc.vector.tensor_scalar_mul, 1, turned_im, i, u)
                            copy_out(dve, nc.vector.tensor_copy, (1, 3, 4), i, u)
        end_stage()

        with ExitStack() as st:
            def sb(name, cols):
                return st.enter_context(nc.sbuf_tensor(name, [P, cols], F32))
            gn2_scale, gn2_shift = keep("gn2_scale", B * 32), keep("gn2_shift", B * 32)
            xin = [sb(f"s3_x{u}", CW) for u in range(2)]
            sp_in = [sb(f"s3_d{u}", B * ND) for u in range(2)]
            sp_neg = [sb(f"s3_n{u}", B * N) for u in range(2)]
            half = [[sb(f"s3_h{u}{h}", 4 * N) for h in range(2)] for u in range(2)]
            x1 = [sb(f"s3_x1_{u}", CW) for u in range(2)]
            sq, zero = sb("s3_sq", CW), sb("s3_zero", 1)
            zero_ready = sem("s3_zero_ready")
            acc, acq = sb("s3_sum", CW), sb("s3_sumsq", CW)
            grp, tmp = sb("s3_grp", 512), sb("s3_tmp", 256)
            x_in, d_in, negated, stored = sem("s3_x_in", 2), sem("s3_d_in", 2), sem("s3_negated", 2), sem("s3_stored", 2, 16)
            col_ps, col_sb, row_ps, added = ([sem(f"s3_{n}{h}_", 2, 1) for h in range(2)] for n in ("col_ps", "col_sb", "row_ps", "added"))
            squared, summed, sqsummed = (sem("s3_" + n, None, 1) for n in ("squared", "summed", "sqsummed"))
            zeroed, tot_ps, lk, var_ready, root_ready = (sem("s3_" + n) for n in ("zeroed", "tot_ps", "link", "var_ready", "root_ready"))
            with nc.Block() as block:
                @block.sync
                def _(sp):
                    def load_spectrum(i, u):
                        sp.wait_ge(*prev2(col_ps[1], i, u))
                        sp.dma_start(sp_in[u][:, :], ds_d[:, bass.ds(2 * i + u, 1), :, :].rearrange("s o b n -> s (o b n)")
                                     ).then_inc(d_in[u], 16)

                    def turn(i, last):
                        for u in range(2):
                            if not (last and u):
                                load_spectrum(i + u, 1 - u)
                            sp.wait_ge(*prev2(added[1], i, u))
                            sp.dma_start(xin[u][:, :], channel_of(x, 2 * i + u)).then_inc(x_in[u], 16)
                    load_spectrum(0, 0)
                    with sp.Fori(0, T // 2 - 1) as i:
                        turn(i, False)
                    turn(T // 2 - 1, True)

                @block.gpsimd
                def _(pool):
                    def negate(i, u):
                        pool.wait_ge(*now(d_in, i, u, 16))
                        pool.wait_ge(*prev2(col_ps[1], i, u))
                        d = sp_in[u][:, :].rearrange("s (b n) -> s b n", b=B)
                        n = sp_neg[u][:, :].rearrange("s (b n) -> s b n", b=B)
                        for dst, src, op in ((n[:, :, 0:1], d[:, :, 0:1], ALU.subtract), (n[:, :, 1:65], d[:, :, 66:130], ALU.subtract),
                                             (n[:, :, 65:128], d[:, :, 2:65], ALU.add)):
                            zeros = zero[:, :].unsqueeze(1).broadcast_to([P, B, dst.shape[2]])
                            nc.gpsimd.tensor_tensor(dst, zeros, src, op).then_inc(negated[u], 1)

                    free_all(pool)
                    nc.gpsimd.memset(zero[:, :], 0.0).then_inc(zero_ready, 1)
                    pool.wait_ge(zero_ready, 1)
                    with pool.Fori(0, T // 2) as i:
                        for u in range(2):
                            negate(i, u)

                @block.tensor
                def _(pe):
                    def cols(i, u):
                        pe.wait_ge(*now(d_in, i, u, 16))
                        pe.wait_ge(*now(negated, i, u, 3))
                        d = sp_in[u][:, :].rearrange("s (b n) -> s b n", b=B)
                        n = sp_neg[u][:, :].rearrange("s (b n) -> s b n", b=B)
                        for h in range(2):
                            pe.wait_ge(*prev2(col_sb[h], i, u))
                            for k in range(4):
                                o = ps[2 * u + h][:, k * N:(k + 1) * N]
                                nc.tensor.matmul(o, d[:, 4 * h + k, 1:129], K("cos0"), start=True, stop=False)
                                last = nc.tensor.matmul(o, n[:, 4 * h + k, :], K("sin0"), start=False, stop=True)
                            last.then_inc(col_ps[h][u], 1)

                    def turn(i, last_turn):
                        for u in range(2):
                            if not (last_turn and u):
                                cols(i + u, 1 - u)
                            for h in range(2):
                                pe.wait_ge(*now(col_sb[h], i, u))
                                pe.wait_ge(*prev2(added[h], i, u))
                                for k in range(4):
                                    last = nc.tensor.matmul(ps[4 + 2 * u + h][:, k * N:(k + 1) * N],
                                                            half[u][h][:, k * N:(k + 1) * N], K("k0"), start=True, stop=True)
                                last.then_inc(row_ps[h][u], 1)
                    cols(0, 0)
                    with pe.Fori(0, T // 2 - 1) as i:
                        turn(i, False)
                    turn(T // 2 - 1, True)
                    for h in range(2):
                        pe.wait_ge(added[h][0], done(added[h], T // 2))
                        pe.wait_ge(added[h][1], done(added[h], T // 2))
                    pe.wait_ge(summed, done(summed, T))
                    pe.wait_ge(sqsummed, done(sqsummed, T))
                    for k in range(2):
                        nc.tensor.matmul(ps[4 + k][:, :], K("ones"), acc[:, k * 512:(k + 1) * 512], start=True, stop=True)
                        last = nc.tensor.matmul(ps[6 + k][:, :], K("ones"), acq[:, k * 512:(k + 1) * 512], start=True, stop=True)
                    last.then_inc(tot_ps, 1)

                @block.scalar
                def _(act):
                    def halves(i, u):
                        for h in range(2):
                            act.wait_ge(*now(col_ps[h], i, u))
                            act.wait_ge(*prev2(row_ps[h], i, u))
                            nc.scalar.copy(half[u][h][:, :], ps[2 * u + h][:, :]).then_inc(col_sb[h][u], 1)

                    def turn(i, last):
                        for u in range(2):
                            if not (last and u):
                                halves(i + u, 1 - u)
                            for h in range(2):
                                act.wait_ge(*now(added[h], i, u))
                            act.dma_start(laid_channel(x1_d, 2 * i + u), x1[u][:, :]).then_inc(stored[u], 16)
                            act.wait_ge(*prev(sqsummed, i, u))
                            nc.scalar.activation(sq[:, :], x1[u][:, :], ACT.Square).then_inc(squared, 1)
                    halves(0, 0)
                    with act.Fori(0, T // 2 - 1) as i:
                        turn(i, False)
                    turn(T // 2 - 1, True)
                    for u in range(2):
                        act.wait_ge(stored[u], done(stored, T // 2, 16))
                    act.wait_ge(var_ready, 1)
                    nc.scalar.activation(gn2_scale[:, :], grp[:, 256:512], ACT.Sqrt).then_inc(root_ready, 1)

                @block.vector
                def _(dve):
                    nc.vector.memset(acc[:, :], 0.0).then_inc(zeroed, 1)
                    nc.vector.memset(acq[:, :], 0.0).then_inc(zeroed, 1)
                    dve.wait_ge(zeroed, 2)
                    with dve.Fori(0, T // 2) as i:
                        for u in range(2):
                            dve.wait_ge(*now(x_in, i, u, 16))
                            dve.wait_ge(*prev2(stored, i, u, 16))
                            for h in range(2):
                                dve.wait_ge(*now(row_ps[h], i, u))
                                nc.vector.tensor_tensor(x1[u][:, 512 * h:512 * h + 512], ps[4 + 2 * u + h][:, :],
                                                        xin[u][:, 512 * h:512 * h + 512], ALU.add).then_inc(added[h][u], 1)
                            for h in range(2):
                                dve.wait_ge(*now(added[h], i, u))
                            dve.wait_ge(*prev(summed, i, u))
                            nc.vector.tensor_tensor(acc[:, :], acc[:, :], x1[u][:, :], ALU.add).then_inc(summed, 1)
                            dve.wait_ge(*now(squared, i, u))
                            dve.wait_ge(*prev(sqsummed, i, u))
                            nc.vector.tensor_tensor(acq[:, :], acq[:, :], sq[:, :], ALU.add).then_inc(sqsummed, 1)
                    link = linker(dve, lk)
                    dve.wait_ge(tot_ps, 1)
                    for k in range(2):
                        for q, c0 in ((4, 0), (6, 256)):
                            link(nc.vector.tensor_reduce(grp[:, c0 + 128 * k:c0 + 128 * k + 128],
                                                         ps[q + k][:, :].rearrange("p (g j) -> p g j", j=GRP), AX.X, ALU.add))
                    link(nc.vector.tensor_scalar_mul(grp[:, :], grp[:, :], 1.0 / PERGRP))
                    mean, var = grp[:, 0:256], grp[:, 256:512]
                    link(nc.vector.tensor_tensor(tmp[:, :], mean, mean, ALU.mult))
                    link(nc.vector.tensor_tensor(var, var, tmp[:, :], ALU.subtract))
                    inv_std(dve, link, var, gn2_scale[:, :], tmp[:, :], var_ready, root_ready, 1)
                    link(nc.vector.tensor_tensor(gn2_shift[:, :], mean, gn2_scale[:, :], ALU.mult))
                    link(nc.vector.tensor_scalar_mul(gn2_shift[:, :], gn2_shift[:, :], -1.0))
        end_stage()

        spec_u = keep("spec_u", MF * NIMG)
        spec_o = keep("spec_o", MF * NIMG)
        scratch = keep("scratch", 3 * JT * NIMG)
        probs_t = scratch[:, 0:NIMG * NH // 4]
        img_sum, img_sumsq = keep("img_sum", NIMG), keep("img_sumsq", NIMG)
        small = keep("small", wat["q_r"][0])
        def W(name, tile, base):
            a, n = wat[name]
            return tile[:, a - base:a - base + n]

        def SM(name):
            return W(name, small, 0)
        mix_t, mix_const = keep("mix_t", 2 * P), keep("mix_const", 2)
        turned = ExitStack()
        spec_v = turned.enter_context(nc.sbuf_tensor("spec_v", [P, MF * NIMG], F32))
        NT = NIMG // CH // 2

        def per_image(tile, i, u, lo=0, hi=B):
            return tile.rearrange("p (b t) -> p t b", t=T)[:, bass.ds(2 * i + u, 1), lo:hi].rearrange("p o b -> p (o b)")

        def images(tile, i, u, lo=0, hi=B):
            return tile.rearrange("p (f b t) -> p t b f", b=B, t=T)[:, bass.ds(2 * i + u, 1), lo:hi, :].rearrange("p o b f -> p (o b) f")

        def forward_rows(pe, i, u, h, tile, row_ps, row_sb):
            for free in row_sb[h]:
                pe.wait_ge(*prev(free, i, u))
            for k in range(4):
                last = nc.tensor.matmul(ps[2 * h + k // 2][:, (k % 2) * 256:(k % 2) * 256 + 256],
                                        tile[:, (4 * h + k) * N:(4 * h + k + 1) * N], K("f1"), start=True, stop=True)
            last.then_inc(row_ps[h][u], 1)

        def forward_cols(pe, i, u, h, rf, row_sb, col_ps, col_free):
            for here in row_sb[h]:
                pe.wait_ge(*now(here, i, u))
            pe.wait_ge(*prev(col_free[h], i, u))
            for k in range(4):
                o = ps[4 + h][:, k * 2 * MF:(k + 1) * 2 * MF]
                nc.tensor.matmul(o, rf[:, 4 * h + k, 0:N], K("ga"), start=True, stop=False)
                last = nc.tensor.matmul(o, rf[:, 4 * h + k, N:2 * N], K("gb"), start=False, stop=True)
            last.then_inc(col_ps[h][u], 1)

        def copy_rows(eng, op, k, i, u, h, rf, row_ps, row_sb, col_ps):
            eng.wait_ge(*now(row_ps[h], i, u))
            eng.wait_ge(*prev2(col_ps[h], i, u))
            op(rf[:, 4 * h + 2 * k:4 * h + 2 * k + 2, :], ps[2 * h + k][:, :].rearrange("w (n r) -> w n r", n=2)
               ).then_inc(row_sb[h][k], 1)

        with ExitStack() as st:
            def sb(name, cols):
                return st.enter_context(nc.sbuf_tensor(name, [P, cols], F32))
            xin = [sb(f"s4_x{u}", CW) for u in range(2)]
            g = [sb(f"s4_g{u}", CW) for u in range(2)]
            sq = sb("s4_sq", CW)
            rf = [sb(f"s4_rowft{u}", CH * 2 * N)[:, :].rearrange("w (n r) -> w n r", n=CH) for u in range(2)]
            x_in, scaled, stored = sem("s4_x_in", 2), sem("s4_scaled", 2, 1), sem("s4_stored", 2, 16)
            g_ready, squared, reduced = sem("s4_g_ready"), sem("s4_squared"), sem("s4_reduced", None, 1)
            row_ps, col_ps = ([sem(f"s4_{n}{h}_", 2, s) for h in range(2)] for n, s in (("row_ps", 0), ("col_ps", 1)))
            row_sb = [sem(f"s4_row_sb{h}_", 2, 1) for h in range(2)]
            col_sb = sem("s4_col_sb", 2, 1)
            small_in = sem("s4_small_in")

            with nc.Block() as block:
                @block.sync
                def _(sp):
                    sp.dma_start(small[:, :], weights[:, 0:wat["q_r"][0]]).then_inc(small_in, 16)
                    with sp.Fori(0, NT) as i:
                        for u in range(2):
                            sp.wait_ge(*prev2(scaled, i, u))
                            sp.dma_start(xin[u][:, :], laid_channel(x1_d, 2 * i + u)).then_inc(x_in[u], 16)
                    sp.wait_ge(small_in, 16)

                @block.gpsimd
                def _(pool):
                    free_all(pool)
                    with pool.Fori(0, NT) as i:
                        for u in range(2):
                            pool.wait_ge(*now(scaled, i, u))
                            gv = g[u][:, :].rearrange("y (m j) -> y m j", j=GRP)
                            sh = gn2_shift[:, :].unsqueeze(2).broadcast_to([P, B * 32, GRP])
                            nc.gpsimd.tensor_tensor(gv, gv, sh, ALU.add).then_inc(g_ready, 1)

                @block.tensor
                def _(pe):
                    def rows(i, u):
                        pe.wait_ge(*now(g_ready, i, u))
                        for h in range(2):
                            forward_rows(pe, i, u, h, g[u], row_ps, row_sb)

                    def turn(i, last):
                        for u in range(2):
                            if not (last and u):
                                rows(i + u, 1 - u)
                            for h in range(2):
                                forward_cols(pe, i, u, h, rf[u], row_sb, col_ps, col_sb)
                    rows(0, 0)
                    with pe.Fori(0, NT - 1) as i:
                        turn(i, False)
                    turn(NT - 1, True)

                def copy_cols(eng, op, i, u, h):
                    eng.wait_ge(*now(col_ps[h], i, u))
                    v = ps[4 + h][:, 0:8 * MF].rearrange("r (n a f) -> r a n f", n=4, a=2)
                    op(images(spec_u[:, :], i, u, 4 * h, 4 * h + 4), v[:, 0])
                    op(images(spec_v[:, :], i, u, 4 * h, 4 * h + 4), v[:, 1]).then_inc(col_sb[h], 1)

                @block.scalar
                def _(act):
                    def store(i, u):
                        act.wait_ge(*now(g_ready, i, u))
                        act.dma_start(channel_of(g_d, 2 * i + u), g[u][:, :]).then_inc(stored[u], 16)

                    def rows(i, u):
                        for h in range(2):
                            copy_rows(act, nc.scalar.copy, 0, i, u, h, rf[u], row_ps, row_sb, col_ps)

                    def square(i, u):
                        act.wait_ge(*prev(reduced, i, u))
                        nc.scalar.activation(sq[:, :], g[u][:, :], ACT.Square).then_inc(squared, 1)

                    def turn(i, last):
                        for u in range(2):
                            if not (last and u):
                                store(i + u, 1 - u)
                                rows(i + u, 1 - u)
                                square(i + u, 1 - u)
                            copy_cols(act, nc.scalar.copy, i, u, 0)
                    store(0, 0)
                    rows(0, 0)
                    square(0, 0)
                    with act.Fori(0, NT - 1) as i:
                        turn(i, False)
                    turn(NT - 1, True)
                    for u in range(2):
                        act.wait_ge(stored[u], done(stored, NT, 16))

                @block.vector
                def _(dve):
                    def scale(i, u):
                        dve.wait_ge(*now(x_in, i, u, 16))
                        dve.wait_ge(*prev2(stored, i, u, 16))
                        by_group = lambda t: t[:, :].rearrange("y (m j) -> y m j", j=GRP)
                        nc.vector.tensor_tensor(by_group(g[u]), by_group(xin[u]), gn2_scale[:, :].unsqueeze(2).broadcast_to([P, B * 32, GRP]),
                                                ALU.mult).then_inc(scaled[u], 1)

                    def rows(i, u):
                        for h in range(2):
                            copy_rows(dve, nc.vector.tensor_copy, 1, i, u, h, rf[u], row_ps, row_sb, col_ps)

                    def turn(i, last):
                        for u in range(2):
                            dve.wait_ge(*now(squared, i, u))
                            nc.vector.tensor_reduce(per_image(img_sumsq[:, :], i, u), sq[:, :].rearrange("y (n w) -> y n w", n=CH), AX.X,
                                                    ALU.add).then_inc(reduced, 1)
                            if not last:
                                dve.wait_ge(*now(reduced, i, u))
                                scale(i + 1, u)
                            if not (last and u):
                                rows(i + u, 1 - u)
                            copy_cols(dve, nc.vector.tensor_copy, i, u, 1)
                    scale(0, 0)
                    scale(0, 1)
                    rows(0, 0)
                    with dve.Fori(0, NT - 1) as i:
                        turn(i, False)
                    turn(NT - 1, True)
        end_stage()

        with ExitStack() as st:
            def sb(name, cols):
                return st.enter_context(nc.sbuf_tensor(name, [P, cols], F32))
            qk_base, qk_end = wat["q_r"][0], wat["v_r"][0]
            qk = sb("s5_qk", qk_end - qk_base)
            def QK(name):
                return W(name, qk, qk_base)
            NJ = NH * JT
            sym_r, sym_i, g_r, g_i, tmp = (sb("s5_" + n, NJ) for n in ("sym_r", "sym_i", "g_r", "g_i", "tmp"))
            mean, ex2, r, r_tmp = (sb("s5_" + n, NIMG + 2) for n in ("mean", "ex2", "r", "r_tmp"))
            low_u, low_v = sb("s5_low_u", JT * NIMG), sb("s5_low_v", JT * NIMG)
            JI = JT * NIMG
            part = [scratch[:, 0:JI], sb("s5_part1", JI)[:, :]]
            prod = [scratch[:, JI:2 * JI], scratch[:, 2 * JI:3 * JI]]
            scores = sb("s5_scores", 2 * NH * 32)
            common = sb("s5_common", 64)
            red = sb("s5_red", 64)
            vecn = sb("s5_vecn", NH)
            vec = sb("s5_vec", 8)
            qk_in, stat_ps, var_ready, root_ready, lk, lkp, v_done, u_done = (
                sem("s5_" + n) for n in ("qk_in", "stat_ps", "var_ready", "root_ready", "link", "linkp", "v_done", "u_done"))
            packed, sym_ps, weighted, common_ps, part_ready, root2 = (
                sem("s5_" + n) for n in ("packed", "sym_ps", "weighted", "common_ps", "part_ready", "root2"))
            prod_ready, score_ps, taken = sem("s5_prod_ready", 2, 1), sem("s5_score_ps", 2, 1), sem("s5_taken", 2, 1)
            shifted, exped, mix_ready, mix_ps, g_done = (sem("s5_" + n) for n in ("shifted", "exped", "mix_ready", "mix_ps", "g_done"))
            u_saved, means_in = sem("s5_u_saved"), sem("s5_means_in")
            TU = NH // 2
            U3, V3, O3 = (t[:, :].rearrange("p (f n) -> p f n", f=MF) for t in (spec_u, spec_v, spec_o))
            LU3, LV3 = (t[:, :].rearrange("p (f n) -> p f n", f=JT) for t in (low_u, low_v))
            with nc.Block() as block:
                @block.sync
                def _(sp):
                    sp.dma_start(u_d, spec_u[:, :]).then_inc(u_saved, 16)
                    sp.dma_start(qk[:, :], weights[:, qk_base:qk_end]).then_inc(qk_in, 16)

                @block.tensor
                def _(pe):
                    pe.wait_ge(means_in, 1)
                    nc.tensor.matmul(ps[0][:, 0:NIMG], K("ones"), img_sum[:, :], start=True, stop=True)
                    nc.tensor.matmul(ps[0][:, NIMG:2 * NIMG], K("ones"), img_sumsq[:, :], start=True, stop=True)
                    for gb in range(2):
                        for k, s in ((0, img_sum), (2, img_sumsq)):
                            last = nc.tensor.matmul(ps[1][:, k + gb:k + gb + 1], s[:, gb * P:(gb + 1) * P],
                                                    K("ones")[:, 0:1], start=True, stop=True)
                    last.then_inc(stat_ps, 1)
                    pe.wait_ge(u_done, 1)
                    nc.tensor.matmul(ps[2][:, 0:NIMG], K("sym"), U3[:, 32, :], start=True, stop=True).then_inc(sym_ps, 1)
                    pe.wait_ge(weighted, 1)
                    for gb in range(2):
                        for f in range(MF):
                            for b in range(4):
                                c = slice(gb * P + 32 * b, gb * P + 32 * b + 32)
                                last = nc.tensor.matmul(ps[3][32 * b:32 * b + 32, 32 * gb:32 * gb + 32], O3[:, f, c], U3[:, f, c],
                                                        start=(f == 0), stop=(f == MF - 1))
                    last.then_inc(common_ps, 1)
                    pe.wait_ge(packed, 1)
                    with pe.Fori(0, TU) as i:
                        for u in range(2):
                            pe.wait_ge(*now(prod_ready, i, u))
                            pe.wait_ge(*prev2(taken, i, u))
                            pr = prod[u].rearrange("p (f n) -> p f n", f=JT)
                            for gb in range(2):
                                for j in range(JT):
                                    for b in range(4):
                                        c = slice(gb * P + 32 * b, gb * P + 32 * b + 32)
                                        last = nc.tensor.matmul(ps[4 + u][32 * b:32 * b + 32, 32 * gb:32 * gb + 32], pr[:, j, c],
                                                                LU3[:, j, c], start=(j == 0), stop=(j == JT - 1))
                            last.then_inc(score_ps[u], 1)
                    pe.wait_ge(mix_ready, 1)
                    for gb in range(2):
                        last = nc.tensor.matmul(ps[6][:, gb:gb + 1], mix_t[:, gb * P:(gb + 1) * P], vec[:, gb:gb + 1],
                                                start=True, stop=True)
                    last.then_inc(mix_ps, 1)

                @block.scalar
                def _(act):
                    act.wait_ge(var_ready, 1)
                    nc.scalar.activation(r[:, :], ex2[:, :], ACT.Sqrt).then_inc(root_ready, 1)
                    act.wait_ge(v_done, 1)
                    act.wait_ge(u_done, 1)
                    for dst, src in ((LU3, U3), (LV3, V3)):
                        nc.scalar.copy(dst[0:64, :, :], src[0:64, 0:17:2, :])
                        last = nc.scalar.copy(dst[64:128, 0:8, :], src[0:64, 1:17:2, :])
                    last.then_inc(packed, 2)
                    act.wait_ge(packed, 2)
                    act.wait_ge(g_done, 1)
                    with act.Fori(0, TU) as i:
                        for u in range(2):
                            act.wait_ge(*prev2(prod_ready, i, u))
                            for j in range(JT):
                                last = nc.scalar.activation(part[u][:, j * NIMG:(j + 1) * NIMG], LU3[:, j, :], ACT.Copy,
                                                            scale=g_r[:, bass.ds((2 * i + u) * JT + j, 1)])
                            last.then_inc(part_ready, 1)
                    act.wait_ge(shifted, 1)
                    nc.scalar.activation(scores[:, :], scores[:, :], ACT.Exp).then_inc(exped, 1)

                @block.gpsimd
                def _(pool):
                    free_all(pool)
                    link = linker(pool, lkp)
                    link(nc.gpsimd.memset(LU3[64:128, 8, :], 0.0))
                    link(nc.gpsimd.memset(LV3[64:128, 8, :], 0.0))
                    pool.wait_ge(root2, 1)
                    rb = r[:, 0:NIMG].unsqueeze(1).broadcast_to([P, MF, NIMG])
                    link(nc.gpsimd.tensor_tensor(V3, V3, rb, ALU.mult))
                    link(nc.gpsimd.memset(V3[0:1, 0, :], 0.0))
                    link(nc.gpsimd.tensor_scalar(V3[32:33, 0, :], V3[32:33, 0, :], 0.0, SM("norm1_b")[32:33, :], ALU.mult, ALU.add))
                    pool.sem_inc(v_done, 1)

                @block.vector
                def _(dve):
                    link = linker(dve, lk)
                    tt, ts = nc.vector.tensor_tensor, nc.vector.tensor_scalar
                    link(nc.vector.memset(img_sum[:, :], 0.0))
                    nc.vector.tensor_scalar_mul(img_sum[0:1, :], spec_u[0:1, 0:NIMG], float(PIX)).then_inc(means_in, 1)
                    dve.wait_ge(stat_ps, 1)
                    link(ts(mean[:, 0:NIMG], ps[0][:, 0:NIMG], 1.0 / PIX, None, ALU.mult))
                    link(ts(ex2[:, 0:NIMG], ps[0][:, NIMG:2 * NIMG], 1.0 / PIX, None, ALU.mult))
                    link(ts(mean[:, NIMG:NIMG + 2], ps[1][:, 0:2], 1.0 / PIX, None, ALU.mult))
                    link(ts(ex2[:, NIMG:NIMG + 2], ps[1][:, 2:4], 1.0 / PIX, None, ALU.mult))
                    link(tt(r_tmp[:, :], mean[:, :], mean[:, :], ALU.mult))
                    link(tt(ex2[:, :], ex2[:, :], r_tmp[:, :], ALU.subtract))
                    inv_std(dve, link, ex2[:, :], r[:, :], r_tmp[:, :], var_ready, root_ready, 1)
                    link(ts(r[:, :], r[:, :], SM("norm1_w"), None, ALU.mult))
                    dve.sem_inc(root2, 1)
                    rb = r[:, 0:NIMG].unsqueeze(1).broadcast_to([P, MF, NIMG])
                    dve.wait_ge(u_saved, 16)
                    link(tt(U3, U3, rb, ALU.mult))
                    link(ts(U3[0:1, 0, :], U3[0:1, 0, :], 0.0, SM("norm1_b")[0:1, :], ALU.mult, ALU.add))
                    link(nc.vector.memset(U3[32:33, 0, :], 0.0))
                    dve.sem_inc(u_done, 1)
                    link(tt(O3[:, 0:32, :], U3[:, 0:32, :], K("wt")[:, 0:32].unsqueeze(2).broadcast_to([P, 32, NIMG]), ALU.mult))
                    dve.wait_ge(sym_ps, 1)
                    link(nc.vector.tensor_copy(O3[:, 32, :], ps[2][:, 0:NIMG]))
                    dve.sem_inc(weighted, 1)
                    dve.wait_ge(qk_in, 16)
                    v3 = lambda t: t.rearrange("p (n j) -> p n j", j=JT)
                    bc = lambda name: SM(name).unsqueeze(2).broadcast_to([P, NH, JT])
                    for c, dst, op in (("r", sym_r, ALU.add), ("i", sym_i, ALU.subtract)):
                        link(nc.vector.tensor_copy(dst[:, :], QK("q_" + c)))
                        z = v3(dst[:, :])[0:64, :, 0:1]
                        link(tt(z, z, QK("qrev_" + c)[0:64, :].unsqueeze(2), op))
                        link(ts(z, z, 0.5, None, ALU.mult))
                    link(tt(v3(sym_r[:, :]), v3(sym_r[:, :]), bc("Qsw"), ALU.add))
                    link(tt(g_r[:, :], sym_r[:, :], QK("k_r"), ALU.mult))
                    link(tt(tmp[:, :], sym_i[:, :], QK("k_i"), ALU.mult))
                    link(tt(g_r[:, :], g_r[:, :], tmp[:, :], ALU.add))
                    link(tt(v3(tmp[:, :]), v3(QK("q_r")), bc("Qsw"), ALU.add))
                    link(tt(v3(tmp[:, :]), v3(tmp[:, :]), bc("Ksw"), ALU.mult))
                    link(tt(g_r[:, :], g_r[:, :], tmp[:, :], ALU.add))
                    link(tt(g_i[:, :], sym_i[:, :], QK("k_r"), ALU.mult))
                    link(tt(tmp[:, :], sym_r[:, :], QK("k_i"), ALU.mult))
                    link(tt(g_i[:, :], g_i[:, :], tmp[:, :], ALU.subtract))
                    link(tt(v3(tmp[:, :]), v3(QK("q_i")), bc("Ksw"), ALU.mult))
                    link(tt(g_i[:, :], g_i[:, :], tmp[:, :], ALU.add))
                    lw = K("lw").unsqueeze(1).broadcast_to([P, NH, JT])
                    link(tt(v3(g_r[:, :]), v3(g_r[:, :]), lw, ALU.mult))
                    link(tt(v3(g_i[:, :]), v3(g_i[:, :]), lw, ALU.mult))
                    dve.sem_inc(g_done, 1)
                    dve.wait_ge(common_ps, 1)
                    link(nc.vector.tensor_copy(common[:, :], ps[3][:, 0:64]))
                    dve.wait_ge(packed, 2)
                    sc4 = scores[:, :].rearrange("p (g n s) -> p g n s", g=2, n=NH)

                    def take(i, u):
                        dve.wait_ge(*now(score_ps, i, u))
                        nc.vector.tensor_copy(sc4[:, :, bass.ds(2 * i + u, 1), :].rearrange("p g o s -> p g (o s)"),
                                              ps[4 + u][:, 0:64].rearrange("p (g s) -> p g s", g=2)).then_inc(taken[u], 1)

                    def head_step(i, u, first):
                        dve.wait_ge(*now(part_ready, i, u))
                        dve.wait_ge(*prev2(score_ps, i, u))
                        for j in range(JT):
                            c = slice(j * NIMG, (j + 1) * NIMG)
                            last = nc.vector.scalar_tensor_tensor(
                                prod[u][:, c], LV3[:, j, :], g_i[:, bass.ds((2 * i + u) * JT + j, 1)],
                                part[u][:, c], ALU.mult, ALU.add)
                        last.then_inc(prod_ready[u], 1)
                        if not first:
                            take(i - 1 + u, 1 - u)
                    head_step(0, 0, True)
                    head_step(0, 1, False)
                    with dve.Fori(1, TU) as i:
                        for u in range(2):
                            head_step(i, u, False)
                    take(TU - 1, 1)
                    for u in range(2):
                        dve.wait_ge(taken[u], done(taken, TU))
                    big = low_u[:, 0:2 * NH * 32]
                    big4 = big.rearrange("p (g n s) -> p g n s", g=2, n=NH)
                    com = common[:, :].rearrange("p (g s) -> p g s", g=2)
                    link(tt(vecn[:, :], SM("Qsw"), SM("Ksw"), ALU.mult))
                    for gb in range(2):
                        link(tt(big4[:, gb], com[:, gb:gb + 1, :].broadcast_to([P, NH, 32]),
                                vecn[:, :].unsqueeze(2).broadcast_to([P, NH, 32]), ALU.mult))
                    link(tt(scores[:, :], scores[:, :], big, ALU.add))
                    s3 = scores[:, :].rearrange("p (m s) -> p m s", s=32)
                    rd = red[:, :].unsqueeze(2).broadcast_to([P, 64, 32])
                    link(nc.vector.tensor_reduce(red[:, :], s3, AX.X, ALU.max))
                    link(tt(s3, s3, rd, ALU.subtract))
                    dve.sem_inc(shifted, 1)
                    dve.wait_ge(exped, 1)
                    link(nc.vector.tensor_reduce(red[:, :], s3, AX.X, ALU.add))
                    link(nc.vector.reciprocal(red[:, :], red[:, :]))
                    link(tt(s3, s3, rd, ALU.mult))
                    link(nc.vector.transpose(big, scores[:, :]))
                    for b in range(4):
                        for q in range(4):
                            link(nc.vector.tensor_copy(
                                probs_t[32 * q:32 * q + 32, :].rearrange("p (g b m) -> p g b m", g=2, b=4)[:, :, b, :],
                                big[32 * b:32 * b + 32, :].rearrange("p (g q m) -> p g q m", g=2, q=4)[:, :, q, :]))
                    link(tt(vecn[:, :], SM("Psw"), SM("Vsw"), ALU.mult))
                    for gb in range(2):
                        link(tt(big4[:, gb], sc4[:, gb], vecn[:, :].unsqueeze(2).broadcast_to([P, NH, 32]), ALU.mult))
                    link(nc.vector.tensor_reduce(red[:, :], big.rearrange("p (g n s) -> p g s n", g=2, n=NH), AX.X, ALU.add))
                    link(nc.vector.transpose(common[:, :], red[:, :]))
                    link(nc.vector.memset(mix_t[:, :], 0.0))
                    for b in range(4):
                        q = slice(32 * b, 32 * b + 32)
                        link(nc.vector.tensor_copy(mix_t[:, :].rearrange("p (g c) -> p g c", g=2)[q, :, q],
                                                   common[q, :].rearrange("p (g t) -> p g t", g=2)))
                    link(tt(vec[:, 0:2], r[:, NIMG:NIMG + 2], mean[:, NIMG:NIMG + 2], ALU.mult))
                    link(ts(vec[:, 0:2], vec[:, 0:2], -1.0, SM("norm1_b"), ALU.mult, ALU.add))
                    dve.sem_inc(mix_ready, 1)
                    dve.wait_ge(mix_ps, 1)
                    link(nc.vector.tensor_copy(mix_const[:, :], ps[6][:, 0:2]))
                    for gb in range(2):
                        m = mix_t[:, gb * P:(gb + 1) * P]
                        link(nc.vector.scalar_tensor_tensor(m, m, r[:, NIMG + gb:NIMG + gb + 1], K("ident"), ALU.mult, ALU.add))
        turned.close()
        end_stage()

        with ExitStack() as st:
            def sb(name, cols):
                return st.enter_context(nc.sbuf_tensor(name, [P, cols], F32))
            NM = MF * NH
            hx = sb("s6_hx", 2 * NH * P)
            vp_base = wat["v_r"][0]
            vp_cols = weights.shape[1] - vp_base
            vp = hx[:, 0:vp_cols]

            def VP(name):
                a, n = wat[name]
                return hx[:, a - vp_base:a - vp_base + n]
            diag = [sb(f"s6_diag{u}", NH * 64) for u in range(2)]
            h_r, h_i = diag[0][:, 0:NM], diag[1][:, 0:NM]
            tmp = sb("s6_tmp", NM)[:, :]
            coef = sb("s6_coef", 2 * NM)
            col = [sb(f"s6_col{u}", 2 * NIMG) for u in range(2)]
            vp_in, lk, coef_ready = sem("s6_vp_in"), sem("s6_link"), sem("s6_coef_ready")
            flat = [sb(f"s6_flat{g}", P) for g in range(2)]
            ready = sem("s6_ready", 2)
            bank_ps, bank_sb = sem("s6_bank_ps", 4), sem("s6_bank_sb", 4, 1)
            out_ps, flat_sb, turned_ps, spec_sb = (sem("s6_" + n, 2, 1) for n in ("out_ps", "flat_sb", "turned_ps", "spec_sb"))
            U3, O3 = (t[:, :].rearrange("p (f n) -> p f n", f=MF) for t in (spec_u, spec_o))
            hx5 = hx[:, :].rearrange("p (b n h c) -> p b n h c", b=B, n=8, h=2)
            FT = MF // 2

            def uses(i, u, g, k):
                return 8 * i + 4 * u + 2 * g + k

            with nc.Block() as block:
                @block.sync
                def _(sp):
                    sp.dma_start(vp, weights[:, vp_base:vp_base + vp_cols]).then_inc(vp_in, 16)

                @block.gpsimd
                def _(pool):
                    free_all(pool)

                @block.tensor
                def _(pe):
                    def apply_h(i, u, g):
                        pe.wait_ge(*now(ready, i, u, 4))
                        for b in range(4):
                            for half in range(2):
                                bank, c0 = 2 * (b % 2) + half, half * NIMG + g * P + 32 * b
                                pe.wait_ge(bank_sb[bank], uses(i, u, g, b // 2) + 1)
                                for q in range(4):
                                    last = nc.tensor.matmul(ps[bank][32 * q:32 * q + 32, :],
                                                            col[u][:, c0:c0 + 32], diag[u][:, 512 * q:512 * q + 512],
                                                            start=True, stop=True, tile_position=(0, 32 * q))
                                last.then_inc(bank_ps[bank], 1)

                    def apply_p(i, u, g):
                        for bank in range(4):
                            pe.wait_ge(bank_sb[bank], uses(i, u, g, 1) + 2)
                        pe.wait_ge(*prev(flat_sb[g], i, u))
                        for n in range(8):
                            for b in range(4):
                                m = (4 * g + b) * 8 + n
                                last = nc.tensor.matmul(ps[4 + g][32 * b:32 * b + 32, 0:P], probs_t[:, m * 32:(m + 1) * 32],
                                                        hx[:, m * P:(m + 1) * P], start=(n == 0), stop=(n == 7),
                                                        tile_position=(0, 32 * b))
                        last.then_inc(out_ps[g], 1)

                    def turn_back(i, u, g):
                        pe.wait_ge(*now(flat_sb[g], i, u))
                        pe.wait_ge(*prev(spec_sb[g], i, u))
                        nc.tensor.matmul(ps[6 + g][:, 0:P], flat[g][:, :], K("ident"), start=True, stop=True).then_inc(turned_ps[g], 1)

                    def step(i, u, first=False, last=False):
                        apply_h(i, u, 1)
                        if not first:
                            turn_back(i - 1 + u, 1 - u, 1)
                        apply_p(i, u, 0)
                        if not last:
                            apply_h(i + u, 1 - u, 0)
                        turn_back(i, u, 0)
                        apply_p(i, u, 1)
                    apply_h(0, 0, 0)
                    step(0, 0, first=True)
                    step(0, 1)
                    with pe.Fori(1, FT) as i:
                        for u in range(2):
                            step(i, u)
                    step(FT, 0, last=True)
                    turn_back(FT, 0, 1)

                def copy_banks(eng, op, half, i, u, g, between=None):
                    for b in range(4):
                        bank = 2 * (b % 2) + half
                        eng.wait_ge(bank_ps[bank], uses(i, u, g, b // 2) + 1)
                        if b == 0:
                            eng.wait_ge(*prev(out_ps[g], i, u))
                        op(hx5[:, 4 * g + b, :, half, :], ps[bank][:, :].rearrange("p (n c) -> p n c", c=64)
                           ).then_inc(bank_sb[bank], 1)
                        if between:
                            between(b)

                @block.scalar
                def _(act):
                    def copy_flat(i, u, g):
                        act.wait_ge(*now(out_ps[g], i, u))
                        act.wait_ge(*prev(turned_ps[g], i, u))
                        nc.scalar.copy(flat[g][:, :], ps[4 + g][:, 0:P]).then_inc(flat_sb[g], 1)

                    def copy_spec(i, u, g):
                        act.wait_ge(*now(turned_ps[g], i, u))
                        nc.scalar.copy(spec_o[:, bass.ds((2 * i + u) * NIMG + g * P, P)], ps[6 + g][:, 0:P]).then_inc(spec_sb[g], 1)

                    def step(i, u, first=False, last=False):
                        copy_banks(act, nc.scalar.copy, 0, i, u, 1)
                        if not first:
                            copy_spec(i - 1 + u, 1 - u, 1)
                        copy_flat(i, u, 0)
                        if not last:
                            copy_banks(act, nc.scalar.copy, 0, i + u, 1 - u, 0)
                        copy_spec(i, u, 0)
                        copy_flat(i, u, 1)
                    act.wait_ge(coef_ready, 1)
                    copy_banks(act, nc.scalar.copy, 0, 0, 0, 0)
                    step(0, 0, first=True)
                    step(0, 1)
                    with act.Fori(1, FT) as i:
                        for u in range(2):
                            step(i, u)
                    step(FT, 0, last=True)
                    copy_spec(FT, 0, 1)

                @block.vector
                def _(dve):
                    link = linker(dve, lk)
                    tt, ts = nc.vector.tensor_tensor, nc.vector.tensor_scalar
                    v3 = lambda t: t.rearrange("p (f n) -> p f n", n=NH)
                    bc = lambda name: SM(name).unsqueeze(1).broadcast_to([P, MF, NH])
                    dve.wait_ge(vp_in, 16)
                    link(tt(v3(h_r), v3(VP("v_r")), bc("Psw"), ALU.mult))
                    link(tt(v3(h_i), v3(VP("v_i")), bc("Psw"), ALU.mult))
                    for c, op in (("r", ALU.add), ("i", ALU.subtract)):
                        z = VP("v_" + c)[:, 0:NH]
                        link(tt(z, z, VP("vrev_" + c), op))
                        link(ts(z, z, 0.5, None, ALU.mult))
                    link(tt(v3(VP("v_r")), v3(VP("v_r")), bc("Vsw"), ALU.add))
                    for dst, a, b, op in ((h_r, "p_r", "v_r", ALU.add), (h_r, "p_i", "v_i", ALU.subtract),
                                          (h_i, "p_r", "v_i", ALU.add), (h_i, "p_i", "v_r", ALU.add)):
                        link(tt(tmp, VP(a), VP(b), ALU.mult))
                        link(tt(dst, dst, tmp, op))
                    c4 = coef[:, :].rearrange("p (m c) -> p m c", c=2)
                    for q in range(4):
                        r4 = slice(32 * q, 32 * q + 32)
                        if q % 2 == 0:
                            link(nc.vector.tensor_copy(c4[r4, :, 0], h_r[r4, :]))
                            link(nc.vector.tensor_copy(c4[r4, :, 1], h_i[r4, :]))
                        else:
                            link(ts(c4[r4, :, 0], h_i[r4, :], -1.0, None, ALU.mult))
                            link(nc.vector.tensor_copy(c4[r4, :, 1], h_r[r4, :]))
                    dve.sem_inc(coef_ready, 1)

                    def prepare(i, u):
                        for k in range(4):
                            prepare_part(i, u, k)

                    def prepare_part(i, u, k):
                        f = 2 * i + u
                        if k == 0:
                            for h in range(2):
                                r = slice(64 * h, 64 * h + 64)
                                nc.vector.tensor_copy(col[u][r, h * NIMG:(h + 1) * NIMG], spec_u[r, bass.ds(f * NIMG, NIMG)])
                        tt(diag[u][:, 512 * k:512 * k + 512].rearrange("p (m k) -> p m k", k=32),
                           coef[:, bass.ds(f * 2 * NH + 16 * k, 16)].unsqueeze(2).broadcast_to([P, 16, 32]),
                           K("mask").unsqueeze(1).broadcast_to([P, 16, 32]), ALU.mult).then_inc(ready[u], 1)

                    def step(i, u, more=True, last=False):
                        copy_banks(dve, nc.vector.tensor_copy, 1, i, u, 1)
                        if not last:
                            copy_banks(dve, nc.vector.tensor_copy, 1, i + u, 1 - u, 0,
                                       (lambda k: prepare_part(i + 1, u, k)) if more else None)
                    for u in range(2):
                        link(nc.vector.memset(col[u][:, :], 0.0))
                    prepare(0, 0)
                    prepare(0, 1)
                    copy_banks(dve, nc.vector.tensor_copy, 1, 0, 0, 0)
                    with dve.Fori(0, FT - 1) as i:
                        for u in range(2):
                            step(i, u)
                    step(FT - 1, 0)
                    step(FT - 1, 1, more=False)
                    step(FT, 0, more=False, last=True)
        end_stage()

        with ExitStack() as st:
            def sb(name, cols):
                return st.enter_context(nc.sbuf_tensor(name, [P, cols], F32))
            PC = 2048
            g = [sb(f"s7_g{u}", PC) for u in range(2)]
            z = [sb(f"s7_z{u}", PC) for u in range(2)]
            g_in, mix_ps, stored = sem("s7_g_in", 2), sem("s7_mix_ps", 2, 1), sem("s7_stored", 2, 16)
            z_act, z_dve = sem("s7_z_act", 2, 1), sem("s7_z_dve", 2, 1)

            def pixels(t, i, u):
                return t.rearrange("b t y w -> (b t) (y w)")[u * P:(u + 1) * P, bass.ds(i * PC, PC)]
            with nc.Block() as block:
                @block.sync
                def _(sp):
                    with sp.Fori(0, PIX // PC) as i:
                        for u in range(2):
                            sp.wait_ge(*prev2(mix_ps, i, u))
                            sp.dma_start(g[u][:, :], pixels(g_d, i, u)).then_inc(g_in[u], 16)

                @block.gpsimd
                def _(pool):
                    free_all(pool)

                @block.tensor
                def _(pe):
                    with pe.Fori(0, PIX // PC) as i:
                        for u in range(2):
                            pe.wait_ge(*now(g_in, i, u, 16))
                            pe.wait_ge(*prev2(z_act, i, u))
                            pe.wait_ge(*prev2(z_dve, i, u))
                            for k in range(4):
                                last = nc.tensor.matmul(ps[4 * u + k][:, :], mix_t[:, u * P:(u + 1) * P],
                                                        g[u][:, k * 512:(k + 1) * 512], start=True, stop=True)
                            last.then_inc(mix_ps[u], 1)

                @block.scalar
                def _(act):
                    with act.Fori(0, PIX // PC) as i:
                        for u in range(2):
                            act.wait_ge(*now(mix_ps, i, u))
                            act.wait_ge(*prev2(stored, i, u, 16))
                            for k in (0, 2):
                                last = nc.scalar.activation(z[u][:, k * 512:(k + 1) * 512], ps[4 * u + k][:, :], ACT.Identity,
                                                            bias=mix_const[:, u:u + 1])
                            last.then_inc(z_act[u], 1)
                            act.wait_ge(*now(z_act, i, u))
                            act.wait_ge(*now(z_dve, i, u))
                            act.dma_start(pixels(z_d, i, u), z[u][:, :]).then_inc(stored[u], 16)
                    for u in range(2):
                        act.wait_ge(stored[u], done(stored, PIX // PC, 16))

                @block.vector
                def _(dve):
                    with dve.Fori(0, PIX // PC) as i:
                        for u in range(2):
                            dve.wait_ge(*now(mix_ps, i, u))
                            dve.wait_ge(*prev2(stored, i, u, 16))
                            for k in (1, 3):
                                last = nc.vector.tensor_scalar(z[u][:, k * 512:(k + 1) * 512], ps[4 * u + k][:, :],
                                                               mix_const[:, u:u + 1], None, ALU.add)
                            last.then_inc(z_dve[u], 1)
        end_stage()

        conv_var = keep("conv_var", NIMG)
        conv = spec_u
        with ExitStack() as st:
            def sb(name, cols):
                return st.enter_context(nc.sbuf_tensor(name, [P, cols], F32))
            gs = [sb(f"s8_gs{u}", NIMG) for u in range(2)]
            gt = [sb(f"s8_gt{u}", NIMG) for u in range(2)]
            ys = [sb(f"s8_ys{u}", NIMG) for u in range(2)]
            pr = [sb(f"s8_pr{u}", NIMG) for u in range(2)]
            sq = [sb(f"s8_sq{u}", NIMG) for u in range(2)]
            h0 = sb("s8_h0", NIMG)
            g_in, t_ps, t_sb, y_ps, y_sb, j_ps, pr_sb, c_sb, sq_sb, e_ps = (
                sem("s8_" + n, 2, s) for n, s in (("g_in", 0), ("t_ps", 1), ("t_sb", 1), ("y_ps", 1), ("y_sb", 1), ("j_ps", 1),
                                                  ("pr_sb", 0), ("c_sb", 1), ("sq_sb", 0), ("e_ps", 1)))
            h_ps, h_sb, d_ps, d_sb, e0_ps = (sem("s8_" + n) for n in ("h_ps", "h_sb", "d_ps", "d_sb", "e0_ps"))
            FT = MF // 2
            E = ps[6][:, 0:NIMG]
            with nc.Block() as block:
                @block.sync
                def _(sp):
                    with sp.Fori(0, FT) as i:
                        for u in range(2):
                            sp.wait_ge(*prev2(t_ps, i, u))
                            sp.dma_start(gs[u][:, :], u_d[:, bass.ds((2 * i + u + 1) * NIMG, NIMG)]).then_inc(g_in[u], 16)
                    sp.wait_ge(*prev2(t_ps, FT, 0))
                    sp.dma_start(gs[0][:, :], u_d[:, 0:NIMG]).then_inc(g_in[0], 16)

                @block.gpsimd
                def _(pool):
                    free_all(pool)

                @block.tensor
                def _(pe):
                    def transpose(i, u):
                        pe.wait_ge(*now(g_in, i, u, 16))
                        pe.wait_ge(*prev2(t_sb, i, u))
                        for g in range(2):
                            last = nc.tensor.matmul(ps[u][:, g * P:(g + 1) * P], gs[u][:, g * P:(g + 1) * P], K("ident"),
                                                    start=True, stop=True)
                        last.then_inc(t_ps[u], 1)

                    def mix(i, u):
                        pe.wait_ge(*now(t_sb, i, u))
                        pe.wait_ge(*prev2(y_sb, i, u))
                        for g in range(2):
                            last = nc.tensor.matmul(ps[2 + u][:, g * P:(g + 1) * P], gt[u][:, g * P:(g + 1) * P],
                                                    mix_t[:, g * P:(g + 1) * P], start=True, stop=True)
                        last.then_inc(y_ps[u], 1)

                    def turn(i, u):
                        pe.wait_ge(*now(y_sb, i, u))
                        pe.wait_ge(*prev2(c_sb, i, u))
                        nc.tensor.matmul(ps[4 + u][:, 0:NIMG], K("turn"), ys[u][:, :], start=True, stop=True).then_inc(j_ps[u], 1)

                    def energy(i, u, first=False):
                        pe.wait_ge(*now(sq_sb, i, u))
                        nc.tensor.matmul(E, K("twos"), sq[u][:, :], start=first, stop=False).then_inc(e_ps[u], 1)

                    def step(i, u, first=False, last=False):
                        mix(i, u)
                        if not last:
                            transpose(i + u, 1 - u)
                        if not first:
                            energy(i - 1 + u, 1 - u, first=(type(i) is int and i + u == 1))
                        turn(i, u)
                    nc.tensor.matmul(ps[7][:, 0:NIMG], K("herm_y"), spec_o[:, 0:NIMG], start=True, stop=True).then_inc(h_ps, 1)
                    transpose(0, 0)
                    step(0, 0, first=True)
                    step(0, 1)
                    with pe.Fori(1, FT) as i:
                        for u in range(2):
                            step(i, u)
                    step(FT, 0, last=True)
                    pe.wait_ge(*now(c_sb, FT, 0))
                    nc.tensor.matmul(ps[7][:, 0:NIMG], K("herm"), conv[:, 0:NIMG], start=True, stop=True).then_inc(d_ps, 1)
                    pe.wait_ge(d_sb, 1)
                    nc.tensor.matmul(E, K("energy0"), sq[0][:, :], start=False, stop=True).then_inc(e0_ps, 1)

                @block.scalar
                def _(act):
                    def copy_turned(i, u):
                        act.wait_ge(*now(t_ps, i, u))
                        act.wait_ge(*prev2(y_ps, i, u))
                        nc.scalar.copy(gt[u][:, :], ps[u][:, 0:NIMG]).then_inc(t_sb[u], 1)

                    def square(i, u):
                        act.wait_ge(*now(c_sb, i, u))
                        act.wait_ge(*prev2(e_ps, i, u))
                        nc.scalar.activation(sq[u][:, :], conv[:, bass.ds((2 * i + u + 1) * NIMG, NIMG)], ACT.Square
                                             ).then_inc(sq_sb[u], 1)
                    copy_turned(0, 0)
                    with act.Fori(0, FT) as i:
                        for u in range(2):
                            copy_turned(i + u, 1 - u)
                            square(i, u)
                    act.wait_ge(d_ps, 1)
                    act.wait_ge(*prev2(e_ps, FT, 0))
                    nc.scalar.activation(sq[0][:, :], ps[7][:, 0:NIMG], ACT.Square).then_inc(d_sb, 1)

                @block.vector
                def _(dve):
                    dve.wait_ge(h_ps, 1)
                    nc.vector.tensor_copy(h0[:, :], ps[7][:, 0:NIMG]).then_inc(h_sb, 1)
                    dve.wait_ge(h_sb, 1)

                    def step(i, u, f, attention):
                        dve.wait_ge(*now(y_ps, i, u))
                        dve.wait_ge(*prev2(j_ps, i, u))
                        nc.vector.tensor_tensor(ys[u][:, :], ps[2 + u][:, 0:NIMG], attention, ALU.add).then_inc(y_sb[u], 1)
                        dve.wait_ge(*now(y_sb, i, u))
                        nc.vector.tensor_scalar(pr[u][:, :], ys[u][:, :], SM("m0_r")[:, f], None, ALU.mult).then_inc(pr_sb[u], 1)
                        dve.wait_ge(*now(pr_sb, i, u))
                        dve.wait_ge(*now(j_ps, i, u))
                        nc.vector.scalar_tensor_tensor(conv[:, bass.ds(f.start * NIMG, NIMG) if type(f) is slice else
                                                            bass.ds((2 * i + u + 1) * NIMG, NIMG)],
                                                       ps[4 + u][:, 0:NIMG], SM("m0_i")[:, f], pr[u][:, :], ALU.mult, ALU.add
                                                       ).then_inc(c_sb[u], 1)
                    with dve.Fori(0, FT) as i:
                        for u in range(2):
                            step(i, u, bass.ds(2 * i + u + 1, 1), spec_o[:, bass.ds((2 * i + u + 1) * NIMG, NIMG)])
                    step(FT, 0, slice(0, 1), h0[:, :])
                    dve.wait_ge(e0_ps, 1)
                    nc.vector.tensor_copy(conv_var[:, :], E)
        end_stage()

        def inverse_rows(pe, i, u, h, spectrum, ready, bank, free, inv_ps):
            pe.wait_ge(*ready)
            pe.wait_ge(*free)
            for k in range(4):
                s = spectrum(4 * h + k)
                nc.tensor.matmul(bank[0:MF, k * N:(k + 1) * N], s, K("inv_re"), start=True, stop=True)
                last = nc.tensor.matmul(bank[64:64 + MF, k * N:(k + 1) * N], s, K("inv_im"), start=True, stop=True)
            last.then_inc(at(inv_ps[h], u), 1)

        def inverse_cols(pe, i, u, h, half, half_sb, bank, free, out_ps):
            pe.wait_ge(*now(half_sb[h], i, u))
            if free:
                pe.wait_ge(*free)
            for k in range(4):
                last = nc.tensor.matmul(bank[:, k * N:(k + 1) * N], half[0:64 + MF, k * N:(k + 1) * N],
                                        K("inv_w", 0, 64 + MF), start=True, stop=True)
            last.then_inc(at(out_ps[h], u), 1)

        def copy_half(i, u, h, half, bank, inv_ps, half_sb, out_ps):
            act = nc.scalar
            act.wait_ge(*now(inv_ps[h], i, u))
            act.wait_ge(*prev2(out_ps[h], i, u))
            nc.scalar.copy(half[0:MF, :], bank[0:MF, :])
            nc.scalar.copy(half[64:64 + MF, :], bank[64:64 + MF, :]).then_inc(half_sb[h][u], 1)

        with ExitStack() as st:
            def sb(name, cols):
                return st.enter_context(nc.sbuf_tensor(name, [P, cols], F32))
            z = [sb(f"s9_z{u}", CW) for u in range(2)]
            y = [sb(f"s9_y{u}", CW) for u in range(2)]
            sq = sb("s9_sq", CW)
            half = [[sb(f"s9_half{u}{h}", 512) for h in range(2)] for u in range(2)]
            chunk = [sb(f"s9_chunk{u}", MF * CH) for u in range(2)]
            ch3 = [c[:, :].rearrange("p (f n) -> p f n", n=CH) for c in chunk]
            z_in, stored, y_ready = sem("s9_z_in", 2), sem("s9_stored", 2, 16), sem("s9_y_ready", 2, 2)
            chunk_ready, zeroed = sem("s9_chunk_ready", 2), sem("s9_zeroed")
            inv_ps, half_sb, out_ps, taken = ([sem(f"s9_{n}{h}_", 2, 1) for h in range(2)] for n in ("inv_ps", "half_sb", "out_ps", "taken"))
            squared, reduced = sem("s9_squared"), sem("s9_reduced", None, 1)
            with nc.Block() as block:
                @block.sync
                def _(sp):
                    with sp.Fori(0, NT) as i:
                        for u in range(2):
                            sp.wait_ge(*prev2(y_ready, i, u, 2))
                            sp.dma_start(z[u][:, :], channel_of(z_d, 2 * i + u)).then_inc(z_in[u], 16)

                @block.gpsimd
                def _(pool):
                    free_all(pool)
                    for t in half[0] + half[1]:
                        nc.gpsimd.memset(t[:, :], 0.0).then_inc(zeroed, 1)

                @block.tensor
                def _(pe):
                    def rows(i, u):
                        for h in range(2):
                            inverse_rows(pe, i, u, h, lambda n: ch3[u][:, :, n], now(chunk_ready, i, u), ps[2 * u + h],
                                         prev2(half_sb[h], i, u), inv_ps)

                    def turn(i, last):
                        for u in range(2):
                            if not (last and u):
                                rows(i + u, 1 - u)
                            for h in range(2):
                                inverse_cols(pe, i, u, h, half[u][h], half_sb, ps[4 + 2 * u + h], prev2(taken[h], i, u), out_ps)
                    rows(0, 0)
                    with pe.Fori(0, NT - 1) as i:
                        turn(i, False)
                    turn(NT - 1, True)

                @block.scalar
                def _(act):
                    def halves(i, u):
                        for h in range(2):
                            copy_half(i, u, h, half[u][h], ps[2 * u + h], inv_ps, half_sb, out_ps)

                    def turn(i, last):
                        for u in range(2):
                            if not (last and u):
                                halves(i + u, 1 - u)
                            act.wait_ge(*now(y_ready, i, u, 2))
                            act.dma_start(laid_channel(y_d, 2 * i + u), y[u][:, :]).then_inc(stored[u], 16)
                            act.wait_ge(*prev(reduced, i, u))
                            nc.scalar.activation(sq[:, :], y[u][:, :], ACT.Square).then_inc(squared, 1)
                    act.wait_ge(zeroed, 4)
                    halves(0, 0)
                    with act.Fori(0, NT - 1) as i:
                        turn(i, False)
                    turn(NT - 1, True)
                    for u in range(2):
                        act.wait_ge(stored[u], done(stored, NT, 16))

                @block.vector
                def _(dve):
                    def prepare(i, u):
                        dve.wait_ge(*prev2(inv_ps[1], i, u))
                        nc.vector.tensor_copy(ch3[u].rearrange("p f n -> p n f"), images(spec_o[:, :], i, u)
                                              ).then_inc(chunk_ready[u], 1)

                    def turn(i, last):
                        for u in range(2):
                            dve.wait_ge(*now(z_in, i, u, 16))
                            dve.wait_ge(*prev2(stored, i, u, 16))
                            for h in range(2):
                                dve.wait_ge(*now(out_ps[h], i, u))
                                w = slice(512 * h, 512 * h + 512)
                                nc.vector.tensor_tensor(y[u][:, w], ps[4 + 2 * u + h][:, :], z[u][:, w], ALU.add).then_inc(y_ready[u], 1)
                                dve.sem_inc(taken[h][u], 1)
                            if not last:
                                prepare(i + 1, u)
                            dve.wait_ge(*now(y_ready, i, u, 2))
                            nc.vector.tensor_reduce(per_image(img_sum[:, :], i, u), y[u][:, :].rearrange("y (n w) -> y n w", n=CH), AX.X, ALU.add)
                            dve.wait_ge(*now(squared, i, u))
                            nc.vector.tensor_reduce(per_image(img_sumsq[:, :], i, u), sq[:, :].rearrange("y (n w) -> y n w", n=CH), AX.X,
                                                    ALU.add).then_inc(reduced, 1)
                    prepare(0, 0)
                    prepare(0, 1)
                    with dve.Fori(0, NT - 1) as i:
                        turn(i, False)
                    turn(NT - 1, True)
        end_stage()

        alpha, a_scale, a_shift, conv_scale, const, y_scale = (
            keep(n, NIMG) for n in ("alpha", "a_scale", "a_shift", "conv_scale", "const", "y_scale"))
        mean, var, root, tmp, tmp2 = (keep("img_" + n, NIMG) for n in ("mean", "var", "root", "tmp", "tmp2"))
        esum = keep("esum", 2 * NIMG)
        cross0 = keep("cross0", NIMG)
        conv1 = spec_o
        conv1_3 = conv1[:, :].rearrange("p (n f) -> p n f", f=MF)

        def conv1_of(i, u, lo=0, hi=B):
            return conv1[:, :].rearrange("p (b t f) -> p t b f", b=B, t=T)[:, bass.ds(2 * i + u, 1), lo:hi, :].rearrange("p o b f -> p (o b) f")

        def counted(eng, link, i, u, per_step):
            count = [0]

            def run(ins, n=1):
                count[0] += n
                ins.then_inc(link, 1)
                eng.wait_ge(link, 2 * per_step * i + per_step * u + count[0])
            return run, count

        with ExitStack() as st:
            def sb(name, cols):
                return st.enter_context(nc.sbuf_tensor("s10_" + name, [P, cols], F32))

            def lsem(n, k=None, starts=0):
                return sem("s10_" + n, k, starts)
            yin = [sb(f"y{u}", CW) for u in range(2)]
            v = [sb(f"v{u}", CW) for u in range(2)]
            sq = sb("sq", CW)
            rf = [sb(f"rowft{u}", CH * 2 * N)[:, :].rearrange("w (n r) -> w n r", n=CH) for u in range(2)]
            half = [[sb(f"half{u}{h}", 512) for h in range(2)] for u in range(2)]
            chunk = [sb(f"chunk{u}", MF * CH) for u in range(2)]
            ch3 = [c[:, :].rearrange("p (f n) -> p f n", n=CH) for c in chunk]
            pr = [sb(f"pr{h}", 4 * MF) for h in range(2)]
            prt = [sb(f"prt{h}", 4 * MF) for h in range(2)]
            prod = [sb(f"prod{h}", 8 * MF) for h in range(2)]
            y_in, chunk_scaled, chunk_ready = lsem("y_in", 2), lsem("chunk_scaled", 2), lsem("chunk_ready", 2)
            inv_ps, half_sb, out_ps, taken, v_ready = ([lsem(f"{n}{h}_", 2, s) for h in range(2)] for n, s in (
                ("inv_ps", 1), ("half_sb", 0), ("out_ps", 1), ("taken", 1), ("v_ready", 0)))
            row_ps, col_ps = ([lsem(f"{n}{h}_", 2, s) for h in range(2)] for n, s in (("row_ps", 0), ("col_ps", 1)))
            spec_done = lsem("spec_done", 2, 1)
            row_sb = [lsem(f"row_sb{h}_", 2, 1) for h in range(2)]
            squared, reduced, zeroed, loop_link = lsem("squared"), lsem("reduced", None, 1), lsem("zeroed"), lsem("loop_link")
            m_stored = lsem("m_stored", 2, 16)
            tot_ps, var_ready, root_ready, lk = (lsem(n) for n in ("tot_ps", "var_ready", "root_ready", "link"))
            MR, MI = SM("m1_r"), SM("m1_i")
            with nc.Block() as block:
                @block.sync
                def _(sp):
                    with sp.Fori(0, NT) as i:
                        for u in range(2):
                            sp.wait_ge(*prev2(taken[1], i, u))
                            sp.dma_start(yin[u][:, :], laid_channel(y_d, 2 * i + u)).then_inc(y_in[u], 16)

                @block.gpsimd
                def _(pool):
                    free_all(pool)
                    for t in half[0] + half[1]:
                        nc.gpsimd.memset(t[:, :], 0.0).then_inc(zeroed, 1)

                @block.tensor
                def _(pe):
                    nc.tensor.matmul(ps[0][:, 0:NIMG], K("ones"), img_sum[:, :], start=True, stop=True)
                    nc.tensor.matmul(ps[0][:, NIMG:2 * NIMG], K("ones"), img_sumsq[:, :], start=True, stop=True).then_inc(tot_ps, 1)

                    def inv_rows(i, u):
                        for h in range(2):
                            inverse_rows(pe, i, u, h, lambda n: ch3[u][:, :, n], now(chunk_ready, i, u), ps[6 + h],
                                         prev(taken[h], i, u), inv_ps)

                    def inv_cols(i, u):
                        for h in range(2):
                            inverse_cols(pe, i, u, h, half[u][h], half_sb, ps[6 + h], None, out_ps)

                    def rows(i, u):
                        for h in range(2):
                            pe.wait_ge(*now(v_ready[h], i, u))
                            forward_rows(pe, i, u, h, v[u], row_ps, row_sb)

                    def cols(i, u):
                        for h in range(2):
                            forward_cols(pe, i, u, h, rf[u], row_sb, col_ps, spec_done)

                    def turn(i, last):
                        for u in range(2):
                            more = not (last and u)
                            if more:
                                inv_rows(i + u, 1 - u)
                            rows(i, u)
                            if more:
                                inv_cols(i + u, 1 - u)
                            cols(i, u)
                    inv_rows(0, 0)
                    inv_cols(0, 0)
                    with pe.Fori(0, NT - 1) as i:
                        turn(i, False)
                    turn(NT - 1, True)

                @block.scalar
                def _(act):
                    for n, t in enumerate((var, tmp2, tmp2)):
                        act.wait_ge(var_ready, n + 1)
                        nc.scalar.activation(root[:, :], t[:, :], ACT.Sqrt).then_inc(root_ready, 1)

                    def halves(i, u):
                        for h in range(2):
                            copy_half(i, u, h, half[u][h], ps[6 + h], inv_ps, half_sb, out_ps)

                    def gelu(i, u):
                        for h in range(2):
                            act.wait_ge(*now(taken[h], i, u))
                            w = slice(512 * h, 512 * h + 512)
                            nc.scalar.activation(v[u][:, w], v[u][:, w], ACT.Gelu).then_inc(v_ready[h][u], 1)
                        for h in range(2):
                            act.wait_ge(*now(v_ready[h], i, u))
                        act.dma_start(laid_channel(m_d, 2 * i + u), v[u][:, :]).then_inc(m_stored[u], 16)

                    def turn(i, last):
                        for u in range(2):
                            more = not (last and u)
                            if more:
                                halves(i + u, 1 - u)
                            for h in range(2):
                                copy_rows(act, nc.scalar.copy, 0, i, u, h, rf[u], row_ps, row_sb, col_ps)
                            copy_rows(act, nc.scalar.copy, 1, i, u, 1, rf[u], row_ps, row_sb, col_ps)
                            if more:
                                gelu(i + u, 1 - u)
                            act.wait_ge(*prev(reduced, i, u))
                            nc.scalar.activation(sq[:, :], v[u][:, :], ACT.Square).then_inc(squared, 1)
                    act.wait_ge(zeroed, 4)
                    halves(0, 0)
                    gelu(0, 0)
                    with act.Fori(0, NT - 1) as i:
                        turn(i, False)
                    turn(NT - 1, True)
                    for u in range(2):
                        act.wait_ge(m_stored[u], done(m_stored, NT, 16))

                @block.vector
                def _(dve):
                    tt, ts, stt = nc.vector.tensor_tensor, nc.vector.tensor_scalar, nc.vector.scalar_tensor_tensor
                    link = linker(dve, lk)
                    dve.wait_ge(tot_ps, 1)
                    link(ts(mean[:, :], ps[0][:, 0:NIMG], 1.0 / PIX, None, ALU.mult))
                    link(ts(var[:, :], ps[0][:, NIMG:2 * NIMG], 1.0 / PIX, None, ALU.mult))
                    link(tt(tmp[:, :], mean[:, :], mean[:, :], ALU.mult))
                    link(tt(var[:, :], var[:, :], tmp[:, :], ALU.subtract))
                    inv_std(dve, link, var[:, :], root[:, :], tmp[:, :], var_ready, root_ready, 1)
                    link(ts(a_scale[:, :], root[:, :], SM("attn_w"), None, ALU.mult))
                    link(tt(a_shift[:, :], mean[:, :], a_scale[:, :], ALU.mult))
                    link(ts(a_shift[:, :], a_shift[:, :], -1.0, SM("attn_b"), ALU.mult, ALU.add))
                    link(ts(var[:, :], var[:, :], -EPS, None, ALU.add))
                    link(tt(tmp2[:, :], a_scale[:, :], a_scale[:, :], ALU.mult))
                    link(tt(tmp2[:, :], tmp2[:, :], var[:, :], ALU.mult))
                    inv_std(dve, link, tmp2[:, :], root[:, :], tmp[:, :], var_ready, root_ready, 2)
                    link(tt(alpha[:, :], a_scale[:, :], root[:, :], ALU.mult))
                    link(ts(alpha[:, :], alpha[:, :], SM("norm2_w"), None, ALU.mult))
                    link(tt(const[:, :], mean[:, :], alpha[:, :], ALU.mult))
                    link(ts(const[:, :], const[:, :], -1.0, SM("norm2_b"), ALU.mult, ALU.add))
                    link(ts(const[:, :], const[:, :], SM("m0sw"), None, ALU.mult))
                    link(ts(y_scale[:, :], alpha[:, :], SM("m0sw"), None, ALU.mult))
                    link(tt(tmp2[:, :], alpha[:, :], alpha[:, :], ALU.mult))
                    link(tt(tmp2[:, :], tmp2[:, :], conv_var[:, :], ALU.mult))
                    inv_std(dve, link, tmp2[:, :], root[:, :], tmp[:, :], var_ready, root_ready, 3)
                    link(tt(conv_scale[:, :], alpha[:, :], root[:, :], ALU.mult))

                    def prepare(i, u):
                        dve.wait_ge(*prev2(inv_ps[1], i, u))
                        tt(ch3[u].rearrange("p f n -> p n f"), images(conv[:, :], i, u),
                           per_image(conv_scale[:, :], i, u).unsqueeze(2).broadcast_to([P, CH, MF]), ALU.mult
                           ).then_inc(chunk_scaled[u], 1)
                        dve.wait_ge(*now(chunk_scaled, i, u))
                        nc.vector.tensor_copy(ch3[u][0:1, 0, :], per_image(const[0:1, :], i, u)).then_inc(chunk_ready[u], 1)

                    def layer_input(i, u):
                        dve.wait_ge(*now(y_in, i, u, 16))
                        dve.wait_ge(*prev2(m_stored, i, u, 16))
                        for h in range(2):
                            dve.wait_ge(*now(out_ps[h], i, u))
                            for n in range(4 * h, 4 * h + 4):
                                w = slice(n * N, (n + 1) * N)
                                k = n - 4 * h
                                last = stt(v[u][:, w], yin[u][:, w], y_scale[:, bass.ds(2 * i + u + T * n, 1)],
                                           ps[6 + h][:, k * N:(k + 1) * N], ALU.mult, ALU.add)
                            last.then_inc(taken[h][u], 1)

                    def turn(i, last):
                        for u in range(2):
                            run, count = counted(dve, loop_link, i, u, 6)
                            if not last:
                                prepare(i + 1, u)
                            copy_rows(dve, nc.vector.tensor_copy, 1, i, u, 0, rf[u], row_ps, row_sb, col_ps)
                            if not (last and u):
                                dve.wait_ge(*prev(reduced, i, u))
                                layer_input(i + u, 1 - u)
                            for h in range(2):
                                dve.wait_ge(*now(col_ps[h], i, u))
                                x = ps[4 + h][:, 0:8 * MF].rearrange("r (n a f) -> r a n f", n=4, a=2)
                                o = lambda t: t[:, :].rearrange("r (n f) -> r n f", n=4)
                                m = lambda w: w.unsqueeze(1).broadcast_to([P, 4, MF])
                                four = (i, u, 4 * h, 4 * h + 4)
                                tt(o(pr[h]), x[:, 0], m(MR), ALU.mult)
                                run(tt(o(prt[h]), x[:, 1], m(MI), ALU.mult))
                                run(tt(conv1_of(*four), o(pr[h]), o(prt[h]), ALU.add))
                                pd = prod[h][:, :].rearrange("p (a n f) -> p a n f", a=2, f=MF)
                                tt(pd[:, 0], conv1_of(*four), conv1_of(*four), ALU.mult)
                                ts(per_image(img_sum[0:1, :], *four), x[0:1, 0, :, 0], float(PIX), None, ALU.mult)
                                run(tt(pd[:, 1], conv1_of(*four), x[:, 0], ALU.mult))
                                dve.sem_inc(spec_done[h], 1)
                                nc.vector.tensor_reduce(images(esum[:, :], *four).rearrange("p n a -> p a n"), pd[:, :, :, 1:MF],
                                                        AX.X, ALU.add)
                                nc.vector.tensor_copy(per_image(cross0[:, :], *four), pd[:, 1, :, 0])
                            assert count[0] == 6
                            dve.wait_ge(*now(squared, i, u))
                            nc.vector.tensor_reduce(per_image(img_sumsq[:, :], i, u), sq[:, :].rearrange("y (n w) -> y n w", n=CH), AX.X,
                                                    ALU.add).then_inc(reduced, 1)
                    link(nc.vector.memset(img_sum[:, :], 0.0))
                    prepare(0, 0)
                    prepare(0, 1)
                    layer_input(0, 0)
                    with dve.Fori(0, NT - 1) as i:
                        turn(i, False)
                    turn(NT - 1, True)
        end_stage()

        with ExitStack() as st:
            def sb(name, cols):
                return st.enter_context(nc.sbuf_tensor("s11_" + name, [P, cols], F32))

            def lsem(n, k=None, starts=0):
                return sem("s11_" + n, k, starts)
            names = ("x", "m", "y")
            tin = {n: [sb(f"{n}{u}", CW) for u in range(2)] for n in names}
            res = [sb(f"res{u}", CW) for u in range(2)]
            half = [[sb(f"half{u}{h}", 512) for h in range(2)] for u in range(2)]
            chunk = [sb(f"chunk{u}", MF * CH) for u in range(2)]
            ch3 = [c[:, :].rearrange("p (n f) -> p n f", f=MF) for c in chunk]
            herm_sq = sb("herm_sq", NIMG)
            m_scale, energy, cov = (sb(n, NIMG) for n in ("m_scale", "energy", "cov"))
            t_in = {n: lsem(f"{n}_in", 2) for n in names}
            stored, finished, part = lsem("stored", 2, 16), lsem("finished", 2, 1), lsem("part", 2, 1)
            chunk_scaled, chunk_ready = lsem("chunk_scaled", 2), lsem("chunk_ready", 2)
            inv_ps, half_sb, out_ps, taken = ([lsem(f"{n}{h}_", 2, 1) for h in range(2)] for n in ("inv_ps", "half_sb", "out_ps", "taken"))
            herm_ps, herm_sb, tot_ps, var_ready, root_ready, lk, zeroed = (
                lsem(n) for n in ("herm_ps", "herm_sb", "tot_ps", "var_ready", "root_ready", "link", "zeroed"))
            src = {"m": m_d, "y": y_d, "x": x1_d}
            with nc.Block() as block:
                @block.sync
                def _(sp):
                    with sp.Fori(0, NT) as i:
                        for u in range(2):
                            for n, free in (("x", taken[1]), ("m", part), ("y", finished)):
                                sp.wait_ge(*prev2(free, i, u))
                                sp.dma_start(tin[n][u][:, :], laid_channel(src[n], 2 * i + u)).then_inc(t_in[n][u], 16)

                @block.gpsimd
                def _(pool):
                    free_all(pool)
                    for t in half[0] + half[1]:
                        nc.gpsimd.memset(t[:, :], 0.0).then_inc(zeroed, 1)

                @block.tensor
                def _(pe):
                    nc.tensor.matmul(ps[2][:, 0:NIMG], K("herm"), conv1_3[:, :, 0], start=True, stop=True).then_inc(herm_ps, 1)
                    nc.tensor.matmul(ps[0][:, 0:NIMG], K("ones"), img_sum[:, :], start=True, stop=True)
                    nc.tensor.matmul(ps[0][:, NIMG:2 * NIMG], K("ones"), img_sumsq[:, :], start=True, stop=True)
                    nc.tensor.matmul(ps[3][:, 0:NIMG], K("twos"), esum[:, NIMG:2 * NIMG], start=True, stop=False)
                    nc.tensor.matmul(ps[3][:, 0:NIMG], K("cov0"), cross0[:, :], start=False, stop=True)
                    nc.tensor.matmul(ps[1][:, 0:NIMG], K("twos"), esum[:, 0:NIMG], start=True, stop=False)
                    pe.wait_ge(herm_sb, 1)
                    nc.tensor.matmul(ps[1][:, 0:NIMG], K("energy0"), herm_sq[:, :], start=False, stop=True).then_inc(tot_ps, 1)

                    def rows(i, u):
                        for h in range(2):
                            inverse_rows(pe, i, u, h, lambda n: ch3[u][:, n, :], now(chunk_ready, i, u), ps[2 * u + h],
                                         prev2(half_sb[h], i, u), inv_ps)

                    def turn(i, last):
                        for u in range(2):
                            if not (last and u):
                                rows(i + u, 1 - u)
                            for h in range(2):
                                inverse_cols(pe, i, u, h, half[u][h], half_sb, ps[4 + 2 * u + h], prev2(taken[h], i, u), out_ps)
                    rows(0, 0)
                    with pe.Fori(0, NT - 1) as i:
                        turn(i, False)
                    turn(NT - 1, True)

                @block.scalar
                def _(act):
                    act.wait_ge(herm_ps, 1)
                    nc.scalar.activation(herm_sq[:, :], ps[2][:, 0:NIMG], ACT.Square).then_inc(herm_sb, 1)
                    for n in range(2):
                        act.wait_ge(var_ready, n + 1)
                        nc.scalar.activation(root[:, :], var[:, :], ACT.Sqrt).then_inc(root_ready, 1)

                    def halves(i, u):
                        for h in range(2):
                            copy_half(i, u, h, half[u][h], ps[2 * u + h], inv_ps, half_sb, out_ps)

                    def turn(i, last):
                        for u in range(2):
                            if not (last and u):
                                halves(i + u, 1 - u)
                            act.wait_ge(*now(finished, i, u))
                            act.dma_start(channel_of(out, 2 * i + u), res[u][:, :]).then_inc(stored[u], 16)
                    act.wait_ge(zeroed, 4)
                    halves(0, 0)
                    with act.Fori(0, NT - 1) as i:
                        turn(i, False)
                    turn(NT - 1, True)
                    for u in range(2):
                        act.wait_ge(stored[u], done(stored, NT, 16))

                @block.vector
                def _(dve):
                    tt, ts, stt = nc.vector.tensor_tensor, nc.vector.tensor_scalar, nc.vector.scalar_tensor_tensor
                    link = linker(dve, lk)
                    dve.wait_ge(tot_ps, 1)
                    link(nc.vector.tensor_copy(energy[:, :], ps[1][:, 0:NIMG]))
                    link(nc.vector.tensor_copy(cov[:, :], ps[3][:, 0:NIMG]))
                    link(nc.vector.tensor_copy(var[:, :], energy[:, :]))
                    inv_std(dve, link, var[:, :], root[:, :], tmp[:, :], var_ready, root_ready, 1)
                    link(nc.vector.tensor_copy(conv_scale[:, :], root[:, :]))
                    link(ts(mean[:, :], ps[0][:, 0:NIMG], 1.0 / PIX, None, ALU.mult))
                    link(ts(var[:, :], ps[0][:, NIMG:2 * NIMG], 1.0 / PIX, None, ALU.mult))
                    link(tt(tmp[:, :], mean[:, :], mean[:, :], ALU.mult))
                    link(tt(var[:, :], var[:, :], tmp[:, :], ALU.subtract))
                    link(tt(cov[:, :], cov[:, :], conv_scale[:, :], ALU.mult))
                    link(ts(cov[:, :], cov[:, :], 2.0, None, ALU.mult))
                    link(stt(var[:, :], var[:, :], SM("m1sw"), cov[:, :], ALU.mult, ALU.add))
                    link(tt(energy[:, :], energy[:, :], conv_scale[:, :], ALU.mult))
                    link(tt(energy[:, :], energy[:, :], conv_scale[:, :], ALU.mult))
                    link(stt(var[:, :], var[:, :], SM("m1sw"), energy[:, :], ALU.mult, ALU.add))
                    inv_std(dve, link, var[:, :], root[:, :], tmp[:, :], var_ready, root_ready, 2)
                    link(ts(root[:, :], root[:, :], SM("mon_w"), None, ALU.mult))
                    link(tt(conv_scale[:, :], conv_scale[:, :], root[:, :], ALU.mult))
                    link(ts(m_scale[:, :], root[:, :], SM("m1sw"), None, ALU.mult))
                    link(tt(tmp[:, :], mean[:, :], m_scale[:, :], ALU.mult))
                    link(tt(tmp[:, :], a_shift[:, :], tmp[:, :], ALU.subtract))
                    link(ts(const[:, :], tmp[:, :], SM("mon_b"), None, ALU.add))

                    def prepare(i, u):
                        dve.wait_ge(*prev2(inv_ps[1], i, u))
                        tt(ch3[u], conv1_of(i, u), per_image(conv_scale[:, :], i, u).unsqueeze(2).broadcast_to([P, CH, MF]), ALU.mult
                           ).then_inc(chunk_scaled[u], 1)
                        dve.wait_ge(*now(chunk_scaled, i, u))
                        nc.vector.tensor_copy(ch3[u][0:1, :, 0], per_image(const[0:1, :], i, u)).then_inc(chunk_ready[u], 1)

                    def turn(i, last):
                        for u in range(2):
                            dve.wait_ge(*now(t_in["x"], i, u, 16))
                            dve.wait_ge(*prev2(stored, i, u, 16))
                            for h in range(2):
                                dve.wait_ge(*now(out_ps[h], i, u))
                                w = slice(512 * h, 512 * h + 512)
                                tt(res[u][:, w], ps[4 + 2 * u + h][:, :], tin["x"][u][:, w], ALU.add).then_inc(taken[h][u], 1)
                            if not last:
                                prepare(i + 1, u)
                            for h in range(2):
                                dve.wait_ge(*now(taken[h], i, u))
                            dve.wait_ge(*now(t_in["m"], i, u, 16))
                            for n in range(CH):
                                w = slice(n * N, (n + 1) * N)
                                c = bass.ds(2 * i + u + T * n, 1)
                                last_m = stt(res[u][:, w], tin["m"][u][:, w], m_scale[:, c], res[u][:, w], ALU.mult, ALU.add)
                            last_m.then_inc(part[u], 1)
                            dve.wait_ge(*now(part, i, u))
                            dve.wait_ge(*now(t_in["y"], i, u, 16))
                            for n in range(CH):
                                w = slice(n * N, (n + 1) * N)
                                c = bass.ds(2 * i + u + T * n, 1)
                                last_y = stt(res[u][:, w], tin["y"][u][:, w], a_scale[:, c], res[u][:, w], ALU.mult, ALU.add)
                            last_y.then_inc(finished[u], 1)
                    prepare(0, 0)
                    prepare(0, 1)
                    with dve.Fori(0, NT - 1) as i:
                        turn(i, False)
                    turn(NT - 1, True)


def kernel(**inputs):
    import concourse.bacc as _bacc
    from concourse.bass_utils import run_bass_kernel_spmd as _run

    nc = _bacc.Bacc("TRN2", target_bir_lowering=False, num_devices=1)
    consts, cat = shape_constants()
    weights, wat = lay_weights(inputs)
    arrays = {
        "in_x": np.ascontiguousarray(inputs["x"]),
        "in_w_re": np.ascontiguousarray(inputs["L0_conv_weight_real"]),
        "in_w_im": np.ascontiguousarray(inputs["L0_conv_weight_imag"]),
        "in_consts": consts, "in_weights": weights,
    }
    ap = {k: nc.dram_tensor(k, a.shape, F32, kind="ExternalInput").ap() for k, a in arrays.items()}
    out = nc.dram_tensor("out_0", (B, T, N, N), F32, kind="ExternalOutput").ap()
    build(nc, ap["in_x"], ap["in_w_re"], ap["in_w_im"], ap["in_consts"], cat, ap["in_weights"], wat, out)
    r = _run(nc, [arrays], core_ids=[0])
    return r.results[0]["out_0"]
```
